# Optimizing a Trainium2 kernel written in Bass

```python
import numpy as np
import jax
import jax.numpy as jnp

def _softmax(x, axis=-1):
    return jax.nn.softmax(x, axis=axis)

def _gelu(x):
    return jax.nn.gelu(x, approximate=True)

def _silu(x):
    return jax.nn.silu(x)

def _sigmoid(x):
    return jax.nn.sigmoid(x)

def _layernorm(x, axis=-1, eps=1e-05):
    m = jnp.mean(x, axis=axis, keepdims=True)
    v = jnp.var(x, axis=axis, keepdims=True)
    return (x - m) / jnp.sqrt(v + eps)

def _scatter_add(tgt, idx, src, axis=0):
    return tgt.at[idx].add(src)

def _segment_sum(src, seg, n):
    return jax.ops.segment_sum(src, seg, n)
kernel_name = 'mk_adaln_attn_ffn_d1_seqx_r8_b8c92d'

def setup_inputs(seed: int=0):
    np.random.seed(seed)
    _w = jnp.asarray

    def _rec_inputs():
        import jax
        import jax.numpy as jnp
        _rk = jax.random.key(seed)
        x = -0.000125 + 0.9999 * jax.random.normal(jax.random.fold_in(_rk, 1), (128, 32, 512), jnp.float32)
        _lenS = 32 - jax.random.randint(jax.random.fold_in(_rk, 7), (128,), 0, max(1, 32 // 4) + 1, jnp.int32)
        _lenS2 = 32 - jax.random.randint(jax.random.fold_in(_rk, 8), (128,), 0, max(1, 32 // 4) + 1, jnp.int32)
        cond_128 = 0.0061147 + 1.02565 * jax.random.normal(jax.random.fold_in(_rk, 11), (128, 128), jnp.float32)
        fside_S_0 = -0.022604 + 0.987366 * jax.random.normal(jax.random.fold_in(_rk, 12), (32,), jnp.float32)
        return (x, cond_128, fside_S_0)
    x, cond_128, fside_S_0 = _rec_inputs()

    def _L0_cond_setup():
        import jax, jax.numpy as jnp
        import numpy as np
        K = 8
        T = 1.0
        D_EMBD = 128
        IN_C = 32
        OUT_C = 32
        BS = 32
        H = 512
        HID = 128
        key = jax.random.key(seed)
        ks = jax.random.split(key, 10)
        s = lambda fan_in: 1.0 / np.sqrt(fan_in)
        return {'x': jax.random.normal(ks[0], (BS, IN_C, H), dtype=jnp.float32), 'embedding': jax.random.normal(ks[1], (BS, D_EMBD), dtype=jnp.float32), 'W0': jax.random.normal(ks[2], (D_EMBD, HID), dtype=jnp.float32) * s(D_EMBD), 'b0': jnp.zeros((HID,), dtype=jnp.float32), 'W1': jax.random.normal(ks[3], (HID, HID), dtype=jnp.float32) * s(HID), 'b1': jnp.zeros((HID,), dtype=jnp.float32), 'W2': jax.random.normal(ks[4], (HID, K), dtype=jnp.float32) * s(HID), 'b2': jnp.zeros((K,), dtype=jnp.float32), 'weight': jax.random.normal(ks[5], (K, OUT_C, IN_C, 1), dtype=jnp.float32) * s(IN_C), 'bias_k': jax.random.normal(ks[6], (K, OUT_C), dtype=jnp.float32) * 0.1}
    _L0_cond_all = _L0_cond_setup()
    _L0_cond_in = {k: v for k, v in _L0_cond_all.items() if k in ('W0', 'b0', 'W1', 'b1', 'W2', 'b2', 'weight', 'bias_k')}
    del _L0_cond_all

    def _L0_attn_setup():
        import jax, jax.numpy as jnp
        import numpy as np
        from jax import lax
        H = 64
        P = 64
        N = 128
        G = 8
        K = 4
        D_MODEL = 512
        I = H * P
        GN = G * N
        CONV_DIM = I + 2 * GN
        PROJ = I + CONV_DIM + H
        EPS = 1e-05
        GROUP_SIZE = I // G

        def _reference_tuple_inner(hidden_states, in_proj_w, conv_weight, conv_bias, dt_bias, A_log, D, norm_weight, out_proj_w):
            B, L, _ = hidden_states.shape
            proj = jnp.einsum('bld,pd->blp', hidden_states, in_proj_w)
            gate = proj[..., :I]
            hbc = proj[..., I:I + CONV_DIM]
            dt = proj[..., -H:]
            pad = jnp.pad(hbc, ((0, 0), (K - 1, 0), (0, 0)))
            conv = conv_bias
            for k in range(K):
                conv = conv + pad[:, k:k + L, :] * conv_weight[:, k]
            xBC = jax.nn.silu(conv)
            x = xBC[..., :I].reshape(B, L, H, P)
            Bm = xBC[..., I:I + GN].reshape(B, L, G, N)
            Cm = xBC[..., I + GN:].reshape(B, L, G, N)
            hpg = H // G
            B_h = jnp.repeat(Bm, hpg, axis=2)
            C_h = jnp.repeat(Cm, hpg, axis=2)
            dt_p = jax.nn.softplus(dt + dt_bias)
            A = -jnp.exp(A_log)
            dA = jnp.exp(dt_p * A)
            dtx = dt_p[..., None] * x

            def step(state, inp):
                dA_t, dtx_t, B_t, C_t = inp
                state = state * dA_t[..., None, None] + dtx_t[..., None] * B_t[:, :, None, :]
                y_t = jnp.einsum('bhpn,bhn->bhp', state, C_t)
                return (state, y_t)
            xs = (jnp.moveaxis(dA, 1, 0), jnp.moveaxis(dtx, 1, 0), jnp.moveaxis(B_h, 1, 0), jnp.moveaxis(C_h, 1, 0))
            state0 = jnp.zeros((B, H, P, N), jnp.float32)
            final_state, ys = lax.scan(step, state0, xs)
            y = jnp.moveaxis(ys, 0, 1) + x * D[None, None, :, None]
            y = y.reshape(B, L, I)
            yg = y.reshape(B, L, G, GROUP_SIZE)
            var = jnp.mean(yg * yg, axis=-1, keepdims=True)
            yn = (yg * lax.rsqrt(var + EPS)).reshape(B, L, I) * norm_weight
            yn = yn * jax.nn.silu(gate)
            out = jnp.einsum('bli,di->bld', yn, out_proj_w)
            conv_state_new = jnp.moveaxis(hbc[:, L - (K - 1):, :], 1, 2)
            return (out, conv_state_new, final_state)
        key = jax.random.key(seed)
        ks = jax.random.split(key, 6)
        B, L = (2, 256)
        s = 0.02
        return {'hidden_states': jax.random.normal(ks[0], (B, L, D_MODEL), jnp.float32), 'in_proj_w': jax.random.normal(ks[1], (PROJ, D_MODEL), jnp.float32) * s, 'conv_weight': jax.random.normal(ks[2], (CONV_DIM, K), jnp.float32) * s, 'conv_bias': jnp.zeros((CONV_DIM,), jnp.float32), 'dt_bias': jnp.ones((H,), jnp.float32), 'A_log': jnp.log(jnp.arange(1, H + 1, dtype=jnp.float32)), 'D': jnp.ones((H,), jnp.float32), 'norm_weight': jnp.ones((I,), jnp.float32), 'out_proj_w': jax.random.normal(ks[3], (D_MODEL, I), jnp.float32) * s}
    _L0_attn_all = _L0_attn_setup()
    _L0_attn_in = {k: v for k, v in _L0_attn_all.items() if k in ('in_proj_w', 'conv_weight', 'conv_bias', 'dt_bias', 'A_log', 'D', 'norm_weight', 'out_proj_w')}
    del _L0_attn_all

    def _L0_cond2_setup():
        import jax, jax.numpy as jnp
        import numpy as np
        from jax import lax
        N, C_IN, L = (32, 32, 512)
        C_OUT, K, GROUPS = (32, 9, 4)
        C_DIM, PAD, STRIDE = (128, 4, 1)
        key = jax.random.key(seed)
        k1, k2, k3, k4, k5 = jax.random.split(key, 5)
        x = jax.random.normal(k1, (N, C_IN, L), dtype=jnp.float32)
        c = jax.random.normal(k2, (N, C_DIM), dtype=jnp.float32)
        weight = jax.random.normal(k3, (C_OUT, C_IN // GROUPS, K), dtype=jnp.float32)
        c_weight = jax.random.normal(k4, (C_OUT, C_DIM), dtype=jnp.float32)
        bias = jax.random.normal(k5, (C_OUT,), dtype=jnp.float32)
        return {'x': x, 'c': c, 'weight': weight, 'c_weight': c_weight, 'bias': bias}
    _L0_cond2_all = _L0_cond2_setup()
    _L0_cond2_in = {k: v for k, v in _L0_cond2_all.items() if k in ('weight', 'c_weight')}
    del _L0_cond2_all

    def _L0_ffn_setup():
        import jax, jax.numpy as jnp
        import numpy as np
        B_L, B_H = (4, 8)
        LIN_SLOPE, LIN_INTER, EST_T = (1.0, 0.0, 64.0)
        BATCH, SEQ, IN_F, OUT_F = (4, 256, 512, 512)
        MAX_BITS = 8

        def dequant_kbit(qweight, lut, bit):
            O, I32 = (qweight.shape[1], qweight.shape[2])
            shifts = jnp.arange(32, dtype=jnp.int32)
            idx = jnp.zeros((O, I32 * 32), dtype=jnp.int32)
            for p in range(bit):
                bits = (qweight[p][:, :, None] >> shifts & 1).reshape(O, I32 * 32)
                idx = idx | bits << p
            return jnp.take_along_axis(lut, idx, axis=1)
        key = jax.random.key(seed)
        k = jax.random.split(key, 5)
        x = jax.random.normal(k[0], (BATCH, SEQ, IN_F), dtype=jnp.float32)
        qweight = jax.random.randint(k[1], (MAX_BITS, OUT_F, IN_F // 32), 0, 2147483647, dtype=jnp.int32)
        lut4 = jax.random.normal(k[2], (OUT_F, 2 ** B_L), dtype=jnp.float32) * 0.02
        lut8 = jax.random.normal(k[3], (OUT_F, 2 ** B_H), dtype=jnp.float32) * 0.02
        bias = jax.random.normal(k[4], (OUT_F,), dtype=jnp.float32) * 0.01
        return {'x': x, 'qweight': qweight, 'lut4': lut4, 'lut8': lut8, 'bias': bias}
    _L0_ffn_all = _L0_ffn_setup()
    _L0_ffn_in = {k: v for k, v in _L0_ffn_all.items() if k in ('qweight', 'lut4', 'lut8', 'bias')}
    del _L0_ffn_all
    return {'x': x, 'cond_128': cond_128, 'fside_S_0': fside_S_0, 'L0_cond_W0': _L0_cond_in['W0'], 'L0_cond_b0': _L0_cond_in['b0'], 'L0_cond_W1': _L0_cond_in['W1'], 'L0_cond_b1': _L0_cond_in['b1'], 'L0_cond_W2': _L0_cond_in['W2'], 'L0_cond_b2': _L0_cond_in['b2'], 'L0_cond_weight': _L0_cond_in['weight'], 'L0_cond_bias_k': _L0_cond_in['bias_k'], 'L0_attn_in_proj_w': _L0_attn_in['in_proj_w'], 'L0_attn_conv_weight': _L0_attn_in['conv_weight'], 'L0_attn_conv_bias': _L0_attn_in['conv_bias'], 'L0_attn_dt_bias': _L0_attn_in['dt_bias'], 'L0_attn_A_log': _L0_attn_in['A_log'], 'L0_attn_D': _L0_attn_in['D'], 'L0_attn_norm_weight': _L0_attn_in['norm_weight'], 'L0_attn_out_proj_w': _L0_attn_in['out_proj_w'], 'L0_cond2_weight': _L0_cond2_in['weight'], 'L0_cond2_c_weight': _L0_cond2_in['c_weight'], 'L0_ffn_qweight': _L0_ffn_in['qweight'], 'L0_ffn_lut4': _L0_ffn_in['lut4'], 'L0_ffn_lut8': _L0_ffn_in['lut8'], 'L0_ffn_bias': _L0_ffn_in['bias']}

def reference(x, cond_128, fside_S_0, L0_cond_W0, L0_cond_b0, L0_cond_W1, L0_cond_b1, L0_cond_W2, L0_cond_b2, L0_cond_weight, L0_cond_bias_k, L0_attn_in_proj_w, L0_attn_conv_weight, L0_attn_conv_bias, L0_attn_dt_bias, L0_attn_A_log, L0_attn_D, L0_attn_norm_weight, L0_attn_out_proj_w, L0_cond2_weight, L0_cond2_c_weight, L0_ffn_qweight, L0_ffn_lut4, L0_ffn_lut8, L0_ffn_bias):
    import jax
    import jax.numpy as jnp

    def _L0_cond_ref(x, embedding, W0, b0, W1, b1, W2, b2, weight, bias_k):
        import jax, jax.numpy as jnp
        import numpy as np
        K = 8
        T = 1.0
        D_EMBD = 128
        IN_C = 32
        OUT_C = 32
        BS = 32
        H = 512
        HID = 128
        h = jax.nn.gelu(embedding @ W0 + b0, approximate=False)
        h = jax.nn.gelu(h @ W1 + b1, approximate=False)
        att = jax.nn.softmax((h @ W2 + b2) / T, axis=-1)
        agg_w = jnp.einsum('bk,koi->boi', att, weight[..., 0])
        agg_b = att @ bias_k
        out = jnp.einsum('boi,bih->boh', agg_w, x) + agg_b[:, :, None]
        return out

    def _L0_attn_ref(hidden_states, in_proj_w, conv_weight, conv_bias, dt_bias, A_log, D, norm_weight, out_proj_w):
        import jax, jax.numpy as jnp
        import numpy as np
        from jax import lax
        H = 64
        P = 64
        N = 128
        G = 8
        K = 4
        D_MODEL = 512
        I = H * P
        GN = G * N
        CONV_DIM = I + 2 * GN
        PROJ = I + CONV_DIM + H
        EPS = 1e-05
        GROUP_SIZE = I // G

        def _reference_tuple_inner(hidden_states, in_proj_w, conv_weight, conv_bias, dt_bias, A_log, D, norm_weight, out_proj_w):
            B, L, _ = hidden_states.shape
            proj = jnp.einsum('bld,pd->blp', hidden_states, in_proj_w)
            gate = proj[..., :I]
            hbc = proj[..., I:I + CONV_DIM]
            dt = proj[..., -H:]
            pad = jnp.pad(hbc, ((0, 0), (K - 1, 0), (0, 0)))
            conv = conv_bias
            for k in range(K):
                conv = conv + pad[:, k:k + L, :] * conv_weight[:, k]
            xBC = jax.nn.silu(conv)
            x = xBC[..., :I].reshape(B, L, H, P)
            Bm = xBC[..., I:I + GN].reshape(B, L, G, N)
            Cm = xBC[..., I + GN:].reshape(B, L, G, N)
            hpg = H // G
            B_h = jnp.repeat(Bm, hpg, axis=2)
            C_h = jnp.repeat(Cm, hpg, axis=2)
            dt_p = jax.nn.softplus(dt + dt_bias)
            A = -jnp.exp(A_log)
            dA = jnp.exp(dt_p * A)
            dtx = dt_p[..., None] * x

            def step(state, inp):
                dA_t, dtx_t, B_t, C_t = inp
                state = state * dA_t[..., None, None] + dtx_t[..., None] * B_t[:, :, None, :]
                y_t = jnp.einsum('bhpn,bhn->bhp', state, C_t)
                return (state, y_t)
            xs = (jnp.moveaxis(dA, 1, 0), jnp.moveaxis(dtx, 1, 0), jnp.moveaxis(B_h, 1, 0), jnp.moveaxis(C_h, 1, 0))
            state0 = jnp.zeros((B, H, P, N), jnp.float32)
            final_state, ys = lax.scan(step, state0, xs)
            y = jnp.moveaxis(ys, 0, 1) + x * D[None, None, :, None]
            y = y.reshape(B, L, I)
            yg = y.reshape(B, L, G, GROUP_SIZE)
            var = jnp.mean(yg * yg, axis=-1, keepdims=True)
            yn = (yg * lax.rsqrt(var + EPS)).reshape(B, L, I) * norm_weight
            yn = yn * jax.nn.silu(gate)
            out = jnp.einsum('bli,di->bld', yn, out_proj_w)
            conv_state_new = jnp.moveaxis(hbc[:, L - (K - 1):, :], 1, 2)
            return (out, conv_state_new, final_state)
        return _reference_tuple_inner(hidden_states, in_proj_w, conv_weight, conv_bias, dt_bias, A_log, D, norm_weight, out_proj_w)[0]

    def _L0_cond2_ref(x, c, weight, c_weight, bias):
        import jax, jax.numpy as jnp
        import numpy as np
        from jax import lax
        N, C_IN, L = (32, 32, 512)
        C_OUT, K, GROUPS = (32, 9, 4)
        C_DIM, PAD, STRIDE = (128, 4, 1)
        out = lax.conv_general_dilated(x, weight, window_strides=(STRIDE,), padding=[(PAD, PAD)], dimension_numbers=('NCH', 'OIH', 'NCH'), feature_group_count=GROUPS)
        ctx = jnp.einsum('nd,od->no', c, c_weight)
        out = out + ctx[:, :, None] + bias[None, :, None]
        return out

    def _L0_ffn_ref(x, qweight, lut4, lut8, bias):
        import jax, jax.numpy as jnp
        import numpy as np
        B_L, B_H = (4, 8)
        LIN_SLOPE, LIN_INTER, EST_T = (1.0, 0.0, 64.0)
        BATCH, SEQ, IN_F, OUT_F = (4, 256, 512, 512)
        MAX_BITS = 8

        def dequant_kbit(qweight, lut, bit):
            O, I32 = (qweight.shape[1], qweight.shape[2])
            shifts = jnp.arange(32, dtype=jnp.int32)
            idx = jnp.zeros((O, I32 * 32), dtype=jnp.int32)
            for p in range(bit):
                bits = (qweight[p][:, :, None] >> shifts & 1).reshape(O, I32 * 32)
                idx = idx | bits << p
            return jnp.take_along_axis(lut, idx, axis=1)
        e = jnp.linalg.norm(x, axis=-1) * LIN_SLOPE + LIN_INTER
        mask = e > EST_T
        w_l = dequant_kbit(qweight, lut4, B_L)
        w_h = dequant_kbit(qweight, lut8, B_H)
        y_l = jnp.einsum('bsi,oi->bso', x, w_l)
        y_h = jnp.einsum('bsi,oi->bso', x, w_h)
        y = jnp.where(mask[..., None], y_h, y_l) + bias
        return y
    x = x + _L0_attn_ref(_L0_cond_ref(x, cond_128, L0_cond_W0, L0_cond_b0, L0_cond_W1, L0_cond_b1, L0_cond_W2, L0_cond_b2, L0_cond_weight, L0_cond_bias_k), L0_attn_in_proj_w, L0_attn_conv_weight, L0_attn_conv_bias, L0_attn_dt_bias, L0_attn_A_log, L0_attn_D, L0_attn_norm_weight, L0_attn_out_proj_w)
    x = x + _L0_ffn_ref(_L0_cond2_ref(x, cond_128, L0_cond2_weight, L0_cond2_c_weight, fside_S_0), L0_ffn_qweight, L0_ffn_lut4, L0_ffn_lut8, L0_ffn_bias)
    return x

_drawn_inputs = setup_inputs


def setup_inputs(seed=0):
    import zlib

    import numpy as np

    out = dict(_drawn_inputs(seed))
    spreads = {'L0_cond_b0': (0.0, 0.8),
     'L0_cond_b1': (0.0, 0.8),
     'L0_cond_b2': (0.0, 2.0),
     'L0_attn_conv_bias': (0.0, 0.1),
     'L0_attn_dt_bias': (1.0, 0.6),
     'L0_attn_D': (1.0, 0.6),
     'L0_attn_norm_weight': (1.0, 0.6)}
    factors = {'L0_cond_W0': 4.013,
     'L0_cond_W1': 3.731,
     'L0_cond_W2': 3.563,
     'L0_cond_bias_k': 8.0,
     'L0_attn_conv_weight': 8.0,
     'L0_attn_A_log': 64.0,
     'L0_ffn_bias': 63.846}
    for name, (base, spread) in spreads.items():
        noise = np.random.default_rng([zlib.crc32(name.encode()), seed]).standard_normal(out[name].shape)
        drawn = base * np.exp(spread * noise) if base else spread * noise
        out[name] = jnp.asarray(drawn.astype(out[name].dtype))
    for name, factor in factors.items():
        out[name] = (out[name] * factor).astype(out[name].dtype)
    return out
```

```python
from contextlib import ExitStack

import concourse.bass as bass
from concourse import mybir

F32 = mybir.dt.float32
F32R = mybir.dt.float32r
BF16 = mybir.dt.bfloat16
I32 = mybir.dt.int32
ALU = mybir.AluOpType
ACT = mybir.ActivationFunctionType
AX = mybir.AxisListType
ds = bass.ds

P = 128
NB, L, DM = 128, 32, 512
TOK = NB * L
BLK = 512
NBLK = TOK // BLK
TT = BLK // P
BT = P // L
KC = DM // P
H, HP, NS, G = 64, 64, 128, 8
INNER = H * HP
GN = G * NS
CONV = INNER + 2 * GN
HG = H // G
GI = INNER // G
CT = GI // P
TAPS = 4
EPS = 1e-5
NEXP = 8
NCODE = 256
OT = DM // P
NIT = G * NBLK
CPI = NCODE // NIT
KW = 9
PADW = KW // 2
CG = 8
MASK_T2 = 64.0 * 64.0 * (1.0 + 2.0 ** -23)
DECAY_FLOOR = -200.0
LOGA_CAP = 85.0

PASSES = ((0, 0), (0, 1), (1, 0))
NCV = 2 + CT
NWC = NCV + CT + KC
C4 = 16 // NBLK
SEGB = TT * HG * L // 512
NSTAGE = 4
PROJ_BANK = (0, 1, 2, 0, 1, 2, 0, 1, 2, 1)


class Shared:
    pass


def stage1(nc, a, sh):
    with ExitStack() as ctx:
        def sb(name, shape, dt=F32):
            return ctx.enter_context(nc.sbuf_tensor(name, shape, dt))

        def sem(name):
            return ctx.enter_context(nc.semaphore(name))

        cond = sb("cond", [NB, 128])
        cond_t = sb("cond_t", [128, NB])
        cw = sb("cw", [L, 128])
        cw_t = sb("cw_t", [128, L])
        w0 = sb("w0", [128, 128])
        w1 = sb("w1", [128, 128])
        b0 = sb("b0", [128, 1])
        b1 = sb("b1", [128, 1])
        w2 = sb("w2", [128, NEXP])
        b2 = sb("b2", [NB, NEXP])
        experts = sb("experts", [NEXP, L * L])
        bias_k = sb("bias_k", [NEXP, L])
        side = sb("side", [NB, L])
        h1 = sb("h1", [128, NB])
        h2 = sb("h2", [128, NB])
        logit = sb("logit", [NB, NEXP])
        nmax = sb("nmax", [NB, 1])
        esum = sb("esum", [NB, 1])
        erec = sb("erec", [NB, 1])
        att = sb("att", [NB, NEXP])
        att_t = sb("att_t", [NEXP, NB])
        agg = sb("agg", [NB, L, L])
        aggb = sb("aggb", [NB, L])
        ctxb = sb("ctxb", [NB, L])
        mix = sb("mix", [P, NBLK * TT, P])
        aggb_row = sb("aggb_row", [1, TOK])
        ones_row = sb("ones_row", [1, P])
        wdt = sb("wdt", [H, DM])
        wdt_t = sb("wdt_t", [P, 2, KC, H], F32R)
        dtb = sb("dtb", [P, H])
        alog = sb("alog", [P, H])
        xb = [sb(f"xb{u}", [P, TT, DM]) for u in range(2)]
        ht = [sb(f"ht_out{u}", [P, 2, KC, BLK], F32R) for u in range(2)]
        sp_e = sb("sp_e", [P, NBLK * TT * H])
        qw = sb("qw", [P, OT, 8, 16], I32)
        bits = sb("bits", [P, OT * 4 * 16, 32], I32)
        code = sb("code", [P, OT, DM])
        code4 = sb("code4", [P, OT, DM])
        lut4 = sb("lut4", [P, OT, 16])
        pick = sb("pick", [P, 2, DM])
        w4 = sb("w4", [P, OT, DM])

        p_mlp = ctx.enter_context(nc.psum_tensor("p_mlp", [P, 512], F32))
        p_agg = [ctx.enter_context(nc.psum_tensor(f"p_agg{u}", [P, 512], F32)) for u in range(2)]
        p_wdt = ctx.enter_context(nc.psum_tensor("p_wdt", [P, 512], F32))
        p_h = [ctx.enter_context(nc.psum_tensor(f"p_h{u}", [P, 512], F32)) for u in range(2)]
        p_dt = [ctx.enter_context(nc.psum_tensor(f"p_dt{u}", [P, 512], F32)) for u in range(2)]

        s_ld = sem("s1_loaded")
        s_q = sem("s1_q_loaded")
        s_const = sem("s1_const")
        s_pe = sem("s1_pe")
        s_act = sem("s1_act")
        s_dve = sem("s1_dve")
        s_rt = sem("s1_roundtrip")
        s_mix = sem("s1_mix")
        s_x = [sem(f"s1_x{u}") for u in range(2)]
        s_hp = sem("s1_hp")
        s_hi = sem("s1_hi")
        s_lo = sem("s1_lo")
        s_hst = [sem(f"s1_hst{u}") for u in range(2)]
        s_dtp = sem("s1_dtp")
        s_dtv = sem("s1_dtv")
        s_spa = sem("s1_spa")
        s_spv = sem("s1_spv")
        s_bits = sem("s1_bits")
        s_pick = sem("s1_pick")
        s_w4 = sem("s1_w4")

        with nc.Block() as block:

            @block.sync
            def _(sp):
                small = [(cond[:, :], a["cond_128"]), (cw[:, :], a["L0_cond2_c_weight"]),
                         (w0[:, :], a["L0_cond_W0"]), (w1[:, :], a["L0_cond_W1"]),
                         (b0[:, :], a["L0_cond_b0"].rearrange("(p o) -> p o", o=1)),
                         (b1[:, :], a["L0_cond_b1"].rearrange("(p o) -> p o", o=1)),
                         (w2[:, :], a["L0_cond_W2"]),
                         (b2[:, :], a["L0_cond_b2"].partition_broadcast(NB)),
                         (experts[:, :], a["L0_cond_weight"].rearrange("k o i u -> k (o i u)")),
                         (bias_k[:, :], a["L0_cond_bias_k"]),
                         (side[:, :], a["fside_S_0"].partition_broadcast(NB)),
                         (wdt[:, :], a["L0_attn_in_proj_w"][INNER + CONV:INNER + CONV + H, :]),
                         (dtb[:, :], a["L0_attn_dt_bias"].partition_broadcast(P)),
                         (alog[:, :], a["L0_attn_A_log"].partition_broadcast(P))]
                for dst, src in small:
                    sp.dma_start(dst, src).then_inc(s_ld, 16)
                sh.n_small = 16 * len(small)
                x_blk = a["x"].rearrange("b i d -> (b i) d").rearrange("(j t p) d -> j p t d", t=TT, p=P)

                def load_x(j, u):
                    sp.dma_start(xb[u][:, :, :], x_blk[ds(j, 1)].rearrange("o p t d -> p (o t) d")).then_inc(s_x[u], 16)

                for u in range(2):
                    sp.sem_inc(s_hst[u], 16)
                    load_x(u, u)
                sp.wait_ge(s_dve, 9)
                sp.dma_start(sh.agg_d.rearrange("b i o -> b (i o)"), agg[:, :, :].rearrange("b i o -> b (i o)")).then_inc(s_rt, 16)
                sp.dma_start(sh.aggb_d, aggb[:, :]).then_inc(s_rt, 16)
                sp.dma_start(sh.ctxb_d, ctxb[:, :]).then_inc(s_rt, 16)
                sp.wait_ge(s_rt, 48)
                sp.wait_ge(s_const, 4)
                agg_v = sh.agg_d.rearrange("(t c) i o -> c i t o", c=BT)
                for c in range(BT):
                    sp.dma_start(mix[c * L:(c + 1) * L, :, c * L:(c + 1) * L], agg_v[c]).then_inc(s_mix, 16)
                sp.dma_start(aggb_row[:, :], sh.aggb_d.rearrange("(u b) o -> u (b o)", u=1)).then_inc(s_mix, 16)
                with sp.Fori(0, NBLK // 2 - 1) as jj:
                    for u in range(2):
                        sp.wait_ge(s_hp, KC * (2 * jj + u + 1))
                        load_x(2 * jj + u + 2, u)
                        sp.wait_ge(s_lo, KC * (2 * jj + u + 1) + 2)
                        sp.dma_start(sh.h_d[ds(2 * jj + u, 1)].rearrange("o p n -> p (o n)"),
                                     ht[u][:, :, :, :].rearrange("p a k n -> p (a k n)").bitcast(F32)).then_inc(s_hst[u], 16)
                for u in range(2):
                    sp.wait_ge(s_lo, KC * (NBLK - 2 + u + 1) + 2)
                    sp.dma_start(sh.h_d[NBLK - 2 + u], ht[u][:, :, :, :].rearrange("p a k n -> p (a k n)").bitcast(F32)).then_inc(s_hst[u], 16)
                for u in range(2):
                    sp.wait_ge(s_hst[u], 16 * (NBLK // 2) + 16)
                sp.wait_ge(s_pick, 2 * 16 * OT)
                sp.dma_start(sh.w4_d, w4[:, :, :].rearrange("p t i -> p (t i)")).then_inc(s_rt, 16)
                sp.wait_ge(s_rt, 64)

            @block.gpsimd
            def _(pool):
                q_v = a["L0_ffn_qweight"].rearrange("n (t p) w -> t p n w", p=P)
                for t in range(OT):
                    pool.dma_start(qw[:, t, :, :], q_v[t]).then_inc(s_q, 16)
                pool.dma_start(lut4[:, :, :], a["L0_ffn_lut4"].rearrange("(t p) c -> p t c", p=P)).then_inc(s_q, 16)
                pool.dma_start(sh.lut8[:, :, :], a["L0_ffn_lut8"].rearrange("(t p) c -> p t c", p=P)).then_inc(s_q, 16)
                pool.memset(sh.ident[:, :], 0.0).then_inc(s_const, 1)
                pool.memset(ones_row[:, :], 1.0).then_inc(s_const, 1)
                pool.wait_ge(s_const, 2)
                pool.affine_select(out=sh.ident[:, :], in_=sh.ident[:, :], compare_op=ALU.not_equal, fill=1.0,
                                   base=0, pattern=[[-1, P]], channel_multiplier=1).then_inc(s_const, 1)
                pool.memset(mix[:, :, :], 0.0).then_inc(s_const, 1)
                pool.iota(sh.code_no[:, :], pattern=[[1, NCODE]], base=0, channel_multiplier=0,
                          allow_small_or_imprecise_dtypes=True).then_inc(s_const, 1)
                pool.memset(sh.mask_cb[:, :], 1.0).then_inc(s_const, 1)
                pool.memset(sh.mask_gt[:, :], 1.0).then_inc(s_const, 1)
                pool.wait_ge(s_const, 7)
                n = 7
                for m, tri in ((sh.mask_cb, "le"), (sh.mask_gt, "gt")):
                    v = m[:, :].rearrange("p (c l) -> p c l", l=L)
                    sel = [(0, [[-L, BT], [0, L]], 1), (L - 1, [[L, BT], [0, L]], -1)]
                    sel.append((0, [[L, BT], [1, L]], -1) if tri == "le" else (-1, [[-L, BT], [-1, L]], 1))
                    for base, pat, cm in sel:
                        pool.affine_select(out=v, in_=v, compare_op=ALU.is_ge, fill=0.0, base=base, pattern=pat,
                                           channel_multiplier=cm).then_inc(s_const, 1)
                        n += 1
                        pool.wait_ge(s_const, n)
                pool.memset(sh.neg_half[:, :], -0.5).then_inc(s_const, 1)
                pool.memset(sh.ones_col[:, :], 1.0).then_inc(s_const, 1)
                pool.memset(sh.w8[:, :, :], 0.0).then_inc(s_const, 1)
                pool.wait_ge(s_q, 16 * (OT + 2))

            @block.tensor
            def _(pe):
                pe.wait_ge(s_ld, sh.n_small)
                pe.wait_ge(s_const, 4)
                pe.transpose(p_mlp[:, 0:NB], cond[:, :], sh.ident[:, :])
                pe.transpose(p_mlp[:, NB:NB + L], cw[:, :], sh.ident[0:L, 0:L]).then_inc(s_pe, 1)
                for k in range(KC):
                    ins = pe.transpose(p_wdt[:, k * H:(k + 1) * H], wdt[:, k * P:(k + 1) * P], sh.ident[0:H, 0:H])
                ins.then_inc(s_pe, 1)
                pe.wait_ge(s_dve, 2)
                pe.matmul(p_mlp[:, 160:160 + L], cond_t[:, :], cw_t[:, :], start=True, stop=True).then_inc(s_pe, 1)
                pe.matmul(p_mlp[:, 256:256 + NB], w0[:, :], cond_t[:, :], start=True, stop=True).then_inc(s_pe, 1)
                pe.wait_ge(s_act, 2)
                pe.matmul(p_mlp[:, 384:384 + NB], w1[:, :], h1[:, :], start=True, stop=True).then_inc(s_pe, 1)
                pe.wait_ge(s_act, 3)
                pe.matmul(p_mlp[:, 192:192 + NEXP], h2[:, :], w2[:, :], start=True, stop=True).then_inc(s_pe, 1)
                pe.wait_ge(s_dve, 7)
                pe.transpose(p_agg[0][0:NEXP, 0:NB], att[:, :], sh.ident[:, :]).then_inc(s_pe, 1)
                pe.wait_ge(s_dve, 8)
                for u in range(2):
                    pe.matmul(p_agg[u][:, :], att_t[:, :], experts[:, u * 512:(u + 1) * 512], start=True, stop=True)
                pe.matmul(p_mlp[:, 208:208 + L], att_t[:, :], bias_k[:, :], start=True, stop=True).then_inc(s_pe, 1)
                pe.wait_ge(s_mix, 16 * (BT + 1))
                with pe.Fori(0, NBLK // 2) as jj:
                    for u in range(2):
                        j = 2 * jj + u
                        pe.wait_ge(s_x[u], 16 * jj + 16)
                        for k in range(KC):
                            pe.wait_ge(s_lo, KC * j + k + 1)
                            for t in range(TT):
                                pe.matmul(p_h[k % 2][:, t * P:(t + 1) * P], xb[u][:, t, k * P:(k + 1) * P],
                                          mix[:, ds(TT * j + t, 1), :].rearrange("p o n -> p (o n)"),
                                          start=(t == 0), stop=False, skip_group_check=True)
                            pe.matmul(p_h[k % 2][:, :], ones_row[:, :], aggb_row[:, ds(BLK * j, BLK)],
                                      start=False, stop=True, skip_group_check=True).then_inc(s_hp, 1)
                        pe.wait_ge(s_lo, KC * (j + 1) + 2)
                        pe.wait_ge(s_dtv, j + 1)
                        for t in range(TT):
                            for n, (l, r) in enumerate(PASSES):
                                for k in range(KC):
                                    ins = pe.matmul(p_dt[u][:, t * H:(t + 1) * H], ht[u][:, l, k, t * P:(t + 1) * P],
                                                    wdt_t[:, r, k, :], start=(n == 0 and k == 0), stop=(n == 2 and k == KC - 1))
                        ins.then_inc(s_dtp, 1)

            @block.scalar
            def _(act):
                act.wait_ge(s_pe, 2)
                act.activation(wdt_t[:, 0, :, :].rearrange("p k h -> p (k h)"), p_wdt[:, 0:KC * H], ACT.Copy).then_inc(s_act, 1)
                act.wait_ge(s_pe, 4)
                act.activation(h1[:, :], p_mlp[:, 256:256 + NB], ACT.Gelu, bias=b0[:, :]).then_inc(s_act, 1)
                act.wait_ge(s_pe, 5)
                act.activation(h2[:, :], p_mlp[:, 384:384 + NB], ACT.Gelu, bias=b1[:, :]).then_inc(s_act, 1)
                act.wait_ge(s_dve, 5)
                act.activation(att[:, :], logit[:, :], ACT.Exp, bias=nmax[:, :], accum_out=esum[:, :]).then_inc(s_act, 1)
                with act.Fori(0, NBLK // 2) as jj:
                    for u in range(2):
                        j = 2 * jj + u
                        act.wait_ge(s_hst[u], 16 * jj + 16)
                        act.wait_ge(s_dtv, j + 1)
                        for k in range(KC):
                            act.wait_ge(s_hp, KC * j + k + 1)
                            act.activation(ht[u][:, 0, k, :], p_h[k % 2][:, :], ACT.Copy).then_inc(s_hi, 1)
                dtv = sh.dt[:, :, :].rearrange("p t h -> p (t h)")
                act.wait_ge(s_dtv, NBLK + 2)
                act.activation(sp_e[:, :], dtv, ACT.Abs).then_inc(s_spa, 1)
                act.wait_ge(s_spa, 1)
                act.activation(sp_e[:, :], sp_e[:, :], ACT.Exp, scale=-1.0).then_inc(s_spa, 1)
                act.wait_ge(s_spa, 2)
                act.activation(sp_e[:, :], sp_e[:, :], ACT.Ln, bias=1.0).then_inc(s_spa, 1)
                act.wait_ge(s_spv, 1)
                act.activation(sh.neg_a[:, :], alog[:, :], ACT.Exp).then_inc(s_spa, 1)

            @block.vector
            def _(dve):
                dve.sem_inc(s_lo, 2)
                dve.sem_inc(s_dtv, 2)
                dve.wait_ge(s_pe, 1)
                dve.tensor_copy(cond_t[:, :], p_mlp[:, 0:NB]).then_inc(s_dve, 1)
                dve.tensor_copy(cw_t[:, :], p_mlp[:, NB:NB + L]).then_inc(s_dve, 1)
                dve.wait_ge(s_act, 1)
                dve.tensor_tensor(wdt_t[:, 1, :, :].rearrange("p k h -> p (k h)"), p_wdt[:, 0:KC * H],
                                  wdt_t[:, 0, :, :].rearrange("p k h -> p (k h)").bitcast(F32), ALU.subtract).then_inc(s_dve, 1)
                dve.wait_ge(s_pe, 6)
                dve.tensor_tensor(logit[:, :], p_mlp[:, 192:192 + NEXP], b2[:, :], ALU.add).then_inc(s_dve, 1)
                dve.wait_ge(s_dve, 4)
                dve.tensor_reduce(nmax[:, :], logit[:, :], axis=AX.X, op=ALU.max, negate=True).then_inc(s_dve, 1)
                dve.wait_ge(s_act, 4)
                dve.reciprocal(erec[:, :], esum[:, :]).then_inc(s_dve, 1)
                dve.wait_ge(s_dve, 6)
                dve.tensor_scalar(att[:, :], att[:, :], erec[:, :], None, ALU.mult).then_inc(s_dve, 1)
                dve.wait_ge(s_pe, 7)
                dve.tensor_copy(att_t[:, :], p_agg[0][0:NEXP, 0:NB]).then_inc(s_dve, 1)
                dve.wait_ge(s_pe, 8)
                for u in range(2):
                    half = L // 2
                    dve.tensor_copy(agg[:, :, u * half:(u + 1) * half].rearrange("b i o -> b o i"),
                                    p_agg[u][:, :].rearrange("b (o i) -> b o i", i=L))
                dve.tensor_copy(aggb[:, :], p_mlp[:, 208:208 + L])
                dve.tensor_tensor(ctxb[:, :], p_mlp[:, 160:160 + L], side[:, :], ALU.add).then_inc(s_dve, 1)

                dve.wait_ge(s_q, 16 * (OT + 2))
                dve.wait_ge(s_const, 5)
                plane = bits[:, :, :].rearrange("p (t n w) s -> p t n (w s)", t=OT, n=4)
                n = 0
                for half in range(2):
                    if half:
                        dve.wait_ge(s_bits, n)
                    for s in range(32):
                        ins = dve.tensor_scalar(bits[:, :, s].rearrange("p (t n) -> p t n", t=OT),
                                                qw[:, :, 4 * half:4 * half + 4, :].rearrange("p t n w -> p t (n w)"), s, 1,
                                                ALU.logical_shift_right, ALU.bitwise_and)
                    ins.then_inc(s_bits, 1)
                    n += 1
                    for b in range(4):
                        dve.wait_ge(s_bits, n)
                        if half == 0 and b == 0:
                            ins = dve.tensor_copy(code4[:, :, :], plane[:, :, 0, :])
                        else:
                            ins = dve.scalar_tensor_tensor((sh.code8 if half and b == 3 else code4 if half == 0 else code)[:, :, :],
                                                           plane[:, :, b, :], float(1 << (4 * half + b)),
                                                           (code4 if half == 0 or b == 0 else code)[:, :, :], ALU.mult, ALU.add)
                        ins.then_inc(s_bits, 1)
                        n += 1
                dve.memset(w4[:, :, :], 0.0).then_inc(s_bits, 1)
                dve.wait_ge(s_bits, n + 1)
                dve.wait_ge(s_const, 16)
                dve.tensor_reduce(sh.mask_le[:, :], sh.mask_cb[:, :].rearrange("p (c l) -> p l c", l=L), axis=AX.X,
                                  op=ALU.add).then_inc(s_w4, 1)
                dve.wait_ge(s_w4, 1)
                with dve.Fori(0, NBLK // 2) as jj:
                    for u in range(2):
                        j = 2 * jj + u
                        for c in range(C4):
                            for t in range(OT):
                                n = 2 * (C4 * OT * j + c * OT + t)
                                dve.tensor_scalar(pick[:, t % 2, :], code4[:, t, :], sh.code_no[:, ds(C4 * j + c, 1)],
                                                  lut4[:, t, ds(C4 * j + c, 1)], ALU.is_equal, ALU.mult).then_inc(s_pick, 1)
                                dve.wait_ge(s_pick, n + 1)
                                dve.tensor_tensor(w4[:, t, :], w4[:, t, :], pick[:, t % 2, :], ALU.add).then_inc(s_pick, 1)
                        for k in range(KC):
                            dve.wait_ge(s_hi, KC * j + k + 1)
                            dve.tensor_tensor(ht[u][:, 1, k, :], p_h[k % 2][:, :], ht[u][:, 0, k, :].bitcast(F32),
                                              ALU.subtract).then_inc(s_lo, 1)
                        dve.wait_ge(s_dtp, j + 1)
                        dve.tensor_tensor(sh.dt[:, ds(TT * j, TT), :], p_dt[u][:, 0:TT * H].rearrange("p (t h) -> p t h", h=H),
                                          dtb[:, :].rearrange("p (o h) -> p o h", o=1).to_broadcast([P, TT, H]), ALU.add).then_inc(s_dtv, 1)
                dve.tensor_scalar(alog[:, :], alog[:, :], LOGA_CAP, None, ALU.min).then_inc(s_spv, 1)
                dve.wait_ge(s_spa, 3)
                dtv = sh.dt[:, :, :].rearrange("p t h -> p (t h)")
                dve.scalar_tensor_tensor(dtv, dtv, 0.0, sp_e[:, :], ALU.max, ALU.add).then_inc(s_spv, 1)
                dve.wait_ge(s_spa, 4)
                dve.wait_ge(s_spv, 2)
                dve.tensor_scalar(sh.neg_a[:, :], sh.neg_a[:, :], -1.0, None, ALU.mult).then_inc(s_spv, 1)
                dve.wait_ge(s_pick, 2 * 16 * OT)
                dve.wait_ge(s_spv, 3)


def stage2(nc, a, sh):
    with ExitStack() as ctx:
        def sb(name, shape, dt=F32):
            return ctx.enter_context(nc.sbuf_tensor(name, shape, dt))

        def sem(name):
            return ctx.enter_context(nc.semaphore(name))

        stage = [sb(f"stage{n}", [P, DM]) for n in range(NSTAGE)]
        wt = sb("wt", [P, 2, KC, (NCV + CT) * P], F32R)
        wot = sb("wot", [P, 2, CT, DM], F32R)
        wo_tmp = sb("wo_tmp", [P, CT, P])
        cvw = sb("cvw", [P, NCV, TAPS])
        cvb = sb("cvb", [P, NCV])
        dsk = sb("dsk", [P, CT])
        nw = sb("nw", [P, CT])
        ht = sb("ht", [P, 2, KC, BLK], F32R)
        acc = sb("acc", [P, TT, DM])
        xc = sb("xc", [P, NCV, BLK])
        z = sb("z", [P, CT, BLK])
        y = sb("y", [P, CT, BLK])
        gy = sb("gy", [P, 2, CT, BLK], F32R)
        adt = sb("adt", [P, TT, HG])
        segr = sb("segr", [P, TT * HG, L])
        decay = sb("decay", [P, TT, HG, L])
        cbm = sb("cbm", [P, TT, P])
        dtx = sb("dtx", [P, TT, GI])
        m = sb("m", [P, TT, HG, P])
        rv = sb("rv", [P, TT])
        r = sb("r", [P, TT])
        pick = sb("pick8", [P, 2, DM])

        bank = [ctx.enter_context(nc.psum_tensor(f"bank{n}", [P, 512], F32)) for n in range(8)]
        XT, SEG, CB, YB, OUT, SSQ = (3, 4), (5, 7), 6, (6, 7), (2, 3, 4, 5), 6

        s_stage = [sem(f"s2_stage{n}") for n in range(NSTAGE)]
        s_par = sem("s2_params")
        s_wps = sem("s2_wps")
        s_wosc = sem("s2_wosc")
        s_whi = sem("s2_whi")
        s_wlo = sem("s2_wlo")
        s_ht = sem("s2_ht")
        s_accin = sem("s2_accin")
        s_accst = sem("s2_accst")
        s_init = sem("s2_init")
        s_proj = sem("s2_proj")
        s_tap = sem("s2_tap")
        s_cvstep = sem("s2_cvstep")
        s_conv = sem("s2_conv")
        s_silu = sem("s2_silu")
        s_z = sem("s2_z")
        s_adt = sem("s2_adt")
        s_segr = sem("s2_segr")
        s_seg = sem("s2_seg")
        s_exp = sem("s2_exp")
        s_xt = sem("s2_xt")
        s_dtx = sem("s2_dtx")
        s_cb = sem("s2_cb")
        s_cbm = sem("s2_cbm")
        s_m = sem("s2_m")
        s_yp = sem("s2_yp")
        s_y = sem("s2_y")
        s_u = sem("s2_u")
        s_uhi = sem("s2_uhi")
        s_ulo = sem("s2_ulo")
        s_sq = sem("s2_sq")
        s_ssq = sem("s2_ssq")
        s_rv = sem("s2_rv")
        s_r = sem("s2_r")
        s_out = sem("s2_out")
        s_acc = sem("s2_acc")
        s_pick = sem("s2_pick")
        s_w8 = sem("s2_w8")

        NPAR = 9

        with nc.Block() as block:

            @block.sync
            def _(sp):
                w_in = a["L0_attn_in_proj_w"]
                w_out = a["L0_attn_out_proj_w"]
                cw = a["L0_attn_conv_weight"]
                cb = a["L0_attn_conv_bias"].rearrange("(c o) -> c o", o=1)
                d_v = a["L0_attn_D"].rearrange("(g c u) -> u g c", g=G, u=2)
                nw_v = a["L0_attn_norm_weight"].rearrange("(g c p) -> g p c", g=G, p=P)
                acc_v = sh.acc_d.rearrange("(j t p) d -> j p t d", t=TT, p=P)

                def load_h(j):
                    sp.dma_start(ht[:, :, :, :].rearrange("p a k n -> p (a k n)").bitcast(F32),
                                 sh.h_d[ds(j, 1)].rearrange("o p n -> p (o n)")).then_inc(s_ht, 16)

                sp.sem_inc(s_accst, 16)
                load_h(0)
                with sp.Fori(0, G) as g:
                    for lo, n, c0 in ((0, 1, INNER + g * NS), (1, 1, INNER + GN + g * NS), (2, CT, g * GI)):
                        sp.dma_start(cvw[:, lo:lo + n, :], cw[ds(c0, n * P), :].rearrange("(c p) k -> p c k", p=P)).then_inc(s_par, 16)
                        sp.dma_start(cvb[:, lo:lo + n], cb[ds(c0, n * P), :].rearrange("(c p) o -> p (c o)", p=P)).then_inc(s_par, 16)
                    for u in range(2):
                        sp.dma_start(dsk[u * HP:(u + 1) * HP, :], d_v[u, ds(g, 1), :].to_broadcast([HP, CT])).then_inc(s_par, 16)
                    sp.dma_start(nw[:, :], nw_v[ds(g, 1)].rearrange("o p c -> p (o c)")).then_inc(s_par, 16)
                    rows = [2 * INNER + g * NS, 2 * INNER + GN + g * NS]
                    rows += [INNER + g * GI + c * P for c in range(CT)] + [g * GI + c * P for c in range(CT)]
                    for n in range(NWC):
                        sp.wait_ge(s_wps, NWC * g + NWC + max(n - NSTAGE + 1, 0))
                        src = w_in[ds(rows[n], P), :] if n < len(rows) else w_out[(n - len(rows)) * P:(n - len(rows) + 1) * P, ds(g * GI, GI)]
                        sp.dma_start(stage[n % NSTAGE][:, :], src).then_inc(s_stage[n % NSTAGE], 16)
                    with sp.Fori(0, NBLK) as j:
                        it = NBLK * g + j
                        sp.wait_ge(s_init, 16 * NBLK)
                        sp.wait_ge(s_accst, 16 * it + 16)
                        sp.dma_start(acc[:, :, :], acc_v[ds(j, 1)].rearrange("o p t d -> p (o t) d")).then_inc(s_accin, 16)
                        sp.wait_ge(s_proj, (NCV + CT) * (it + 1))
                        load_h((j + 1) % NBLK)
                        sp.wait_ge(s_acc, TT * it + 2 * TT)
                        sp.dma_start(acc_v[ds(j, 1)].rearrange("o p t d -> p (o t) d"), acc[:, :, :]).then_inc(s_accst, 16)
                sp.wait_ge(s_accst, 16 * NIT + 16)
                sp.wait_ge(s_ht, 16 * NIT + 16)

            @block.gpsimd
            def _(pool):
                x_v = a["x"].rearrange("b i d -> (b i) d")
                for j in range(NBLK):
                    pool.dma_start(sh.acc_d[j * BLK:(j + 1) * BLK, :], x_v[j * BLK:(j + 1) * BLK, :]).then_inc(s_init, 16)
                pool.sem_inc(s_segr, 1)
                pool.sem_inc(s_w8, 2)
                with pool.Fori(0, NIT) as it:
                    pool.wait_ge(s_adt, 2 * it + 2)
                    pool.wait_ge(s_seg, SEGB * it + SEGB)
                    pool.tensor_tensor(segr[:, :, :], adt[:, :, :].rearrange("p t h -> p (t h)").unsqueeze(2).to_broadcast([P, TT * HG, L]),
                                       sh.mask_le[:, :].unsqueeze(1).to_broadcast([P, TT * HG, L]), ALU.mult).then_inc(s_segr, 1)
                    for n in range(CPI * OT):
                        pool.wait_ge(s_pick, CPI * OT * it + n + 1)
                        pool.wait_ge(s_w8, CPI * OT * it + n + 2)
                        pool.tensor_tensor(sh.w8[:, n % OT, :], sh.w8[:, n % OT, :], pick[:, n % 2, :], ALU.add).then_inc(s_w8, 1)
                    pool.wait_ge(s_rv, it + 2)
                    pool.tensor_tensor(r[:, :], rv[:, :], sh.neg_half[:, 0:TT], ALU.pow).then_inc(s_r, 1)

            @block.tensor
            def _(pe):
                pe.sem_inc(s_wps, NWC)
                pe.sem_inc(s_seg, SEGB)
                with pe.Fori(0, G) as g:
                    pe.wait_ge(s_acc, TT * NBLK * g + TT)
                    pe.wait_ge(s_z, CT * NBLK * g + CT)
                    for n in range(NWC):
                        slot = n % NSTAGE
                        per = (NWC - slot + NSTAGE - 1) // NSTAGE
                        pe.wait_ge(s_stage[slot], 16 * (per * g + n // NSTAGE + 1))
                        if n >= 3:
                            pe.wait_ge(s_wlo, NWC * g + n - 2)
                        for k in range(KC):
                            ins = pe.transpose(bank[n % 3][:, k * P:(k + 1) * P], stage[slot][:, k * P:(k + 1) * P], sh.ident[:, :])
                        ins.then_inc(s_wps, 1)
                    with pe.Fori(0, NBLK) as j:
                        it = NBLK * g + j

                        def project(n):
                            pb = bank[PROJ_BANK[n]]
                            for q, (l, rr) in enumerate(PASSES):
                                for k in range(KC):
                                    ins = pe.matmul(pb[:, :], wt[:, l, k, n * P:(n + 1) * P], ht[:, rr, k, :],
                                                    start=(q == 0 and k == 0), stop=(q == 2 and k == KC - 1))
                            return ins

                        pe.wait_ge(s_wlo, NWC * g + NWC)
                        pe.wait_ge(s_ht, 16 * it + 16)
                        pe.wait_ge(s_z, CT * it + CT)
                        pe.wait_ge(s_acc, TT * it + TT)
                        for n in range(NCV):
                            if n >= 3:
                                pe.wait_ge(s_conv, NCV * it + n - 2)
                            project(n).then_inc(s_proj, 1)
                        pe.wait_ge(s_segr, it + 2)
                        pe.wait_ge(s_y, CT * it + CT)
                        for q in range(SEGB):
                            pe.matmul(bank[SEG[q]][:, :], sh.mask_gt[:, :],
                                      segr[:, q * 2 * HG:(q + 1) * 2 * HG, :].rearrange("p h l -> p (h l)"),
                                      start=True, stop=True).then_inc(s_seg, 1)
                        pe.wait_ge(s_conv, NCV * it + 4)
                        project(NCV).then_inc(s_proj, 1)
                        pe.wait_ge(s_silu, NCV * it + NCV)
                        for t in range(TT):
                            if t >= 2:
                                pe.wait_ge(s_dtx, TT * it + t - 1)
                            for c in range(CT):
                                ins = pe.transpose(bank[XT[t % 2]][:, c * P:(c + 1) * P], xc[:, 2 + c, t * P:(t + 1) * P], sh.ident[:, :])
                            ins.then_inc(s_xt, 1)
                        pe.wait_ge(s_rv, it + 1)
                        for t in range(TT):
                            ins = pe.matmul(bank[CB][:, t * P:(t + 1) * P], xc[:, 0, t * P:(t + 1) * P], xc[:, 1, t * P:(t + 1) * P],
                                            start=True, stop=True)
                        ins.then_inc(s_cb, 1)
                        for c in range(1, CT):
                            if c < 3:
                                pe.wait_ge(s_conv, NCV * it + 4 + c)
                            else:
                                pe.wait_ge(s_z, CT * it + CT + 2)
                            project(NCV + c).then_inc(s_proj, 1)
                        for c in range(CT):
                            if c == 0:
                                pe.wait_ge(s_cbm, it + 1)
                            elif c == 1:
                                pe.wait_ge(s_exp, SEGB * it + SEGB)
                            else:
                                pe.wait_ge(s_y, CT * it + CT + c - 1)
                            for u in range(2):
                                for t in range(TT):
                                    if c == 0 and u == 0:
                                        pe.wait_ge(s_m, TT * it + t + 1)
                                    h = 2 * c + u
                                    ins = pe.matmul(bank[YB[c % 2]][u * HP:(u + 1) * HP, t * P:(t + 1) * P], dtx[:, t, h * HP:(h + 1) * HP],
                                                    m[:, t, h, :], start=True, stop=True)
                            ins.then_inc(s_yp, 1)
                        pe.wait_ge(s_z, CT * it + CT + 3)
                        pe.wait_ge(s_dtx, TT * it + TT)
                        for c in range(CT):
                            if c == CT - 1:
                                pe.wait_ge(s_y, CT * it + CT + 3)
                                pe.wait_ge(s_sq, CT * it + CT)
                                for t in range(TT):
                                    for cc in range(CT):
                                        ins = pe.matmul(bank[SSQ][:, t:t + 1], y[:, cc, t * P:(t + 1) * P], sh.ones_col[:, 0:1],
                                                        start=(cc == 0), stop=(cc == CT - 1))
                                ins.then_inc(s_ssq, 1)
                            pe.wait_ge(s_ulo, CT * it + c + 1)
                            for t in range(TT):
                                for q, (l, rr) in enumerate(PASSES):
                                    ins = pe.matmul(bank[OUT[t]][:, :], gy[:, l, c, t * P:(t + 1) * P], wot[:, rr, c, :],
                                                    start=(c == 0 and q == 0), stop=(c == CT - 1 and q == 2))
                                if c == CT - 1:
                                    ins.then_inc(s_out, 1)

            @block.scalar
            def _(act):
                act.sem_inc(s_z, CT)
                with act.Fori(0, G) as g:
                    for n in range(NWC):
                        if n < NCV + CT:
                            act.wait_ge(s_wps, NWC * g + NWC + n + 1)
                            act.activation(wt[:, 0, :, n * P:(n + 1) * P], bank[n % 3][:, :].rearrange("p (k c) -> p k c", k=KC),
                                           ACT.Copy).then_inc(s_whi, 1)
                        else:
                            k = n - NCV - CT
                            act.wait_ge(s_wosc, KC * g + k + 1)
                            act.activation(wot[:, 0, :, k * P:(k + 1) * P], wo_tmp[:, :, :], ACT.Copy).then_inc(s_whi, 1)
                    act.wait_ge(s_par, 16 * NPAR * (g + 1))
                    with act.Fori(0, NBLK) as j:
                        it = NBLK * g + j

                        def silu(n):
                            act.wait_ge(s_conv, NCV * it + n + 1)
                            act.activation(xc[:, n, :], xc[:, n, :], ACT.Silu).then_inc(s_silu, 1)

                        for n in range(NCV):
                            act.wait_ge(s_proj, (NCV + CT) * it + n + 1)
                            act.activation(xc[:, n, :], bank[PROJ_BANK[n]][:, :], ACT.Identity, bias=cvb[:, n:n + 1],
                                           scale=cvw[:, n, TAPS - 1:TAPS]).then_inc(s_tap, 1)
                            if n:
                                silu(n - 1)
                        silu(NCV - 1)
                        for c in range(CT):
                            if c == 1:
                                for q in range(SEGB):
                                    act.wait_ge(s_seg, SEGB * it + SEGB + q + 1)
                                    act.activation(decay[:, 2 * q:2 * q + 2, :, :].rearrange("p t h l -> p (t h l)"),
                                                   bank[SEG[q]][:, :], ACT.Exp).then_inc(s_exp, 1)
                            act.wait_ge(s_proj, (NCV + CT) * it + NCV + c + 1)
                            act.activation(z[:, c, :], bank[PROJ_BANK[NCV + c]][:, :], ACT.Silu).then_inc(s_z, 1)
                        for c in range(CT):
                            act.wait_ge(s_u, CT * it + c + 1)
                            act.activation(gy[:, 0, c, :], z[:, c, :], ACT.Copy).then_inc(s_uhi, 1)
                            act.activation(y[:, c, :], y[:, c, :], ACT.Square).then_inc(s_sq, 1)

            @block.vector
            def _(dve):
                dve.sem_inc(s_y, CT)
                dve.sem_inc(s_acc, TT)
                dve.sem_inc(s_rv, 1)
                with dve.Fori(0, G) as g:
                    dve.wait_ge(s_par, 16 * NPAR * (g + 1))
                    for n in range(NWC):
                        if n < NCV + CT:
                            dve.wait_ge(s_whi, NWC * g + n + 1)
                            dve.tensor_tensor(wt[:, 1, :, n * P:(n + 1) * P], bank[n % 3][:, :].rearrange("p (k c) -> p k c", k=KC),
                                              wt[:, 0, :, n * P:(n + 1) * P].bitcast(F32), ALU.subtract).then_inc(s_wlo, 1)
                        else:
                            k = n - NCV - CT
                            dve.wait_ge(s_wps, NWC * g + NWC + n + 1)
                            dve.wait_ge(s_wlo, NWC * g + n)
                            dve.tensor_tensor(wo_tmp[:, :, :], bank[n % 3][:, :].rearrange("p (c d) -> p c d", c=CT),
                                              nw[:, :].unsqueeze(2).to_broadcast([P, CT, P]), ALU.mult).then_inc(s_wosc, 1)
                            dve.wait_ge(s_whi, NWC * g + n + 1)
                            dve.wait_ge(s_wosc, KC * g + k + 1)
                            dve.tensor_tensor(wot[:, 1, :, k * P:(k + 1) * P], wo_tmp[:, :, :],
                                              wot[:, 0, :, k * P:(k + 1) * P].bitcast(F32), ALU.subtract).then_inc(s_wlo, 1)
                    with dve.Fori(0, NBLK) as j:
                        it = NBLK * g + j
                        picked = [0]

                        def pick8(count=1):
                            for _ in range(count):
                                n = picked[0]
                                picked[0] += 1
                                dve.wait_ge(s_w8, CPI * OT * it + n + 1)
                                dve.tensor_scalar(pick[:, n % 2, :], sh.code8[:, n % OT, :], sh.code_no[:, ds(CPI * it + n // OT, 1)],
                                                  sh.lut8[:, n % OT, ds(CPI * it + n // OT, 1)], ALU.is_equal, ALU.mult).then_inc(s_pick, 1)

                        dve.wait_ge(s_segr, it + 1)
                        dve.tensor_tensor(adt[:, :, :], sh.dt[:, ds(TT * j, TT), ds(HG * g, HG)],
                                          sh.neg_a[:, ds(HG * g, HG)].unsqueeze(1).to_broadcast([P, TT, HG]), ALU.mult).then_inc(s_adt, 1)
                        dve.wait_ge(s_adt, 2 * it + 1)
                        dve.tensor_scalar(adt[:, :, :], adt[:, :, :], DECAY_FLOOR, None, ALU.max).then_inc(s_adt, 1)
                        for n in range(NCV):
                            dve.wait_ge(s_tap, NCV * it + n + 1)
                            for k in range(1, TAPS):
                                src = bank[PROJ_BANK[n]][:, :].rearrange("p (b l) -> p b l", l=L)[:, :, 0:L - k]
                                dst = xc[:, n, :].rearrange("p (b l) -> p b l", l=L)[:, :, k:L]
                                ins = dve.scalar_tensor_tensor(dst, src, cvw[:, n, TAPS - 1 - k:TAPS - k], dst, ALU.mult, ALU.add)
                                if k < TAPS - 1:
                                    ins.then_inc(s_cvstep, 1)
                                    dve.wait_ge(s_cvstep, (TAPS - 2) * (NCV * it + n) + k)
                            ins.then_inc(s_conv, 1)
                            pick8()
                        for t in range(TT):
                            dve.wait_ge(s_xt, TT * it + t + 1)
                            dve.tensor_tensor(dtx[:, t, :].rearrange("p (h c) -> p h c", h=HG),
                                              bank[XT[t % 2]][:, :].rearrange("p (h c) -> p h c", h=HG),
                                              sh.dt[:, ds(TT * j + t, 1), ds(HG * g, HG)].rearrange("p o h -> p (o h)").unsqueeze(2).to_broadcast([P, HG, HP]),
                                              ALU.mult).then_inc(s_dtx, 1)
                        dve.wait_ge(s_cb, it + 1)
                        dve.tensor_tensor(cbm[:, :, :], bank[CB][:, :].rearrange("p (t n) -> p t n", t=TT),
                                          sh.mask_cb[:, :].unsqueeze(1).to_broadcast([P, TT, P]), ALU.mult).then_inc(s_cbm, 1)
                        dve.wait_ge(s_cbm, it + 1)
                        for t in range(TT):
                            dve.wait_ge(s_exp, SEGB * it + t // 2 + 1)
                            dve.tensor_tensor(m[:, t, :, :].rearrange("p h (c l) -> p h c l", l=L),
                                              cbm[:, t, :].rearrange("p (c l) -> p c l", l=L).unsqueeze(1).to_broadcast([P, HG, BT, L]),
                                              decay[:, t, :, :].unsqueeze(2).to_broadcast([P, HG, BT, L]), ALU.mult).then_inc(s_m, 1)
                            pick8()

                        def low(c):
                            dve.wait_ge(s_uhi, CT * it + c + 1)
                            dve.tensor_tensor(gy[:, 1, c, :], z[:, c, :], gy[:, 0, c, :].bitcast(F32), ALU.subtract).then_inc(s_ulo, 1)

                        for c in range(CT):
                            dve.wait_ge(s_yp, CT * it + c + 1)
                            dve.scalar_tensor_tensor(y[:, c, :], xc[:, 2 + c, :], dsk[:, c:c + 1], bank[YB[c % 2]][:, :],
                                                     ALU.mult, ALU.add).then_inc(s_y, 1)
                            dve.wait_ge(s_z, CT * it + CT + c + 1)
                            dve.wait_ge(s_y, CT * it + CT + c + 1)
                            dve.tensor_tensor(z[:, c, :], z[:, c, :], y[:, c, :], ALU.mult).then_inc(s_u, 1)
                            if c:
                                low(c - 1)
                        low(CT - 1)
                        pick8(CPI * OT - picked[0])
                        dve.wait_ge(s_ssq, it + 1)
                        dve.tensor_scalar(rv[:, :], bank[SSQ][:, 0:TT], 1.0 / GI, EPS, ALU.mult, ALU.add).then_inc(s_rv, 1)
                        dve.wait_ge(s_r, it + 1)
                        dve.wait_ge(s_accin, 16 * it + 16)
                        for t in range(TT):
                            dve.wait_ge(s_out, TT * it + t + 1)
                            dve.scalar_tensor_tensor(acc[:, t, :], bank[OUT[t]][:, :], r[:, t:t + 1], acc[:, t, :],
                                                     ALU.mult, ALU.add).then_inc(s_acc, 1)


def stage3(nc, a, sh, out):
    with ExitStack() as ctx:
        def sb(name, shape, dt=F32):
            return ctx.enter_context(nc.sbuf_tensor(name, shape, dt))

        def sem(name):
            return ctx.enter_context(nc.semaphore(name))

        w4 = sb("w4_nat", [P, OT, DM])
        wq = sb("wq", [P, 2, 2, KC, DM], F32R)
        cbn = sb("cbn", [P, CG, KW])
        cbd = sb("cbd", [P, KW, P])
        gmask = sb("gmask", [P, P])
        cbs = sb("cbs", [P, 2, KW, P], F32R)
        ctxp = sb("ctxp", [P, TOK // P])
        bias = sb("bias", [P, DM])
        x2 = sb("x2", [P, TT, DM])
        x2s = sb("x2s", [P, 2, TT, DM + 2 * PADW], F32R)
        xb = sb("x2b", [P, TT, DM])
        x3 = sb("x3", [P, TT, DM])
        sq = sb("sq", [P, DM])
        ssq = sb("ssq", [P, TT])
        hot = sb("hot", [P, TT])
        cold = sb("cold", [P, TT])
        x3t = sb("x3t", [P, 2, TT, KC, P], F32R)
        res = sb("res", [P, TT, DM])

        p_cv = [ctx.enter_context(nc.psum_tensor(f"p_cv{u}", [P, 512], F32)) for u in range(2)]
        p_tr = [ctx.enter_context(nc.psum_tensor(f"p_tr{u}", [P, 512], F32)) for u in range(2)]
        p_y = [[ctx.enter_context(nc.psum_tensor(f"p_y{u}{q}", [P, 512], F32)) for q in range(2)] for u in range(2)]

        s_w = sem("s3_w")
        s_zero = sem("s3_zero")
        s_cbn = sem("s3_cbn")
        s_cbd = sem("s3_cbd")
        s_cbhi = sem("s3_cbhi")
        s_cblo = sem("s3_cblo")
        s_wps = sem("s3_wps")
        s_whi = sem("s3_whi")
        s_wlo = sem("s3_wlo")
        s_x2 = sem("s3_x2")
        s_x2hi = sem("s3_x2hi")
        s_x2lo = sem("s3_x2lo")
        s_xb = sem("s3_xb")
        s_cv = sem("s3_cv")
        s_x3 = sem("s3_x3")
        s_sq = sem("s3_sq")
        s_hot = sem("s3_hot")
        s_tr = sem("s3_tr")
        s_x3hi = sem("s3_x3hi")
        s_x3lo = sem("s3_x3lo")
        s_y = sem("s3_y")
        s_half = sem("s3_half")
        s_fin = sem("s3_fin")
        s_out = sem("s3_out")

        with nc.Block() as block:
            x2_v = sh.acc_d.rearrange("(j t p) d -> j p t d", t=TT, p=P)
            out_v = out.rearrange("b i d -> (b i) d").rearrange("(j t p) d -> j p t d", t=TT, p=P)

            @block.sync
            def _(sp):
                sp.sem_inc(s_out, 16)
                sp.dma_start(w4[:, :, :].rearrange("p t i -> p (t i)"), sh.w4_d).then_inc(s_w, 16)
                sp.dma_start(ctxp[:, :], sh.ctxb_d.rearrange("(t c) o -> (c o) t", c=BT)).then_inc(s_w, 16)
                sp.dma_start(bias[:, :], a["L0_ffn_bias"].partition_broadcast(P)).then_inc(s_w, 16)

                def load(j):
                    sp.dma_start(x2[:, :, :], x2_v[ds(j, 1)].rearrange("o p t d -> p (o t) d")).then_inc(s_x2, 16)

                def store(j):
                    sp.wait_ge(s_fin, TT * (j + 1) + 2)
                    sp.dma_start(out_v[ds(j, 1)].rearrange("o p t d -> p (o t) d"), res[:, :, :]).then_inc(s_out, 16)

                load(0)
                w_v = a["L0_cond2_weight"].rearrange("(q o) i k -> q i o k", o=CG)
                for c in range(BT):
                    for q in range(L // CG):
                        lo = c * L + q * CG
                        sp.dma_start(cbn[lo:lo + CG, :, :], w_v[q]).then_inc(s_cbn, 16)
                with sp.Fori(0, NBLK - 1) as j:
                    sp.wait_ge(s_xb, TT * (j + 1))
                    load(j + 1)
                    store(j)
                store(NBLK - 1)
                sp.wait_ge(s_out, 16 * NBLK + 16)

            @block.gpsimd
            def _(pool):
                pool.memset(gmask[:, :], 1.0).then_inc(s_zero, 1)
                v = gmask[:, :].rearrange("p (q o) -> p q o", o=CG)
                for n, (base, step, cm) in enumerate(((0, -CG, 1), (CG - 1, CG, -1))):
                    pool.wait_ge(s_zero, n + 1)
                    pool.affine_select(out=v, in_=v, compare_op=ALU.is_ge, fill=0.0, base=base,
                                       pattern=[[step, P // CG], [0, CG]], channel_multiplier=cm).then_inc(s_zero, 1)
                pool.memset(x2s[:, :, :, 0:PADW].bitcast(F32), 0.0).then_inc(s_zero, 1)
                pool.memset(x2s[:, :, :, PADW + DM:].bitcast(F32), 0.0).then_inc(s_zero, 1)
                pool.wait_ge(s_w, 48)
                with pool.Fori(0, NBLK) as j:
                    for t in range(TT):
                        pool.wait_ge(s_x2hi, TT * j + t + 1)
                        pool.tensor_tensor(x2s[:, 1, t, PADW:PADW + DM], x2[:, t, :], x2s[:, 0, t, PADW:PADW + DM].bitcast(F32),
                                           ALU.subtract).then_inc(s_x2lo, 1)
                    for t in range(TT):
                        pool.wait_ge(s_fin, TT * j + 2)
                        pool.tensor_tensor(xb[:, t, :], x2[:, t, :], bias[:, :], ALU.add).then_inc(s_xb, 1)

            @block.tensor
            def _(pe):
                pe.sem_inc(s_cv, TT)
                pe.wait_ge(s_w, 48)
                n = 0
                for q, w in ((0, w4), (1, sh.w8)):
                    for k in range(KC):
                        if n >= 2:
                            pe.wait_ge(s_wlo, n - 1)
                        for t in range(OT):
                            ins = pe.transpose(p_tr[n % 2][:, t * P:(t + 1) * P], w[:, t, k * P:(k + 1) * P], sh.ident[:, :])
                        ins.then_inc(s_wps, 1)
                        n += 1
                pe.wait_ge(s_wlo, n)
                pe.wait_ge(s_cblo, 1)
                pe.wait_ge(s_zero, 5)
                with pe.Fori(0, NBLK) as j:
                    def conv(t):
                        pe.wait_ge(s_x2lo, TT * j + t + 1)
                        pe.wait_ge(s_x3, TT * j + t + 1)
                        for n, (l, rr) in enumerate(PASSES):
                            for k in range(KW):
                                ins = pe.matmul(p_cv[t % 2][:, :], cbs[:, l, k, :], x2s[:, rr, t, k:k + DM],
                                                start=(n == 0 and k == 0), stop=(n == 2 and k == KW - 1))
                        ins.then_inc(s_cv, 1)

                    def turn(t):
                        pe.wait_ge(s_x3, TT * j + t + 3)
                        pe.wait_ge(s_x3lo, TT * j + t + 1)
                        for k in range(KC):
                            ins = pe.transpose(p_tr[t % 2][:, k * P:(k + 1) * P], x3[:, t, k * P:(k + 1) * P], sh.ident[:, :])
                        ins.then_inc(s_tr, 1)

                    def ffn(t):
                        pe.wait_ge(s_x3lo, TT * j + t + 3)
                        pe.wait_ge(s_fin, TT * j + t + 1)
                        for q in range(2):
                            for n, (l, rr) in enumerate(PASSES):
                                for k in range(KC):
                                    ins = pe.matmul(p_y[t % 2][q][:, :], x3t[:, l, t, k, :], wq[:, q, rr, k, :],
                                                    start=(n == 0 and k == 0), stop=(n == 2 and k == KC - 1))
                        ins.then_inc(s_y, 1)

                    conv(0)
                    conv(1)
                    turn(0)
                    conv(2)
                    turn(1)
                    ffn(0)
                    conv(3)
                    turn(2)
                    ffn(1)
                    turn(3)
                    ffn(2)
                    ffn(3)

            @block.scalar
            def _(act):
                act.sem_inc(s_x3, 2)
                for n in range(2 * KC):
                    act.wait_ge(s_wps, n + 1)
                    act.activation(wq[:, n // KC, 0, n % KC, :], p_tr[n % 2][:, :], ACT.Copy).then_inc(s_whi, 1)
                act.wait_ge(s_cbd, 1)
                act.activation(cbs[:, 0, :, :], cbd[:, :, :], ACT.Copy).then_inc(s_cbhi, 1)
                with act.Fori(0, NBLK) as j:
                    act.wait_ge(s_x2, 16 * j + 16)
                    for t in range(TT):
                        act.wait_ge(s_cv, TT * j + t + 1)
                        act.activation(x2s[:, 0, t, PADW:PADW + DM], x2[:, t, :], ACT.Copy).then_inc(s_x2hi, 1)

                    def evac(t):
                        act.wait_ge(s_cv, TT * j + TT + t + 1)
                        act.activation(x3[:, t, :], p_cv[t % 2][:, :], ACT.Identity, bias=ctxp[:, ds(TT * j + t, 1)]).then_inc(s_x3, 1)
                        act.wait_ge(s_x3, TT * j + t + 3)
                        act.activation(sq[:, :], x3[:, t, :], ACT.Square, accum_out=ssq[:, t:t + 1]).then_inc(s_sq, 1)

                    def high(t):
                        act.wait_ge(s_tr, TT * j + t + 1)
                        act.activation(x3t[:, 0, t, :, :].rearrange("p k n -> p (k n)"), p_tr[t % 2][:, :], ACT.Copy).then_inc(s_x3hi, 1)

                    evac(0)
                    evac(1)
                    high(0)
                    evac(2)
                    high(1)
                    evac(3)
                    high(2)
                    high(3)

            @block.vector
            def _(dve):
                dve.sem_inc(s_x3lo, 2)
                dve.wait_ge(s_cbn, 16 * BT * (L // CG))
                dve.wait_ge(s_zero, 3)
                q = P // CG
                dve.tensor_tensor(cbd[:, :, :].rearrange("p k (q o) -> p k q o", o=CG),
                                  cbn[:, :, :].rearrange("p o k -> p k o").unsqueeze(2).to_broadcast([P, KW, q, CG]),
                                  gmask[:, :].rearrange("p (q o) -> p q o", o=CG).unsqueeze(1).to_broadcast([P, KW, q, CG]),
                                  ALU.mult).then_inc(s_cbd, 1)
                dve.sem_inc(s_fin, 2)
                for n in range(2 * KC):
                    dve.wait_ge(s_whi, n + 1)
                    dve.tensor_tensor(wq[:, n // KC, 1, n % KC, :], p_tr[n % 2][:, :], wq[:, n // KC, 0, n % KC, :].bitcast(F32),
                                      ALU.subtract).then_inc(s_wlo, 1)
                dve.wait_ge(s_cbhi, 1)
                dve.tensor_tensor(cbs[:, 1, :, :], cbd[:, :, :], cbs[:, 0, :, :].bitcast(F32), ALU.subtract).then_inc(s_cblo, 1)
                with dve.Fori(0, NBLK) as j:
                    def low(t):
                        dve.wait_ge(s_x3hi, TT * j + t + 1)
                        dve.tensor_tensor(x3t[:, 1, t, :, :].rearrange("p k n -> p (k n)"), p_tr[t % 2][:, :],
                                          x3t[:, 0, t, :, :].rearrange("p k n -> p (k n)").bitcast(F32), ALU.subtract).then_inc(s_x3lo, 1)

                    def choose(t):
                        dve.wait_ge(s_sq, TT * j + t + 1)
                        dve.tensor_scalar(hot[:, t:t + 1], ssq[:, t:t + 1], MASK_T2, None, ALU.is_gt).then_inc(s_hot, 1)
                        dve.tensor_scalar(cold[:, t:t + 1], ssq[:, t:t + 1], MASK_T2, None, ALU.is_le).then_inc(s_hot, 1)

                    def finish(t):
                        dve.wait_ge(s_y, TT * j + t + 1)
                        dve.wait_ge(s_xb, TT * j + t + 1)
                        dve.wait_ge(s_hot, 2 * (TT * j + t + 1))
                        if t == 0:
                            dve.wait_ge(s_out, 16 * j + 16)
                        dve.scalar_tensor_tensor(res[:, t, :], p_y[t % 2][1][:, :], hot[:, t:t + 1], xb[:, t, :],
                                                 ALU.mult, ALU.add).then_inc(s_half, 1)
                        dve.wait_ge(s_half, TT * j + t + 1)
                        dve.scalar_tensor_tensor(res[:, t, :], p_y[t % 2][0][:, :], cold[:, t:t + 1], res[:, t, :],
                                                 ALU.mult, ALU.add).then_inc(s_fin, 1)

                    choose(0)
                    choose(1)
                    low(0)
                    choose(2)
                    low(1)
                    choose(3)
                    low(2)
                    finish(0)
                    low(3)
                    finish(1)
                    finish(2)
                    finish(3)


def build(nc, a, out):
    sh = Shared()
    with ExitStack() as ctx:
        def sb(name, shape, dt=F32):
            return ctx.enter_context(nc.sbuf_tensor(name, shape, dt))

        ctx.enter_context(nc.allow_non_contiguous_dma(reason="parameters laid out by channel, a few KB"))
        sh.ident = sb("ident", [P, P])
        sh.mask_cb = sb("mask_cb", [P, P])
        sh.mask_gt = sb("mask_gt", [P, P])
        sh.mask_le = sb("mask_le", [P, L])
        sh.neg_half = sb("neg_half", [P, TT])
        sh.ones_col = sb("ones_col", [P, 2])
        sh.code_no = sb("code_no", [P, NCODE])
        sh.dt = sb("dt_all", [P, TOK // P, H])
        sh.neg_a = sb("neg_a", [P, H])
        sh.code8 = sb("code8", [P, OT, DM], BF16)
        sh.lut8 = sb("lut8", [P, OT, NCODE])
        sh.w8 = sb("w8", [P, OT, DM])
        sh.h_d = nc.dram_tensor("h_d", (NBLK, P, 2 * KC * BLK), F32).ap()
        sh.acc_d = nc.dram_tensor("acc_d", (TOK, DM), F32).ap()
        sh.agg_d = nc.dram_tensor("agg_d", (NB, L, L), F32).ap()
        sh.aggb_d = nc.dram_tensor("aggb_d", (NB, L), F32).ap()
        sh.ctxb_d = nc.dram_tensor("ctxb_d", (NB, L), F32).ap()
        sh.w4_d = nc.dram_tensor("w4_d", (P, OT * DM), F32).ap()
        stage1(nc, a, sh)
        stage2(nc, a, sh)
        stage3(nc, a, sh, out)


_INS = ["x", "cond_128", "fside_S_0", "L0_cond_W0", "L0_cond_b0", "L0_cond_W1", "L0_cond_b1", "L0_cond_W2", "L0_cond_b2",
        "L0_cond_weight", "L0_cond_bias_k", "L0_attn_in_proj_w", "L0_attn_conv_weight", "L0_attn_conv_bias",
        "L0_attn_dt_bias", "L0_attn_A_log", "L0_attn_D", "L0_attn_norm_weight", "L0_attn_out_proj_w",
        "L0_cond2_weight", "L0_cond2_c_weight", "L0_ffn_qweight", "L0_ffn_lut4", "L0_ffn_lut8", "L0_ffn_bias"]


def kernel(**inputs):
    import numpy as np
    import concourse.bacc as bacc
    from concourse.bass_utils import run_bass_kernel_spmd

    nc = bacc.Bacc("TRN2", target_bir_lowering=False, num_devices=1)
    arrays, aps = {}, {}
    for name in _INS:
        v = np.ascontiguousarray(inputs[name])
        arrays[f"in_{name}"] = v
        aps[name] = nc.dram_tensor(f"in_{name}", v.shape, mybir.dt.from_np(v.dtype), kind="ExternalInput").ap()
    out = nc.dram_tensor("out_0", (NB, L, DM), F32, kind="ExternalOutput").ap()
    build(nc, aps, out)
    got = run_bass_kernel_spmd(nc, [arrays], core_ids=[0])
    return got.results[0]["out_0"]
```

```python
from contextlib import ExitStack

import concourse.bass as bass
from concourse import mybir

F32 = mybir.dt.float32
F32R = mybir.dt.float32r
BF16 = mybir.dt.bfloat16
I32 = mybir.dt.int32
ALU = mybir.AluOpType
ACT = mybir.ActivationFunctionType
AX = mybir.AxisListType
ds = bass.ds

P = 128
NB, L, DM = 128, 32, 512
TOK = NB * L
BLK = 512
NBLK = TOK // BLK
TT = BLK // P
BT = P // L
KC = DM // P
H, HP, NS, G = 64, 64, 128, 8
INNER = H * HP
GN = G * NS
CONV = INNER + 2 * GN
HG = H // G
GI = INNER // G
CT = GI // P
TAPS = 4
EPS = 1e-5
NEXP = 8
NCODE = 256
OT = DM // P
NIT = G * NBLK
CPI = NCODE // NIT
KW = 9
PADW = KW // 2
CG = 8
MASK_T2 = 64.0 * 64.0 * (1.0 + 2.0 ** -23)
DECAY_FLOOR = -200.0
LOGA_CAP = 85.0

PASSES = ((0, 0), (0, 1), (1, 0))
NCV = 2 + CT
NWC = NCV + CT + KC
C4 = 16 // NBLK
SEGB = TT * HG * L // 512
NSTAGE = 4
PROJ_BANK = (0, 1, 2, 0, 1, 2, 0, 1, 2, 0)


class Shared:
    pass


def stage1(nc, a, sh):
    with ExitStack() as ctx:
        def sb(name, shape, dt=F32):
            return ctx.enter_context(nc.sbuf_tensor(name, shape, dt))

        def sem(name):
            return ctx.enter_context(nc.semaphore(name))

        cond = sb("cond", [NB, 128])
        cond_t = sb("cond_t", [128, NB])
        cw = sb("cw", [L, 128])
        cw_t = sb("cw_t", [128, L])
        w0 = sb("w0", [128, 128])
        w1 = sb("w1", [128, 128])
        b0 = sb("b0", [128, 1])
        b1 = sb("b1", [128, 1])
        w2 = sb("w2", [128, NEXP])
        b2 = sb("b2", [NB, NEXP])
        experts = sb("experts", [NEXP, L * L])
        bias_k = sb("bias_k", [NEXP, L])
        side = sb("side", [NB, L])
        h1 = sb("h1", [128, NB])
        h2 = sb("h2", [128, NB])
        logit = sb("logit", [NB, NEXP])
        nmax = sb("nmax", [NB, 1])
        esum = sb("esum", [NB, 1])
        erec = sb("erec", [NB, 1])
        att = sb("att", [NB, NEXP])
        att_t = sb("att_t", [NEXP, NB])
        agg = sb("agg", [NB, L, L])
        aggb = sb("aggb", [NB, L])
        ctxb = sb("ctxb", [NB, L])
        mix = sb("mix", [P, NBLK * TT, P])
        aggb_row = sb("aggb_row", [1, TOK])
        ones_row = sb("ones_row", [1, P])
        wdt = sb("wdt", [H, DM])
        wdt_t = sb("wdt_t", [P, 2, KC, H], F32R)
        dtb = sb("dtb", [P, H])
        alog = sb("alog", [P, H])
        xb = [sb(f"xb{u}", [P, TT, DM]) for u in range(2)]
        ht = [sb(f"ht_out{u}", [P, 2, KC, BLK], F32R) for u in range(2)]
        sp_e = sb("sp_e", [P, NBLK * TT * H])
        qw = sb("qw", [P, OT, 8, 16], I32)
        bits = sb("bits", [P, OT * 4 * 16, 32], I32)
        code = sb("code", [P, OT, DM])
        code4 = sb("code4", [P, OT, DM])
        lut4 = sb("lut4", [P, OT, 16])
        pick = sb("pick", [P, 2, DM])
        w4 = sb("w4", [P, OT, DM])

        p_mlp = ctx.enter_context(nc.psum_tensor("p_mlp", [P, 512], F32))
        p_agg = [ctx.enter_context(nc.psum_tensor(f"p_agg{u}", [P, 512], F32)) for u in range(2)]
        p_wdt = ctx.enter_context(nc.psum_tensor("p_wdt", [P, 512], F32))
        p_h = [ctx.enter_context(nc.psum_tensor(f"p_h{u}", [P, 512], F32)) for u in range(2)]
        p_dt = [ctx.enter_context(nc.psum_tensor(f"p_dt{u}", [P, 512], F32)) for u in range(2)]

        s_ld = sem("s1_loaded")
        s_q = sem("s1_q_loaded")
        s_const = sem("s1_const")
        s_pe = sem("s1_pe")
        s_act = sem("s1_act")
        s_dve = sem("s1_dve")
        s_rt = sem("s1_roundtrip")
        s_mix = sem("s1_mix")
        s_x = [sem(f"s1_x{u}") for u in range(2)]
        s_hp = sem("s1_hp")
        s_hi = sem("s1_hi")
        s_lo = sem("s1_lo")
        s_hst = [sem(f"s1_hst{u}") for u in range(2)]
        s_dtp = sem("s1_dtp")
        s_dtv = sem("s1_dtv")
        s_spa = sem("s1_spa")
        s_spv = sem("s1_spv")
        s_bits = sem("s1_bits")
        s_pick = sem("s1_pick")
        s_w4 = sem("s1_w4")

        with nc.Block() as block:

            @block.sync
            def _(sp):
                small = [(cond[:, :], a["cond_128"]), (cw[:, :], a["L0_cond2_c_weight"]),
                         (w0[:, :], a["L0_cond_W0"]), (w1[:, :], a["L0_cond_W1"]),
                         (b0[:, :], a["L0_cond_b0"].rearrange("(p o) -> p o", o=1)),
                         (b1[:, :], a["L0_cond_b1"].rearrange("(p o) -> p o", o=1)),
                         (w2[:, :], a["L0_cond_W2"]),
                         (b2[:, :], a["L0_cond_b2"].partition_broadcast(NB)),
                         (experts[:, :], a["L0_cond_weight"].rearrange("k o i u -> k (o i u)")),
                         (bias_k[:, :], a["L0_cond_bias_k"]),
                         (side[:, :], a["fside_S_0"].partition_broadcast(NB)),
                         (wdt[:, :], a["L0_attn_in_proj_w"][INNER + CONV:INNER + CONV + H, :]),
                         (dtb[:, :], a["L0_attn_dt_bias"].partition_broadcast(P)),
                         (alog[:, :], a["L0_attn_A_log"].partition_broadcast(P))]
                for dst, src in small:
                    sp.dma_start(dst, src).then_inc(s_ld, 16)
                sh.n_small = 16 * len(small)
                x_blk = a["x"].rearrange("b i d -> (b i) d").rearrange("(j t p) d -> j p t d", t=TT, p=P)

                def load_x(j, u):
                    sp.dma_start(xb[u][:, :, :], x_blk[ds(j, 1)].rearrange("o p t d -> p (o t) d")).then_inc(s_x[u], 16)

                for u in range(2):
                    sp.sem_inc(s_hst[u], 16)
                    load_x(u, u)
                sp.wait_ge(s_dve, 9)
                sp.dma_start(sh.agg_d.rearrange("b i o -> b (i o)"), agg[:, :, :].rearrange("b i o -> b (i o)")).then_inc(s_rt, 16)
                sp.dma_start(sh.aggb_d, aggb[:, :]).then_inc(s_rt, 16)
                sp.dma_start(sh.ctxb_d, ctxb[:, :]).then_inc(s_rt, 16)
                sp.wait_ge(s_rt, 48)
                sp.wait_ge(s_const, 4)
                agg_v = sh.agg_d.rearrange("(t c) i o -> c i t o", c=BT)
                for c in range(BT):
                    sp.dma_start(mix[c * L:(c + 1) * L, :, c * L:(c + 1) * L], agg_v[c]).then_inc(s_mix, 16)
                sp.dma_start(aggb_row[:, :], sh.aggb_d.rearrange("(u b) o -> u (b o)", u=1)).then_inc(s_mix, 16)
                with sp.Fori(0, NBLK // 2 - 1) as jj:
                    for u in range(2):
                        sp.wait_ge(s_hp, KC * (2 * jj + u + 1))
                        load_x(2 * jj + u + 2, u)
                        sp.wait_ge(s_lo, KC * (2 * jj + u + 1) + 2)
                        sp.dma_start(sh.h_d[ds(2 * jj + u, 1)].rearrange("o p n -> p (o n)"),
                                     ht[u][:, :, :, :].rearrange("p a k n -> p (a k n)").bitcast(F32)).then_inc(s_hst[u], 16)
                for u in range(2):
                    sp.wait_ge(s_lo, KC * (NBLK - 2 + u + 1) + 2)
                    sp.dma_start(sh.h_d[NBLK - 2 + u], ht[u][:, :, :, :].rearrange("p a k n -> p (a k n)").bitcast(F32)).then_inc(s_hst[u], 16)
                for u in range(2):
                    sp.wait_ge(s_hst[u], 16 * (NBLK // 2) + 16)
                sp.wait_ge(s_pick, 2 * 16 * OT)
                sp.dma_start(sh.w4_d, w4[:, :, :].rearrange("p t i -> p (t i)")).then_inc(s_rt, 16)
                sp.wait_ge(s_rt, 64)

            @block.gpsimd
            def _(pool):
                q_v = a["L0_ffn_qweight"].rearrange("n (t p) w -> t p n w", p=P)
                for t in range(OT):
                    pool.dma_start(qw[:, t, :, :], q_v[t]).then_inc(s_q, 16)
                pool.dma_start(lut4[:, :, :], a["L0_ffn_lut4"].rearrange("(t p) c -> p t c", p=P)).then_inc(s_q, 16)
                pool.dma_start(sh.lut8[:, :, :], a["L0_ffn_lut8"].rearrange("(t p) c -> p t c", p=P)).then_inc(s_q, 16)
                pool.memset(sh.ident[:, :], 0.0).then_inc(s_const, 1)
                pool.memset(ones_row[:, :], 1.0).then_inc(s_const, 1)
                pool.wait_ge(s_const, 2)
                pool.affine_select(out=sh.ident[:, :], in_=sh.ident[:, :], compare_op=ALU.not_equal, fill=1.0,
                                   base=0, pattern=[[-1, P]], channel_multiplier=1).then_inc(s_const, 1)
                pool.memset(mix[:, :, :], 0.0).then_inc(s_const, 1)
                pool.iota(sh.code_no[:, :], pattern=[[1, NCODE]], base=0, channel_multiplier=0,
                          allow_small_or_imprecise_dtypes=True).then_inc(s_const, 1)
                pool.memset(sh.mask_cb[:, :], 1.0).then_inc(s_const, 1)
                pool.memset(sh.mask_gt[:, :], 1.0).then_inc(s_const, 1)
                pool.wait_ge(s_const, 7)
                n = 7
                for m, tri in ((sh.mask_cb, "le"), (sh.mask_gt, "gt")):
                    v = m[:, :].rearrange("p (c l) -> p c l", l=L)
                    sel = [(0, [[-L, BT], [0, L]], 1), (L - 1, [[L, BT], [0, L]], -1)]
                    sel.append((0, [[L, BT], [1, L]], -1) if tri == "le" else (-1, [[-L, BT], [-1, L]], 1))
                    for base, pat, cm in sel:
                        pool.affine_select(out=v, in_=v, compare_op=ALU.is_ge, fill=0.0, base=base, pattern=pat,
                                           channel_multiplier=cm).then_inc(s_const, 1)
                        n += 1
                        pool.wait_ge(s_const, n)
                pool.memset(sh.neg_half[:, :], -0.5).then_inc(s_const, 1)
                pool.memset(sh.ones[:, :], 1.0).then_inc(s_const, 1)
                pool.memset(sh.w8[:, :, :], 0.0).then_inc(s_const, 1)
                pool.wait_ge(s_q, 16 * (OT + 2))

            @block.tensor
            def _(pe):
                pe.wait_ge(s_ld, sh.n_small)
                pe.wait_ge(s_const, 4)
                pe.transpose(p_mlp[:, 0:NB], cond[:, :], sh.ident[:, :])
                pe.transpose(p_mlp[:, NB:NB + L], cw[:, :], sh.ident[0:L, 0:L]).then_inc(s_pe, 1)
                for k in range(KC):
                    ins = pe.transpose(p_wdt[:, k * H:(k + 1) * H], wdt[:, k * P:(k + 1) * P], sh.ident[0:H, 0:H])
                ins.then_inc(s_pe, 1)
                pe.wait_ge(s_dve, 2)
                pe.matmul(p_mlp[:, 160:160 + L], cond_t[:, :], cw_t[:, :], start=True, stop=True).then_inc(s_pe, 1)
                pe.matmul(p_mlp[:, 256:256 + NB], w0[:, :], cond_t[:, :], start=True, stop=True).then_inc(s_pe, 1)
                pe.wait_ge(s_act, 2)
                pe.matmul(p_mlp[:, 384:384 + NB], w1[:, :], h1[:, :], start=True, stop=True).then_inc(s_pe, 1)
                pe.wait_ge(s_act, 3)
                pe.matmul(p_mlp[:, 192:192 + NEXP], h2[:, :], w2[:, :], start=True, stop=True).then_inc(s_pe, 1)
                pe.wait_ge(s_dve, 7)
                pe.transpose(p_agg[0][0:NEXP, 0:NB], att[:, :], sh.ident[:, :]).then_inc(s_pe, 1)
                pe.wait_ge(s_dve, 8)
                for u in range(2):
                    pe.matmul(p_agg[u][:, :], att_t[:, :], experts[:, u * 512:(u + 1) * 512], start=True, stop=True)
                pe.matmul(p_mlp[:, 208:208 + L], att_t[:, :], bias_k[:, :], start=True, stop=True).then_inc(s_pe, 1)
                pe.wait_ge(s_mix, 16 * (BT + 1))
                with pe.Fori(0, NBLK // 2) as jj:
                    for u in range(2):
                        j = 2 * jj + u
                        pe.wait_ge(s_x[u], 16 * jj + 16)
                        for k in range(KC):
                            pe.wait_ge(s_lo, KC * j + k + 1)
                            for t in range(TT):
                                pe.matmul(p_h[k % 2][:, t * P:(t + 1) * P], xb[u][:, t, k * P:(k + 1) * P],
                                          mix[:, ds(TT * j + t, 1), :].rearrange("p o n -> p (o n)"),
                                          start=(t == 0), stop=False, skip_group_check=True)
                            pe.matmul(p_h[k % 2][:, :], ones_row[:, :], aggb_row[:, ds(BLK * j, BLK)],
                                      start=False, stop=True, skip_group_check=True).then_inc(s_hp, 1)
                        pe.wait_ge(s_lo, KC * (j + 1) + 2)
                        pe.wait_ge(s_dtv, j + 1)
                        for t in range(TT):
                            for n, (l, r) in enumerate(PASSES):
                                for k in range(KC):
                                    ins = pe.matmul(p_dt[u][:, t * H:(t + 1) * H], ht[u][:, l, k, t * P:(t + 1) * P],
                                                    wdt_t[:, r, k, :], start=(n == 0 and k == 0), stop=(n == 2 and k == KC - 1))
                        ins.then_inc(s_dtp, 1)

            @block.scalar
            def _(act):
                act.wait_ge(s_pe, 2)
                act.activation(wdt_t[:, 0, :, :].rearrange("p k h -> p (k h)"), p_wdt[:, 0:KC * H], ACT.Copy).then_inc(s_act, 1)
                act.wait_ge(s_pe, 4)
                act.activation(h1[:, :], p_mlp[:, 256:256 + NB], ACT.Gelu, bias=b0[:, :]).then_inc(s_act, 1)
                act.wait_ge(s_pe, 5)
                act.activation(h2[:, :], p_mlp[:, 384:384 + NB], ACT.Gelu, bias=b1[:, :]).then_inc(s_act, 1)
                act.wait_ge(s_dve, 5)
                act.activation(att[:, :], logit[:, :], ACT.Exp, bias=nmax[:, :], accum_out=esum[:, :]).then_inc(s_act, 1)
                with act.Fori(0, NBLK // 2) as jj:
                    for u in range(2):
                        j = 2 * jj + u
                        act.wait_ge(s_hst[u], 16 * jj + 16)
                        act.wait_ge(s_dtv, j + 1)
                        for k in range(KC):
                            act.wait_ge(s_hp, KC * j + k + 1)
                            act.activation(ht[u][:, 0, k, :], p_h[k % 2][:, :], ACT.Copy).then_inc(s_hi, 1)
                dtv = sh.dt[:, :, :].rearrange("p t h -> p (t h)")
                act.wait_ge(s_dtv, NBLK + 2)
                act.activation(sp_e[:, :], dtv, ACT.Abs).then_inc(s_spa, 1)
                act.wait_ge(s_spa, 1)
                act.activation(sp_e[:, :], sp_e[:, :], ACT.Exp, scale=-1.0).then_inc(s_spa, 1)
                act.wait_ge(s_spa, 2)
                act.activation(sp_e[:, :], sp_e[:, :], ACT.Ln, bias=1.0).then_inc(s_spa, 1)
                act.wait_ge(s_spv, 1)
                act.activation(sh.neg_a[:, :], alog[:, :], ACT.Exp).then_inc(s_spa, 1)

            @block.vector
            def _(dve):
                dve.sem_inc(s_lo, 2)
                dve.sem_inc(s_dtv, 2)
                dve.wait_ge(s_pe, 1)
                dve.tensor_copy(cond_t[:, :], p_mlp[:, 0:NB]).then_inc(s_dve, 1)
                dve.tensor_copy(cw_t[:, :], p_mlp[:, NB:NB + L]).then_inc(s_dve, 1)
                dve.wait_ge(s_act, 1)
                dve.tensor_tensor(wdt_t[:, 1, :, :].rearrange("p k h -> p (k h)"), p_wdt[:, 0:KC * H],
                                  wdt_t[:, 0, :, :].rearrange("p k h -> p (k h)").bitcast(F32), ALU.subtract).then_inc(s_dve, 1)
                dve.wait_ge(s_pe, 6)
                dve.tensor_tensor(logit[:, :], p_mlp[:, 192:192 + NEXP], b2[:, :], ALU.add).then_inc(s_dve, 1)
                dve.wait_ge(s_dve, 4)
                dve.tensor_reduce(nmax[:, :], logit[:, :], axis=AX.X, op=ALU.max, negate=True).then_inc(s_dve, 1)
                dve.wait_ge(s_act, 4)
                dve.reciprocal(erec[:, :], esum[:, :]).then_inc(s_dve, 1)
                dve.wait_ge(s_dve, 6)
                dve.tensor_scalar(att[:, :], att[:, :], erec[:, :], None, ALU.mult).then_inc(s_dve, 1)
                dve.wait_ge(s_pe, 7)
                dve.tensor_copy(att_t[:, :], p_agg[0][0:NEXP, 0:NB]).then_inc(s_dve, 1)
                dve.wait_ge(s_pe, 8)
                for u in range(2):
                    half = L // 2
                    dve.tensor_copy(agg[:, :, u * half:(u + 1) * half].rearrange("b i o -> b o i"),
                                    p_agg[u][:, :].rearrange("b (o i) -> b o i", i=L))
                dve.tensor_copy(aggb[:, :], p_mlp[:, 208:208 + L])
                dve.tensor_tensor(ctxb[:, :], p_mlp[:, 160:160 + L], side[:, :], ALU.add).then_inc(s_dve, 1)

                dve.wait_ge(s_q, 16 * (OT + 2))
                dve.wait_ge(s_const, 5)
                plane = bits[:, :, :].rearrange("p (t n w) s -> p t n (w s)", t=OT, n=4)
                n = 0
                for half in range(2):
                    if half:
                        dve.wait_ge(s_bits, n)
                    for s in range(32):
                        ins = dve.tensor_scalar(bits[:, :, s].rearrange("p (t n) -> p t n", t=OT),
                                                qw[:, :, 4 * half:4 * half + 4, :].rearrange("p t n w -> p t (n w)"), s, 1,
                                                ALU.logical_shift_right, ALU.bitwise_and)
                    ins.then_inc(s_bits, 1)
                    n += 1
                    for b in range(4):
                        dve.wait_ge(s_bits, n)
                        if half == 0 and b == 0:
                            ins = dve.tensor_copy(code4[:, :, :], plane[:, :, 0, :])
                        else:
                            ins = dve.scalar_tensor_tensor((sh.code8 if half and b == 3 else code4 if half == 0 else code)[:, :, :],
                                                           plane[:, :, b, :], float(1 << (4 * half + b)),
                                                           (code4 if half == 0 or b == 0 else code)[:, :, :], ALU.mult, ALU.add)
                        ins.then_inc(s_bits, 1)
                        n += 1
                dve.memset(w4[:, :, :], 0.0).then_inc(s_bits, 1)
                dve.wait_ge(s_bits, n + 1)
                dve.wait_ge(s_const, 16)
                dve.tensor_reduce(sh.mask_le[:, :], sh.mask_cb[:, :].rearrange("p (c l) -> p l c", l=L), axis=AX.X,
                                  op=ALU.add).then_inc(s_w4, 1)
                dve.wait_ge(s_w4, 1)
                with dve.Fori(0, NBLK // 2) as jj:
                    for u in range(2):
                        j = 2 * jj + u
                        for c in range(C4):
                            for t in range(OT):
                                n = 2 * (C4 * OT * j + c * OT + t)
                                dve.tensor_scalar(pick[:, t % 2, :], code4[:, t, :], sh.code_no[:, ds(C4 * j + c, 1)],
                                                  lut4[:, t, ds(C4 * j + c, 1)], ALU.is_equal, ALU.mult).then_inc(s_pick, 1)
                                dve.wait_ge(s_pick, n + 1)
                                dve.tensor_tensor(w4[:, t, :], w4[:, t, :], pick[:, t % 2, :], ALU.add).then_inc(s_pick, 1)
                        for k in range(KC):
                            dve.wait_ge(s_hi, KC * j + k + 1)
                            dve.tensor_tensor(ht[u][:, 1, k, :], p_h[k % 2][:, :], ht[u][:, 0, k, :].bitcast(F32),
                                              ALU.subtract).then_inc(s_lo, 1)
                        dve.wait_ge(s_dtp, j + 1)
                        dve.tensor_tensor(sh.dt[:, ds(TT * j, TT), :], p_dt[u][:, 0:TT * H].rearrange("p (t h) -> p t h", h=H),
                                          dtb[:, :].rearrange("p (o h) -> p o h", o=1).to_broadcast([P, TT, H]), ALU.add).then_inc(s_dtv, 1)
                dve.tensor_scalar(alog[:, :], alog[:, :], LOGA_CAP, None, ALU.min).then_inc(s_spv, 1)
                dve.wait_ge(s_spa, 3)
                dtv = sh.dt[:, :, :].rearrange("p t h -> p (t h)")
                dve.scalar_tensor_tensor(dtv, dtv, 0.0, sp_e[:, :], ALU.max, ALU.add).then_inc(s_spv, 1)
                dve.wait_ge(s_spa, 4)
                dve.wait_ge(s_spv, 2)
                dve.tensor_scalar(sh.neg_a[:, :], sh.neg_a[:, :], -1.0, None, ALU.mult).then_inc(s_spv, 1)
                dve.wait_ge(s_pick, 2 * 16 * OT)
                dve.wait_ge(s_spv, 3)


def stage2(nc, a, sh):
    with ExitStack() as ctx:
        def sb(name, shape, dt=F32):
            return ctx.enter_context(nc.sbuf_tensor(name, shape, dt))

        def sem(name):
            return ctx.enter_context(nc.semaphore(name))

        stage = [sb(f"stage{n}", [P, DM]) for n in range(NSTAGE)]
        wt = sb("wt", [P, NCV + CT, 2, KC, P], F32R)
        wot = sb("wot", [P, 2, CT, DM], F32R)
        wnext = sb("wnext", [P, 2, 2, DM], F32R)
        cvw = sb("cvw", [P, NCV, TAPS])
        cvb = sb("cvb", [P, NCV])
        dsk = sb("dsk", [P, CT])
        nw = sb("nw", [P, CT])
        ht = sb("ht", [P, 2, KC, BLK], F32R)
        acc = sb("acc", [P, TT, DM])
        xc = sb("xc", [P, NCV, BLK])
        z = sb("z", [P, CT, BLK])
        y = sb("y", [P, CT, BLK])
        gy = sb("gy", [P, 2, CT, BLK], F32R)
        adt = sb("adt", [P, TT, HG])
        segr = sb("segr", [P, TT * HG, L])
        decay = sb("decay", [P, TT, HG, L])
        cbm = sb("cbm", [P, TT, P])
        dtx = sb("dtx", [P, TT, GI])
        m = sb("m", [P, TT, HG, P])
        rv = sb("rv", [P, TT])
        r = sb("r", [P, TT])
        pick = sb("pick8", [P, 2, DM])

        bank = [ctx.enter_context(nc.psum_tensor(f"bank{n}", [P, 512], F32)) for n in range(8)]
        XT, SEG, CB, YB, OUT, SSQ, NEXT = (3, 4), (5, 7), 6, (6, 7), (2, 3, 4, 5), 6, (3, 4)

        s_stage = [sem(f"s2_stage{n}") for n in range(NSTAGE)]
        s_wps = sem("s2_wps")
        s_whi = sem("s2_whi")
        s_wlo = sem("s2_wlo")
        s_raw = [sem(f"s2_raw{u}") for u in range(2)]
        s_nps = sem("s2_nps")
        s_nhi = sem("s2_nhi")
        s_nlo = sem("s2_nlo")
        s_nst = sem("s2_nst")
        s_wt = [sem(f"s2_wt{n}") for n in range(NCV + CT)]
        s_wot = sem("s2_wot")
        s_cvp = sem("s2_conv_params")
        s_dnp = sem("s2_d_norm_params")
        s_ht = sem("s2_ht")
        s_accin = sem("s2_accin")
        s_accst = sem("s2_accst")
        s_proj = sem("s2_proj")
        s_tap = sem("s2_tap")
        s_cvstep = sem("s2_cvstep")
        s_conv = sem("s2_conv")
        s_silu = sem("s2_silu")
        s_z = sem("s2_z")
        s_adt = sem("s2_adt")
        s_segr = sem("s2_segr")
        s_seg = sem("s2_seg")
        s_exp = sem("s2_exp")
        s_xt = sem("s2_xt")
        s_dtx = sem("s2_dtx")
        s_cb = sem("s2_cb")
        s_cbm = sem("s2_cbm")
        s_m = sem("s2_m")
        s_yp = sem("s2_yp")
        s_y = sem("s2_y")
        s_u = sem("s2_u")
        s_uhi = sem("s2_uhi")
        s_ulo = sem("s2_ulo")
        s_sq = sem("s2_sq")
        s_sqsum = sem("s2_sqsum")
        s_ssq = sem("s2_ssq")
        s_rv = sem("s2_rv")
        s_r = sem("s2_r")
        s_out = sem("s2_out")
        s_acc = sem("s2_acc")
        s_pick = sem("s2_pick")
        s_w8 = sem("s2_w8")

        NCP, NDP = 6, 3
        NPJ = NCV + CT

        with nc.Block() as block:

            @block.sync
            def _(sp):
                w_in = a["L0_attn_in_proj_w"]
                w_out = a["L0_attn_out_proj_w"]
                cw = a["L0_attn_conv_weight"]
                cb = a["L0_attn_conv_bias"].rearrange("(c o) -> c o", o=1)
                d_v = a["L0_attn_D"].rearrange("(g c u) -> u g c", g=G, u=2)
                nw_v = a["L0_attn_norm_weight"].rearrange("(g c p) -> g p c", g=G, p=P)
                acc_v = sh.acc_d.rearrange("(j t p) d -> j p t d", t=TT, p=P)
                x_v = a["x"].rearrange("b i d -> (b i) d").rearrange("(j t p) d -> j p t d", t=TT, p=P)

                def load_h(j):
                    sp.dma_start(ht[:, :, :, :].rearrange("p a k n -> p (a k n)").bitcast(F32), sh.h_d[j]).then_inc(s_ht, 16)

                def load_conv_params(g):
                    for lo, n, c0 in ((0, 1, INNER + g * NS), (1, 1, INNER + GN + g * NS), (2, CT, g * GI)):
                        sp.dma_start(cvw[:, lo:lo + n, :], cw[ds(c0, n * P), :].rearrange("(c p) k -> p c k", p=P)).then_inc(s_cvp, 16)
                        sp.dma_start(cvb[:, lo:lo + n], cb[ds(c0, n * P), :].rearrange("(c p) o -> p (c o)", p=P)).then_inc(s_cvp, 16)

                def load_d_norm(g):
                    for u in range(2):
                        sp.dma_start(dsk[u * HP:(u + 1) * HP, :], d_v[u, ds(g, 1), :].to_broadcast([HP, CT])).then_inc(s_dnp, 16)
                    sp.dma_start(nw[:, :], nw_v[ds(g, 1)].rearrange("o p c -> p (o c)")).then_inc(s_dnp, 16)

                def rows_of(n, g):
                    if n >= NPJ:
                        return w_out[(n - NPJ) * P:(n - NPJ + 1) * P, ds(g * GI, GI)]
                    first = ([2 * INNER + g * NS, 2 * INNER + GN + g * NS] + [INNER + g * GI + c * P for c in range(CT)]
                             + [g * GI + c * P for c in range(CT)])
                    return w_in[ds(first[n], P), :]

                def next_chunks(j):
                    return 2 + j, (j % 2 if j < NBLK - KC else NPJ + j - (NBLK - KC))

                def load_raw(g, j):
                    for u, n in enumerate(next_chunks(j)):
                        sp.dma_start(stage[u][:, :], rows_of(n, g)).then_inc(s_raw[u], 16)

                def step(g, j, resid, last):
                    it = NBLK * g + j
                    over = last and j == NBLK - 1
                    nxt = g if last else g + 1
                    turn = j == NBLK - 1 and not last
                    sp.wait_ge(s_accst, 16 * it + 16)
                    load_raw(nxt, j)
                    if turn:
                        sp.wait_ge(s_nst, 32 * it + 32)
                    sp.dma_start(acc[:, :, :], resid[j]).then_inc(s_accin, 16)
                    if turn:
                        for n in range(NPJ - 1):
                            sp.wait_ge(s_proj, NPJ * it + n + 1)
                            sp.dma_start(wt[:, n, :, :, :].rearrange("p a k n -> p (a k n)").bitcast(F32),
                                         sh.wt_d[ds(g, 1), n].rearrange("o p n -> p (o n)")).then_inc(s_wt[n], 16)
                            if n == NCV:
                                sp.wait_ge(s_conv, NCV * (it + 1))
                                load_conv_params(nxt)
                    sp.wait_ge(s_nlo, 2 * it + 2)
                    for u, n in enumerate(next_chunks(j)):
                        sp.dma_start(sh.wt_d[ds(g, 1), n].rearrange("o p n -> p (o n)"),
                                     wnext[:, u, :, :].rearrange("p a n -> p (a n)").bitcast(F32)).then_inc(s_nst, 16)
                    sp.wait_ge(s_proj, NPJ * (it + 1))
                    if not over:
                        load_h((j + 1) % NBLK)
                    if turn:
                        n = NPJ - 1
                        sp.wait_ge(s_nst, 32 * it + 64)
                        sp.dma_start(wt[:, n, :, :, :].rearrange("p a k n -> p (a k n)").bitcast(F32),
                                     sh.wt_d[ds(g, 1), n].rearrange("o p n -> p (o n)")).then_inc(s_wt[n], 16)
                        sp.wait_ge(s_u, CT * (it + 1))
                        load_d_norm(nxt)
                        sp.wait_ge(s_out, TT * (it + 1))
                        for k in range(KC):
                            sp.dma_start(wot[:, :, :, k * P:(k + 1) * P].rearrange("p a c n -> p (a c) n").bitcast(F32),
                                         sh.wt_d[ds(g, 1), NPJ + k].rearrange("o p (a n) -> p (o a) n", n=P)).then_inc(s_wot, 16)
                    sp.wait_ge(s_acc, TT * it + 2 * TT)
                    sp.dma_start(acc_v[j], acc[:, :, :]).then_inc(s_accst, 16)

                sp.sem_inc(s_accst, 16)
                sp.sem_inc(s_nst, 32)
                for n in range(NPJ):
                    sp.sem_inc(s_wt[n], 16)
                sp.sem_inc(s_wot, 16 * KC)
                for n in range(NWC):
                    if n >= NSTAGE:
                        sp.wait_ge(s_wps, n - NSTAGE + 1)
                    sp.dma_start(stage[n % NSTAGE][:, :], rows_of(n, 0)).then_inc(s_stage[n % NSTAGE], 16)
                    if n == NSTAGE - 1:
                        load_h(0)
                        load_conv_params(0)
                        load_d_norm(0)
                sp.wait_ge(s_wps, NWC)
                for j in range(NBLK):
                    step(0, j, x_v, False)
                with sp.Fori(1, G - 1) as g:
                    for j in range(NBLK):
                        step(g, j, acc_v, False)
                for j in range(NBLK):
                    step(G - 1, j, acc_v, True)
                sp.wait_ge(s_accst, 16 * NIT + 16)
                sp.wait_ge(s_nst, 32 * NIT + 32)

            @block.gpsimd
            def _(pool):
                pool.sem_inc(s_segr, 1)
                pool.sem_inc(s_w8, 2)
                with pool.Fori(0, NIT) as it:
                    added = [0]

                    def add8(count=1):
                        for _ in range(count):
                            n = added[0]
                            added[0] += 1
                            pool.wait_ge(s_pick, CPI * OT * it + n + 1)
                            pool.wait_ge(s_w8, CPI * OT * it + n + 2)
                            pool.tensor_tensor(sh.w8[:, n % OT, :], sh.w8[:, n % OT, :], pick[:, n % 2, :], ALU.add).then_inc(s_w8, 1)

                    def low(c):
                        pool.wait_ge(s_uhi, CT * it + c + 1)
                        pool.tensor_tensor(gy[:, 1, c, :], z[:, c, :], gy[:, 0, c, :].bitcast(F32), ALU.subtract).then_inc(s_ulo, 1)

                    def sum_squares(c):
                        pool.wait_ge(s_sq, CT * it + c + 1)
                        if c > 1:
                            pool.wait_ge(s_sqsum, (CT - 1) * it + c - 1)
                        pool.tensor_tensor(y[:, 0, :], y[:, 0, :], y[:, c, :], ALU.add).then_inc(s_sqsum, 1)

                    pool.wait_ge(s_adt, 2 * it + 2)
                    pool.wait_ge(s_seg, SEGB * it + SEGB)
                    pool.tensor_tensor(segr[:, :, :], adt[:, :, :].rearrange("p t h -> p (t h)").unsqueeze(2).to_broadcast([P, TT * HG, L]),
                                       sh.mask_le[:, :].unsqueeze(1).to_broadcast([P, TT * HG, L]), ALU.mult).then_inc(s_segr, 1)
                    add8(9)
                    low(0)
                    low(1)
                    add8(2)
                    sum_squares(1)
                    low(2)
                    sum_squares(2)
                    low(3)
                    sum_squares(3)
                    add8(3)
                    pool.wait_ge(s_rv, it + 2)
                    pool.tensor_tensor(r[:, :], rv[:, :], sh.neg_half[:, 0:TT], ALU.pow).then_inc(s_r, 1)
                    add8(CPI * OT - added[0])

            @block.tensor
            def _(pe):
                pe.sem_inc(s_seg, SEGB)
                for n in range(NWC):
                    slot = n % NSTAGE
                    pe.wait_ge(s_stage[slot], 16 * (n // NSTAGE + 1))
                    if n >= 3:
                        pe.wait_ge(s_wlo, n - 2)
                    for k in range(KC):
                        ins = pe.transpose(bank[n % 3][:, k * P:(k + 1) * P], stage[slot][:, k * P:(k + 1) * P], sh.ident[:, :])
                    ins.then_inc(s_wps, 1)
                pe.wait_ge(s_wlo, NWC)
                with pe.Fori(0, G) as g:
                    with pe.Fori(0, NBLK) as j:
                        it = NBLK * g + j

                        def project(n):
                            pe.wait_ge(s_wt[n], 16 * g + 16)
                            pb = bank[PROJ_BANK[n]]
                            for q, (l, rr) in enumerate(PASSES):
                                for k in range(KC):
                                    ins = pe.matmul(pb[:, :], wt[:, n, l, k, :], ht[:, rr, k, :],
                                                    start=(q == 0 and k == 0), stop=(q == 2 and k == KC - 1))
                            ins.then_inc(s_proj, 1)

                        def turn_x(t):
                            for c in range(CT):
                                ins = pe.transpose(bank[XT[t % 2]][:, c * P:(c + 1) * P], xc[:, 2 + c, t * P:(t + 1) * P], sh.ident[:, :])
                            ins.then_inc(s_xt, 1)

                        def scan(c):
                            for u in range(2):
                                for t in range(TT):
                                    if c == 0 and u == 0:
                                        pe.wait_ge(s_m, TT * it + t + 1)
                                    h = 2 * c + u
                                    ins = pe.matmul(bank[YB[c % 2]][u * HP:(u + 1) * HP, t * P:(t + 1) * P], dtx[:, t, h * HP:(h + 1) * HP],
                                                    m[:, t, h, :], start=True, stop=True)
                            ins.then_inc(s_yp, 1)

                        pe.wait_ge(s_ht, 16 * it + 16)
                        for n in range(NCV):
                            if n == 0:
                                pe.wait_ge(s_z, CT * it + CT)
                            elif n == 2:
                                pe.wait_ge(s_acc, TT * it + 1)
                            elif n >= 3:
                                pe.wait_ge(s_conv, NCV * it + n - 2)
                            project(n)
                        pe.wait_ge(s_segr, it + 2)
                        pe.wait_ge(s_acc, TT * it + TT)
                        pe.wait_ge(s_y, CT * it + CT)
                        for q in range(SEGB):
                            pe.matmul(bank[SEG[q]][:, :], sh.mask_gt[:, :],
                                      segr[:, q * 2 * HG:(q + 1) * 2 * HG, :].rearrange("p h l -> p (h l)"),
                                      start=True, stop=True).then_inc(s_seg, 1)
                        pe.wait_ge(s_conv, NCV * it + 4)
                        project(NCV)
                        pe.wait_ge(s_silu, NCV * it + NCV)
                        turn_x(0)
                        turn_x(1)
                        pe.wait_ge(s_rv, it + 1)
                        for t in range(TT):
                            ins = pe.matmul(bank[CB][:, t * P:(t + 1) * P], xc[:, 0, t * P:(t + 1) * P], xc[:, 1, t * P:(t + 1) * P],
                                            start=True, stop=True)
                        ins.then_inc(s_cb, 1)
                        for t in range(2, TT):
                            pe.wait_ge(s_dtx, TT * it + t - 1)
                            turn_x(t)
                        for c in (1, 2):
                            pe.wait_ge(s_conv, NCV * it + 4 + c)
                            project(NCV + c)
                        for u in range(2):
                            pe.wait_ge(s_raw[u], 16 * it + 16)
                            pe.wait_ge(s_dtx, TT * it + 3 + u)
                            for k in range(KC):
                                ins = pe.transpose(bank[NEXT[u]][:, k * P:(k + 1) * P], stage[u][:, k * P:(k + 1) * P], sh.ident[:, :])
                            ins.then_inc(s_nps, 1)
                        pe.wait_ge(s_cbm, it + 1)
                        scan(0)
                        pe.wait_ge(s_exp, SEGB * it + SEGB)
                        scan(1)
                        pe.wait_ge(s_z, CT * it + CT + 1)
                        project(NCV + 3)
                        for c in (2, 3):
                            pe.wait_ge(s_y, CT * it + CT + c - 1)
                            scan(c)
                        pe.wait_ge(s_z, CT * it + CT + 3)
                        pe.wait_ge(s_nlo, 2 * it + 2)
                        pe.wait_ge(s_wot, 16 * KC * g + 16 * KC)
                        for c in range(CT):
                            if c == CT - 1:
                                pe.wait_ge(s_y, CT * it + CT + 3)
                                pe.wait_ge(s_sqsum, (CT - 1) * (it + 1))
                                for t in range(TT):
                                    ins = pe.matmul(bank[SSQ][:, t * P:(t + 1) * P], y[:, 0, t * P:(t + 1) * P], sh.ones[:, :],
                                                    start=True, stop=True)
                                ins.then_inc(s_ssq, 1)
                            pe.wait_ge(s_ulo, CT * it + c + 1)
                            for t in range(TT):
                                for q, (l, rr) in enumerate(PASSES):
                                    ins = pe.matmul(bank[OUT[t]][:, :], gy[:, l, c, t * P:(t + 1) * P], wot[:, rr, c, :],
                                                    start=(c == 0 and q == 0), stop=(c == CT - 1 and q == 2))
                                if c == CT - 1:
                                    ins.then_inc(s_out, 1)

            @block.scalar
            def _(act):
                act.sem_inc(s_z, CT)
                for n in range(NWC):
                    act.wait_ge(s_wps, n + 1)
                    if n < NPJ:
                        act.activation(wt[:, n, 0, :, :].rearrange("p k c -> p (k c)"), bank[n % 3][:, :], ACT.Copy).then_inc(s_whi, 1)
                    else:
                        k = n - NPJ
                        act.activation(wot[:, 0, :, k * P:(k + 1) * P], bank[n % 3][:, :].rearrange("p (c d) -> p c d", c=CT),
                                       ACT.Copy).then_inc(s_whi, 1)
                with act.Fori(0, G) as g:
                    with act.Fori(0, NBLK) as j:
                        it = NBLK * g + j

                        def silu(n):
                            act.wait_ge(s_conv, NCV * it + n + 1)
                            act.activation(xc[:, n, :], xc[:, n, :], ACT.Silu).then_inc(s_silu, 1)

                        def gate(c):
                            act.wait_ge(s_proj, NPJ * it + NCV + c + 1)
                            act.activation(z[:, c, :], bank[PROJ_BANK[NCV + c]][:, :], ACT.Silu).then_inc(s_z, 1)

                        def high(c):
                            act.wait_ge(s_u, CT * it + c + 1)
                            act.activation(gy[:, 0, c, :], z[:, c, :], ACT.Copy).then_inc(s_uhi, 1)
                            act.activation(y[:, c, :], y[:, c, :], ACT.Square).then_inc(s_sq, 1)

                        for n in range(NCV):
                            act.wait_ge(s_proj, NPJ * it + n + 1)
                            if n == 0:
                                act.wait_ge(s_cvp, 16 * NCP * g + 16 * NCP)
                            act.activation(xc[:, n, :], bank[PROJ_BANK[n]][:, :], ACT.Identity, bias=cvb[:, n:n + 1],
                                           scale=cvw[:, n, TAPS - 1:TAPS]).then_inc(s_tap, 1)
                            if n:
                                silu(n - 1)
                        silu(NCV - 1)
                        gate(0)
                        for q in range(SEGB):
                            act.wait_ge(s_seg, SEGB * it + SEGB + q + 1)
                            act.activation(decay[:, 2 * q:2 * q + 2, :, :].rearrange("p t h l -> p (t h l)"),
                                           bank[SEG[q]][:, :], ACT.Exp).then_inc(s_exp, 1)
                        gate(1)
                        gate(2)
                        for u in range(2):
                            act.wait_ge(s_nps, 2 * it + u + 1)
                            act.wait_ge(s_nst, 32 * it + 32)
                            act.activation(wnext[:, u, 0, :], bank[NEXT[u]][:, :], ACT.Copy).then_inc(s_nhi, 1)
                        high(0)
                        high(1)
                        gate(3)
                        high(2)
                        high(3)

            @block.vector
            def _(dve):
                dve.sem_inc(s_y, CT)
                dve.sem_inc(s_acc, TT)
                dve.sem_inc(s_rv, 1)
                for n in range(NWC):
                    dve.wait_ge(s_whi, n + 1)
                    if n < NPJ:
                        dve.tensor_tensor(wt[:, n, 1, :, :].rearrange("p k c -> p (k c)"), bank[n % 3][:, :],
                                          wt[:, n, 0, :, :].rearrange("p k c -> p (k c)").bitcast(F32), ALU.subtract).then_inc(s_wlo, 1)
                    else:
                        k = n - NPJ
                        dve.tensor_tensor(wot[:, 1, :, k * P:(k + 1) * P], bank[n % 3][:, :].rearrange("p (c d) -> p c d", c=CT),
                                          wot[:, 0, :, k * P:(k + 1) * P].bitcast(F32), ALU.subtract).then_inc(s_wlo, 1)
                with dve.Fori(0, G) as g:
                    with dve.Fori(0, NBLK) as j:
                        it = NBLK * g + j
                        picked = [0]

                        def pick8(count=1):
                            for _ in range(count):
                                n = picked[0]
                                picked[0] += 1
                                dve.wait_ge(s_w8, CPI * OT * it + n + 1)
                                dve.tensor_scalar(pick[:, n % 2, :], sh.code8[:, n % OT, :], sh.code_no[:, ds(CPI * it + n // OT, 1)],
                                                  sh.lut8[:, n % OT, ds(CPI * it + n // OT, 1)], ALU.is_equal, ALU.mult).then_inc(s_pick, 1)

                        dve.wait_ge(s_segr, it + 1)
                        dve.tensor_tensor(adt[:, :, :], sh.dt[:, ds(TT * j, TT), ds(HG * g, HG)],
                                          sh.neg_a[:, ds(HG * g, HG)].unsqueeze(1).to_broadcast([P, TT, HG]), ALU.mult).then_inc(s_adt, 1)
                        dve.wait_ge(s_adt, 2 * it + 1)
                        dve.tensor_scalar(adt[:, :, :], adt[:, :, :], DECAY_FLOOR, None, ALU.max).then_inc(s_adt, 1)
                        pick8(2)
                        for n in range(NCV):
                            dve.wait_ge(s_tap, NCV * it + n + 1)
                            for k in range(1, TAPS):
                                src = bank[PROJ_BANK[n]][:, :].rearrange("p (b l) -> p b l", l=L)[:, :, 0:L - k]
                                dst = xc[:, n, :].rearrange("p (b l) -> p b l", l=L)[:, :, k:L]
                                ins = dve.scalar_tensor_tensor(dst, src, cvw[:, n, TAPS - 1 - k:TAPS - k], dst, ALU.mult, ALU.add)
                                if k < TAPS - 1:
                                    ins.then_inc(s_cvstep, 1)
                                    dve.wait_ge(s_cvstep, (TAPS - 2) * (NCV * it + n) + k)
                            ins.then_inc(s_conv, 1)
                            pick8()
                        pick8()
                        for t in range(TT):
                            dve.wait_ge(s_xt, TT * it + t + 1)
                            dve.tensor_tensor(dtx[:, t, :].rearrange("p (h c) -> p h c", h=HG),
                                              bank[XT[t % 2]][:, :].rearrange("p (h c) -> p h c", h=HG),
                                              sh.dt[:, ds(TT * j + t, 1), ds(HG * g, HG)].rearrange("p o h -> p (o h)").unsqueeze(2).to_broadcast([P, HG, HP]),
                                              ALU.mult).then_inc(s_dtx, 1)
                        dve.wait_ge(s_cb, it + 1)
                        dve.tensor_tensor(cbm[:, :, :], bank[CB][:, :].rearrange("p (t n) -> p t n", t=TT),
                                          sh.mask_cb[:, :].unsqueeze(1).to_broadcast([P, TT, P]), ALU.mult).then_inc(s_cbm, 1)
                        dve.wait_ge(s_cbm, it + 1)
                        for t in range(TT):
                            dve.wait_ge(s_exp, SEGB * it + t // 2 + 1)
                            dve.tensor_tensor(m[:, t, :, :].rearrange("p h (c l) -> p h c l", l=L),
                                              cbm[:, t, :].rearrange("p (c l) -> p c l", l=L).unsqueeze(1).to_broadcast([P, HG, BT, L]),
                                              decay[:, t, :, :].unsqueeze(2).to_broadcast([P, HG, BT, L]), ALU.mult).then_inc(s_m, 1)
                        for u in range(2):
                            dve.wait_ge(s_nhi, 2 * it + u + 1)
                            dve.tensor_tensor(wnext[:, u, 1, :], bank[NEXT[u]][:, :], wnext[:, u, 0, :].bitcast(F32),
                                              ALU.subtract).then_inc(s_nlo, 1)
                        for c in range(CT):
                            dve.wait_ge(s_yp, CT * it + c + 1)
                            if c == 0:
                                dve.wait_ge(s_dnp, 16 * NDP * g + 16 * NDP)
                            dve.scalar_tensor_tensor(y[:, c, :], xc[:, 2 + c, :], dsk[:, c:c + 1], bank[YB[c % 2]][:, :],
                                                     ALU.mult, ALU.add).then_inc(s_y, 1)
                            dve.wait_ge(s_z, CT * it + CT + c + 1)
                            dve.wait_ge(s_y, CT * it + CT + c + 1)
                            dve.scalar_tensor_tensor(z[:, c, :], z[:, c, :], nw[:, c:c + 1], y[:, c, :], ALU.mult, ALU.mult).then_inc(s_u, 1)
                            if c == 1:
                                pick8(2)
                        pick8(CPI * OT - picked[0])
                        dve.wait_ge(s_ssq, it + 1)
                        dve.tensor_scalar(rv[:, :], bank[SSQ][:, :].rearrange("p (t n) -> p t n", t=TT)[:, :, 0], 1.0 / GI, EPS,
                                          ALU.mult, ALU.add).then_inc(s_rv, 1)
                        dve.wait_ge(s_r, it + 1)
                        dve.wait_ge(s_accin, 16 * it + 16)
                        for t in range(TT):
                            dve.wait_ge(s_out, TT * it + t + 1)
                            dve.scalar_tensor_tensor(acc[:, t, :], bank[OUT[t]][:, :], r[:, t:t + 1], acc[:, t, :],
                                                     ALU.mult, ALU.add).then_inc(s_acc, 1)


def stage3(nc, a, sh, out):
    with ExitStack() as ctx:
        def sb(name, shape, dt=F32):
            return ctx.enter_context(nc.sbuf_tensor(name, shape, dt))

        def sem(name):
            return ctx.enter_context(nc.semaphore(name))

        w4 = sb("w4_nat", [P, OT, DM])
        wq = sb("wq", [P, 2, 2, KC, DM], F32R)
        cbn = sb("cbn", [P, CG, KW])
        cbd = sb("cbd", [P, KW, P])
        gmask = sb("gmask", [P, P])
        cbs = sb("cbs", [P, 2, KW, P], F32R)
        ctxp = sb("ctxp", [P, TOK // P])
        bias = sb("bias", [P, DM])
        x2 = sb("x2", [P, TT, DM])
        x2s = sb("x2s", [P, 2, TT, DM + 2 * PADW], F32R)
        xb = sb("x2b", [P, TT, DM])
        x3 = sb("x3", [P, TT, DM])
        sq = sb("sq", [P, DM])
        ssq = sb("ssq", [P, TT])
        hot = sb("hot", [P, TT])
        cold = sb("cold", [P, TT])
        x3t = sb("x3t", [P, 2, TT, KC, P], F32R)
        res = sb("res", [P, TT, DM])

        p_cv = [ctx.enter_context(nc.psum_tensor(f"p_cv{u}", [P, 512], F32)) for u in range(2)]
        p_tr = [ctx.enter_context(nc.psum_tensor(f"p_tr{u}", [P, 512], F32)) for u in range(2)]
        p_y = [[ctx.enter_context(nc.psum_tensor(f"p_y{u}{q}", [P, 512], F32)) for q in range(2)] for u in range(2)]

        s_w = sem("s3_w")
        s_zero = sem("s3_zero")
        s_cbn = sem("s3_cbn")
        s_cbd = sem("s3_cbd")
        s_cbhi = sem("s3_cbhi")
        s_cblo = sem("s3_cblo")
        s_wps = sem("s3_wps")
        s_whi = sem("s3_whi")
        s_wlo = sem("s3_wlo")
        s_x2 = sem("s3_x2")
        s_x2hi = sem("s3_x2hi")
        s_x2lo = sem("s3_x2lo")
        s_xb = sem("s3_xb")
        s_cv = sem("s3_cv")
        s_x3 = sem("s3_x3")
        s_sq = sem("s3_sq")
        s_hot = sem("s3_hot")
        s_tr = sem("s3_tr")
        s_x3hi = sem("s3_x3hi")
        s_x3lo = sem("s3_x3lo")
        s_y = sem("s3_y")
        s_half = sem("s3_half")
        s_fin = sem("s3_fin")
        s_out = sem("s3_out")

        with nc.Block() as block:
            x2_v = sh.acc_d.rearrange("(j t p) d -> j p t d", t=TT, p=P)
            out_v = out.rearrange("b i d -> (b i) d").rearrange("(j t p) d -> j p t d", t=TT, p=P)

            @block.sync
            def _(sp):
                sp.sem_inc(s_out, 16)
                sp.dma_start(w4[:, :, :].rearrange("p t i -> p (t i)"), sh.w4_d).then_inc(s_w, 16)
                sp.dma_start(ctxp[:, :], sh.ctxb_d.rearrange("(t c) o -> (c o) t", c=BT)).then_inc(s_w, 16)
                sp.dma_start(bias[:, :], a["L0_ffn_bias"].partition_broadcast(P)).then_inc(s_w, 16)

                def load(j):
                    sp.dma_start(x2[:, :, :], x2_v[ds(j, 1)].rearrange("o p t d -> p (o t) d")).then_inc(s_x2, 16)

                def store(j):
                    sp.wait_ge(s_fin, TT * (j + 1) + 2)
                    sp.dma_start(out_v[ds(j, 1)].rearrange("o p t d -> p (o t) d"), res[:, :, :]).then_inc(s_out, 16)

                load(0)
                w_v = a["L0_cond2_weight"].rearrange("(q o) i k -> q i o k", o=CG)
                for c in range(BT):
                    for q in range(L // CG):
                        lo = c * L + q * CG
                        sp.dma_start(cbn[lo:lo + CG, :, :], w_v[q]).then_inc(s_cbn, 16)
                with sp.Fori(0, NBLK - 1) as j:
                    sp.wait_ge(s_xb, TT * (j + 1))
                    load(j + 1)
                    store(j)
                store(NBLK - 1)
                sp.wait_ge(s_out, 16 * NBLK + 16)

            @block.gpsimd
            def _(pool):
                pool.memset(gmask[:, :], 1.0).then_inc(s_zero, 1)
                v = gmask[:, :].rearrange("p (q o) -> p q o", o=CG)
                for n, (base, step, cm) in enumerate(((0, -CG, 1), (CG - 1, CG, -1))):
                    pool.wait_ge(s_zero, n + 1)
                    pool.affine_select(out=v, in_=v, compare_op=ALU.is_ge, fill=0.0, base=base,
                                       pattern=[[step, P // CG], [0, CG]], channel_multiplier=cm).then_inc(s_zero, 1)
                pool.memset(x2s[:, :, :, 0:PADW].bitcast(F32), 0.0).then_inc(s_zero, 1)
                pool.memset(x2s[:, :, :, PADW + DM:].bitcast(F32), 0.0).then_inc(s_zero, 1)
                pool.wait_ge(s_w, 48)
                with pool.Fori(0, NBLK) as j:
                    for t in range(TT):
                        pool.wait_ge(s_x2hi, TT * j + t + 1)
                        pool.tensor_tensor(x2s[:, 1, t, PADW:PADW + DM], x2[:, t, :], x2s[:, 0, t, PADW:PADW + DM].bitcast(F32),
                                           ALU.subtract).then_inc(s_x2lo, 1)
                    for t in range(TT):
                        pool.wait_ge(s_fin, TT * j + 2)
                        pool.tensor_tensor(xb[:, t, :], x2[:, t, :], bias[:, :], ALU.add).then_inc(s_xb, 1)

            @block.tensor
            def _(pe):
                pe.sem_inc(s_cv, TT)
                pe.wait_ge(s_w, 48)
                n = 0
                for q, w in ((0, w4), (1, sh.w8)):
                    for k in range(KC):
                        if n >= 2:
                            pe.wait_ge(s_wlo, n - 1)
                        for t in range(OT):
                            ins = pe.transpose(p_tr[n % 2][:, t * P:(t + 1) * P], w[:, t, k * P:(k + 1) * P], sh.ident[:, :])
                        ins.then_inc(s_wps, 1)
                        n += 1
                pe.wait_ge(s_wlo, n)
                pe.wait_ge(s_cblo, 1)
                pe.wait_ge(s_zero, 5)
                with pe.Fori(0, NBLK) as j:
                    def conv(t):
                        pe.wait_ge(s_x2lo, TT * j + t + 1)
                        pe.wait_ge(s_x3, TT * j + t + 1)
                        for n, (l, rr) in enumerate(PASSES):
                            for k in range(KW):
                                ins = pe.matmul(p_cv[t % 2][:, :], cbs[:, l, k, :], x2s[:, rr, t, k:k + DM],
                                                start=(n == 0 and k == 0), stop=(n == 2 and k == KW - 1))
                        ins.then_inc(s_cv, 1)

                    def turn(t):
                        pe.wait_ge(s_x3, TT * j + t + 3)
                        pe.wait_ge(s_x3lo, TT * j + t + 1)
                        for k in range(KC):
                            ins = pe.transpose(p_tr[t % 2][:, k * P:(k + 1) * P], x3[:, t, k * P:(k + 1) * P], sh.ident[:, :])
                        ins.then_inc(s_tr, 1)

                    def ffn(t):
                        pe.wait_ge(s_x3lo, TT * j + t + 3)
                        pe.wait_ge(s_fin, TT * j + t + 1)
                        for q in range(2):
                            for n, (l, rr) in enumerate(PASSES):
                                for k in range(KC):
                                    ins = pe.matmul(p_y[t % 2][q][:, :], x3t[:, l, t, k, :], wq[:, q, rr, k, :],
                                                    start=(n == 0 and k == 0), stop=(n == 2 and k == KC - 1))
                        ins.then_inc(s_y, 1)

                    conv(0)
                    conv(1)
                    turn(0)
                    conv(2)
                    turn(1)
                    ffn(0)
                    conv(3)
                    turn(2)
                    ffn(1)
                    turn(3)
                    ffn(2)
                    ffn(3)

            @block.scalar
            def _(act):
                act.sem_inc(s_x3, 2)
                for n in range(2 * KC):
                    act.wait_ge(s_wps, n + 1)
                    act.activation(wq[:, n // KC, 0, n % KC, :], p_tr[n % 2][:, :], ACT.Copy).then_inc(s_whi, 1)
                act.wait_ge(s_cbd, 1)
                act.activation(cbs[:, 0, :, :], cbd[:, :, :], ACT.Copy).then_inc(s_cbhi, 1)
                with act.Fori(0, NBLK) as j:
                    act.wait_ge(s_x2, 16 * j + 16)
                    for t in range(TT):
                        act.wait_ge(s_cv, TT * j + t + 1)
                        act.activation(x2s[:, 0, t, PADW:PADW + DM], x2[:, t, :], ACT.Copy).then_inc(s_x2hi, 1)

                    def evac(t):
                        act.wait_ge(s_cv, TT * j + TT + t + 1)
                        act.activation(x3[:, t, :], p_cv[t % 2][:, :], ACT.Identity, bias=ctxp[:, ds(TT * j + t, 1)]).then_inc(s_x3, 1)
                        act.wait_ge(s_x3, TT * j + t + 3)
                        act.activation(sq[:, :], x3[:, t, :], ACT.Square, accum_out=ssq[:, t:t + 1]).then_inc(s_sq, 1)

                    def high(t):
                        act.wait_ge(s_tr, TT * j + t + 1)
                        act.activation(x3t[:, 0, t, :, :].rearrange("p k n -> p (k n)"), p_tr[t % 2][:, :], ACT.Copy).then_inc(s_x3hi, 1)

                    evac(0)
                    evac(1)
                    high(0)
                    evac(2)
                    high(1)
                    evac(3)
                    high(2)
                    high(3)

            @block.vector
            def _(dve):
                dve.sem_inc(s_x3lo, 2)
                dve.wait_ge(s_cbn, 16 * BT * (L // CG))
                dve.wait_ge(s_zero, 3)
                q = P // CG
                dve.tensor_tensor(cbd[:, :, :].rearrange("p k (q o) -> p k q o", o=CG),
                                  cbn[:, :, :].rearrange("p o k -> p k o").unsqueeze(2).to_broadcast([P, KW, q, CG]),
                                  gmask[:, :].rearrange("p (q o) -> p q o", o=CG).unsqueeze(1).to_broadcast([P, KW, q, CG]),
                                  ALU.mult).then_inc(s_cbd, 1)
                dve.sem_inc(s_fin, 2)
                for n in range(2 * KC):
                    dve.wait_ge(s_whi, n + 1)
                    dve.tensor_tensor(wq[:, n // KC, 1, n % KC, :], p_tr[n % 2][:, :], wq[:, n // KC, 0, n % KC, :].bitcast(F32),
                                      ALU.subtract).then_inc(s_wlo, 1)
                dve.wait_ge(s_cbhi, 1)
                dve.tensor_tensor(cbs[:, 1, :, :], cbd[:, :, :], cbs[:, 0, :, :].bitcast(F32), ALU.subtract).then_inc(s_cblo, 1)
                with dve.Fori(0, NBLK) as j:
                    def low(t):
                        dve.wait_ge(s_x3hi, TT * j + t + 1)
                        dve.tensor_tensor(x3t[:, 1, t, :, :].rearrange("p k n -> p (k n)"), p_tr[t % 2][:, :],
                                          x3t[:, 0, t, :, :].rearrange("p k n -> p (k n)").bitcast(F32), ALU.subtract).then_inc(s_x3lo, 1)

                    def choose(t):
                        dve.wait_ge(s_sq, TT * j + t + 1)
                        dve.tensor_scalar(hot[:, t:t + 1], ssq[:, t:t + 1], MASK_T2, None, ALU.is_gt).then_inc(s_hot, 1)
                        dve.tensor_scalar(cold[:, t:t + 1], ssq[:, t:t + 1], MASK_T2, None, ALU.is_le).then_inc(s_hot, 1)

                    def finish(t):
                        dve.wait_ge(s_y, TT * j + t + 1)
                        dve.wait_ge(s_xb, TT * j + t + 1)
                        dve.wait_ge(s_hot, 2 * (TT * j + t + 1))
                        if t == 0:
                            dve.wait_ge(s_out, 16 * j + 16)
                        dve.scalar_tensor_tensor(res[:, t, :], p_y[t % 2][1][:, :], hot[:, t:t + 1], xb[:, t, :],
                                                 ALU.mult, ALU.add).then_inc(s_half, 1)
                        dve.wait_ge(s_half, TT * j + t + 1)
                        dve.scalar_tensor_tensor(res[:, t, :], p_y[t % 2][0][:, :], cold[:, t:t + 1], res[:, t, :],
                                                 ALU.mult, ALU.add).then_inc(s_fin, 1)

                    choose(0)
                    choose(1)
                    low(0)
                    choose(2)
                    low(1)
                    choose(3)
                    low(2)
                    finish(0)
                    low(3)
                    finish(1)
                    finish(2)
                    finish(3)


def build(nc, a, out):
    sh = Shared()
    with ExitStack() as ctx:
        def sb(name, shape, dt=F32):
            return ctx.enter_context(nc.sbuf_tensor(name, shape, dt))

        ctx.enter_context(nc.allow_non_contiguous_dma(reason="parameters laid out by channel, a few KB"))
        sh.ident = sb("ident", [P, P])
        sh.mask_cb = sb("mask_cb", [P, P])
        sh.mask_gt = sb("mask_gt", [P, P])
        sh.mask_le = sb("mask_le", [P, L])
        sh.neg_half = sb("neg_half", [P, TT])
        sh.ones = sb("ones", [P, P])
        sh.code_no = sb("code_no", [P, NCODE])
        sh.dt = sb("dt_all", [P, TOK // P, H])
        sh.neg_a = sb("neg_a", [P, H])
        sh.code8 = sb("code8", [P, OT, DM], BF16)
        sh.lut8 = sb("lut8", [P, OT, NCODE])
        sh.w8 = sb("w8", [P, OT, DM])
        sh.h_d = nc.dram_tensor("h_d", (NBLK, P, 2 * KC * BLK), F32).ap()
        sh.acc_d = nc.dram_tensor("acc_d", (TOK, DM), F32).ap()
        sh.agg_d = nc.dram_tensor("agg_d", (NB, L, L), F32).ap()
        sh.aggb_d = nc.dram_tensor("aggb_d", (NB, L), F32).ap()
        sh.ctxb_d = nc.dram_tensor("ctxb_d", (NB, L), F32).ap()
        sh.wt_d = nc.dram_tensor("wt_d", (G, NWC, P, 2 * KC * P), F32).ap()
        sh.w4_d = nc.dram_tensor("w4_d", (P, OT * DM), F32).ap()
        stage1(nc, a, sh)
        stage2(nc, a, sh)
        stage3(nc, a, sh, out)


_INS = ["x", "cond_128", "fside_S_0", "L0_cond_W0", "L0_cond_b0", "L0_cond_W1", "L0_cond_b1", "L0_cond_W2", "L0_cond_b2",
        "L0_cond_weight", "L0_cond_bias_k", "L0_attn_in_proj_w", "L0_attn_conv_weight", "L0_attn_conv_bias",
        "L0_attn_dt_bias", "L0_attn_A_log", "L0_attn_D", "L0_attn_norm_weight", "L0_attn_out_proj_w",
        "L0_cond2_weight", "L0_cond2_c_weight", "L0_ffn_qweight", "L0_ffn_lut4", "L0_ffn_lut8", "L0_ffn_bias"]


def kernel(**inputs):
    import numpy as np
    import concourse.bacc as bacc
    from concourse.bass_utils import run_bass_kernel_spmd

    nc = bacc.Bacc("TRN2", target_bir_lowering=False, num_devices=1)
    arrays, aps = {}, {}
    for name in _INS:
        v = np.ascontiguousarray(inputs[name])
        arrays[f"in_{name}"] = v
        aps[name] = nc.dram_tensor(f"in_{name}", v.shape, mybir.dt.from_np(v.dtype), kind="ExternalInput").ap()
    out = nc.dram_tensor("out_0", (NB, L, DM), F32, kind="ExternalOutput").ap()
    build(nc, aps, out)
    got = run_bass_kernel_spmd(nc, [arrays], core_ids=[0])
    return got.results[0]["out_0"]
```

```python
from contextlib import ExitStack

import concourse.bass as bass
from concourse import mybir

F32 = mybir.dt.float32
F32R = mybir.dt.float32r
BF16 = mybir.dt.bfloat16
I32 = mybir.dt.int32
ALU = mybir.AluOpType
ACT = mybir.ActivationFunctionType
AX = mybir.AxisListType
ds = bass.ds

P = 128
NB, L, DM = 128, 32, 512
TOK = NB * L
BLK = 512
NBLK = TOK // BLK
TT = BLK // P
BT = P // L
KC = DM // P
H, HP, NS, G = 64, 64, 128, 8
INNER = H * HP
GN = G * NS
CONV = INNER + 2 * GN
HG = H // G
GI = INNER // G
CT = GI // P
TAPS = 4
EPS = 1e-5
NEXP = 8
NCODE = 256
OT = DM // P
NIT = G * NBLK
CPI = NCODE // NIT
KW = 9
R = 4
NQ = (KW - 1 + R - 1) // R + 1
XW = DM + R * (NQ - 1)
CG = 8
NSQ = P
NCBQ = KW * R
MASK_T2 = 64.0 * 64.0 * (1.0 + 2.0 ** -23)
DECAY_FLOOR = -200.0
LOGA_CAP = 85.0

PASSES = ((0, 0), (0, 1), (1, 0))
NCV = 2 + CT
NWC = NCV + CT + KC
C4 = 16 // NBLK
NPK4 = 8
SEGB = TT * HG * L // 512
NSTAGE = 4
PREP = 8
PROJ_BANK = (0, 1, 2, 0, 1, 2, 0, 1, 2, 0)


class Shared:
    pass


def stage1(nc, a, sh):
    with ExitStack() as ctx:
        def sb(name, shape, dt=F32):
            return ctx.enter_context(nc.sbuf_tensor(name, shape, dt))

        def sem(name):
            return ctx.enter_context(nc.semaphore(name))

        cond = sb("cond", [NB, 128])
        cond_t = sb("cond_t", [128, NB])
        cw = sb("cw", [L, 128])
        cw_t = sb("cw_t", [128, L])
        w0 = sb("w0", [128, 128])
        w1 = sb("w1", [128, 128])
        b0 = sb("b0", [128, 1])
        b1 = sb("b1", [128, 1])
        w2 = sb("w2", [128, NEXP])
        b2 = sb("b2", [NB, NEXP])
        experts = sb("experts", [NEXP, L * L])
        bias_k = sb("bias_k", [NEXP, L])
        side = sb("side", [NB, L])
        h1 = sb("h1", [128, NB])
        h2 = sb("h2", [128, NB])
        logit = sb("logit", [NB, NEXP])
        nmax = sb("nmax", [NB, 1])
        esum = sb("esum", [NB, 1])
        erec = sb("erec", [NB, 1])
        att = sb("att", [NB, NEXP])
        att_t = sb("att_t", [NEXP, NB])
        agg = sb("agg", [NB, L, L])
        aggb = sb("aggb", [NB, 2, L], F32R)
        ctxb = sb("ctxb", [NB, L])
        mix = sb("mix", [P, NBLK * TT, P])
        aggb_row = sb("aggb_row", [2, TOK], F32R)
        ones_row = sb("ones_row", [2, P], F32R)
        wdt = sb("wdt", [H, DM])
        wdt_t = sb("wdt_t", [P, 2, KC, H], F32R)
        dtb = sb("dtb", [H, 1])
        dt_t = sb("dt_t", [H, TOK])
        sp_e = sb("sp_e", [H, BLK])
        alog = sb("alog", [P, H])
        xb = [sb(f"xb{u}", [P, TT, DM]) for u in range(2)]
        ht = [sb(f"ht_out{u}", [P, 2, KC, BLK], F32R) for u in range(2)]
        qw = sb("qw", [P, OT, 8, 16], I32)
        bits = sb("bits", [P, OT * 4 * 16, 32], I32)
        code = sb("code", [P, OT, DM])
        code4 = sb("code4", [P, OT, DM])
        lut4 = sb("lut4", [P, OT, 16])
        pick = bits[:, 0:NPK4 * DM // 32, :].bitcast(F32).rearrange("p (n k) s -> p n (k s)", n=NPK4)
        w4 = sb("w4", [P, OT, DM])

        p_mlp = ctx.enter_context(nc.psum_tensor("p_mlp", [P, 512], F32))
        p_agg = [ctx.enter_context(nc.psum_tensor(f"p_agg{u}", [P, 512], F32)) for u in range(2)]
        p_wdt = ctx.enter_context(nc.psum_tensor("p_wdt", [P, 512], F32))
        p_h = [ctx.enter_context(nc.psum_tensor(f"p_h{u}", [P, 512], F32)) for u in range(2)] + p_agg
        p_dt = [ctx.enter_context(nc.psum_tensor(f"p_dt{u}", [P, 512], F32)) for u in range(2)]

        s_ld = sem("s1_loaded")
        s_q = sem("s1_q_loaded")
        s_const = sem("s1_const")
        s_pe = sem("s1_pe")
        s_act = sem("s1_act")
        s_dve = sem("s1_dve")
        s_rt = sem("s1_roundtrip")
        s_mix = sem("s1_mix")
        s_x = [sem(f"s1_x{u}") for u in range(2)]
        s_hp = sem("s1_hp")
        s_hi = sem("s1_hi")
        s_lo = sem("s1_lo")
        s_hst = [sem(f"s1_hst{u}") for u in range(2)]
        s_dtp = sem("s1_dtp")
        s_dtabs = sem("s1_dtabs")
        s_dtpos = sem("s1_dtpos")
        s_dtexp = sem("s1_dtexp")
        s_dtsp = sem("s1_dtsp")
        s_dtT = sem("s1_dtT")
        s_dt = sem("s1_dt")
        s_neg = sem("s1_neg")
        s_bits = sem("s1_bits")
        s_pick = sem("s1_pick")
        s_w4 = sem("s1_w4")

        with nc.Block() as block:

            @block.sync
            def _(sp):
                small = [(cond[:, :], a["cond_128"]), (cw[:, :], a["L0_cond2_c_weight"]),
                         (w0[:, :], a["L0_cond_W0"]), (w1[:, :], a["L0_cond_W1"]),
                         (b0[:, :], a["L0_cond_b0"].rearrange("(p o) -> p o", o=1)),
                         (b1[:, :], a["L0_cond_b1"].rearrange("(p o) -> p o", o=1)),
                         (w2[:, :], a["L0_cond_W2"]),
                         (b2[:, :], a["L0_cond_b2"].partition_broadcast(NB)),
                         (experts[:, :], a["L0_cond_weight"].rearrange("k o i u -> k (o i u)")),
                         (bias_k[:, :], a["L0_cond_bias_k"]),
                         (side[:, :], a["fside_S_0"].partition_broadcast(NB)),
                         (wdt[:, :], a["L0_attn_in_proj_w"][INNER + CONV:INNER + CONV + H, :]),
                         (dtb[:, :], a["L0_attn_dt_bias"].rearrange("(p o) -> p o", o=1)),
                         (alog[:, :], a["L0_attn_A_log"].partition_broadcast(P))]
                for dst, src in small:
                    sp.dma_start(dst, src).then_inc(s_ld, 16)
                sh.n_small = 16 * len(small)
                x_blk = a["x"].rearrange("b i d -> (b i) d").rearrange("(j t p) d -> j p t d", t=TT, p=P)

                def load_x(j, u):
                    sp.dma_start(xb[u][:, :, :], x_blk[ds(j, 1)].rearrange("o p t d -> p (o t) d")).then_inc(s_x[u], 16)

                for u in range(2):
                    sp.sem_inc(s_hst[u], 16)
                    load_x(u, u)
                sp.wait_ge(s_dve, 11)
                sp.dma_start(sh.agg_d.rearrange("b i o -> b (i o)"), agg[:, :, :].rearrange("b i o -> b (i o)")).then_inc(s_rt, 16)
                sp.dma_start(sh.aggb_d.rearrange("h b o -> b h o"), aggb[:, :, :].bitcast(F32)).then_inc(s_rt, 16)
                sp.dma_start(sh.ctxb_d, ctxb[:, :]).then_inc(s_rt, 16)
                sp.wait_ge(s_rt, 48)
                sp.wait_ge(s_const, 4)
                agg_v = sh.agg_d.rearrange("(t c) i o -> c i t o", c=BT)
                for c in range(BT):
                    sp.dma_start(mix[c * L:(c + 1) * L, :, c * L:(c + 1) * L], agg_v[c]).then_inc(s_mix, 16)
                sp.dma_start(aggb_row[:, :].bitcast(F32), sh.aggb_d.rearrange("h b o -> h (b o)")).then_inc(s_mix, 16)
                with sp.Fori(0, NBLK // 2 - 1) as jj:
                    for u in range(2):
                        sp.wait_ge(s_hp, KC * (2 * jj + u + 1))
                        load_x(2 * jj + u + 2, u)
                        sp.wait_ge(s_lo, KC * (2 * jj + u + 1) + KC)
                        sp.dma_start(sh.h_d[ds(2 * jj + u, 1)].rearrange("o p n -> p (o n)"),
                                     ht[u][:, :, :, :].rearrange("p a k n -> p (a k n)").bitcast(F32)).then_inc(s_hst[u], 16)
                for u in range(2):
                    sp.wait_ge(s_lo, KC * (NBLK - 2 + u + 1) + KC)
                    sp.dma_start(sh.h_d[NBLK - 2 + u], ht[u][:, :, :, :].rearrange("p a k n -> p (a k n)").bitcast(F32)).then_inc(s_hst[u], 16)
                for u in range(2):
                    sp.wait_ge(s_hst[u], 16 * (NBLK // 2) + 16)
                sp.wait_ge(s_w4, 16 * OT + NPK4)
                sp.dma_start(sh.w4_d, w4[:, :, :].rearrange("p t i -> p (t i)")).then_inc(s_rt, 16)
                sp.wait_ge(s_rt, 64)

            @block.gpsimd
            def _(pool):
                q_v = a["L0_ffn_qweight"].rearrange("n (t p) w -> t p n w", p=P)
                for t in range(OT):
                    pool.dma_start(qw[:, t, :, :], q_v[t]).then_inc(s_q, 16)
                pool.dma_start(lut4[:, :, :], a["L0_ffn_lut4"].rearrange("(t p) c -> p t c", p=P)).then_inc(s_q, 16)
                pool.dma_start(sh.lut8[:, :, :], a["L0_ffn_lut8"].rearrange("(t p) c -> p t c", p=P)).then_inc(s_q, 16)
                pool.memset(sh.ident[:, :], 0.0).then_inc(s_const, 1)
                pool.memset(ones_row[:, :].bitcast(F32), 1.0).then_inc(s_const, 1)
                pool.wait_ge(s_const, 2)
                pool.affine_select(out=sh.ident[:, :], in_=sh.ident[:, :], compare_op=ALU.not_equal, fill=1.0,
                                   base=0, pattern=[[-1, P]], channel_multiplier=1).then_inc(s_const, 1)
                pool.memset(mix[:, :, :], 0.0).then_inc(s_const, 1)
                pool.iota(sh.code_no[:, :], pattern=[[1, NCODE]], base=0, channel_multiplier=0,
                          allow_small_or_imprecise_dtypes=True).then_inc(s_const, 1)
                pool.memset(sh.mask_cb[:, :], 1.0).then_inc(s_const, 1)
                pool.memset(sh.mask_gt[:, :], 1.0).then_inc(s_const, 1)
                pool.wait_ge(s_const, 7)
                n = 7
                for m, tri in ((sh.mask_cb, "le"), (sh.mask_gt, "gt")):
                    v = m[:, :].rearrange("p (c l) -> p c l", l=L)
                    sel = [(0, [[-L, BT], [0, L]], 1), (L - 1, [[L, BT], [0, L]], -1)]
                    sel.append((0, [[L, BT], [1, L]], -1) if tri == "le" else (-1, [[-L, BT], [-1, L]], 1))
                    for base, pat, cm in sel:
                        pool.affine_select(out=v, in_=v, compare_op=ALU.is_ge, fill=0.0, base=base, pattern=pat,
                                           channel_multiplier=cm).then_inc(s_const, 1)
                        n += 1
                        pool.wait_ge(s_const, n)
                pool.memset(sh.neg_half[:, :], -0.5).then_inc(s_const, 1)
                pool.memset(sh.ones[:, :], 1.0).then_inc(s_const, 1)
                pool.memset(w4[:, :, :], 0.0).then_inc(s_const, 1)
                pool.memset(sh.w8[:, :, :], 0.0).then_inc(s_const, 1)
                pool.wait_ge(s_q, 16 * (OT + 2))
                pool.wait_ge(s_const, 16)
                pool.sem_inc(s_w4, NPK4)
                with pool.Fori(0, NBLK) as j:
                    for n in range(C4 * OT):
                        pool.wait_ge(s_pick, C4 * OT * j + n + 1)
                        pool.wait_ge(s_w4, C4 * OT * j + n + NPK4)
                        pool.tensor_tensor(w4[:, n % OT, :], w4[:, n % OT, :], pick[:, n % NPK4, :], ALU.add).then_inc(s_w4, 1)

            @block.tensor
            def _(pe):
                pe.wait_ge(s_ld, sh.n_small)
                pe.wait_ge(s_const, 4)
                pe.transpose(p_mlp[:, 0:NB], cond[:, :], sh.ident[:, :])
                pe.transpose(p_mlp[:, NB:NB + L], cw[:, :], sh.ident[0:L, 0:L]).then_inc(s_pe, 1)
                for k in range(KC):
                    ins = pe.transpose(p_wdt[:, k * H:(k + 1) * H], wdt[:, k * P:(k + 1) * P], sh.ident[0:H, 0:H])
                ins.then_inc(s_pe, 1)
                pe.wait_ge(s_dve, 2)
                pe.matmul(p_mlp[:, 160:160 + L], cond_t[:, :], cw_t[:, :], start=True, stop=True).then_inc(s_pe, 1)
                pe.matmul(p_mlp[:, 256:256 + NB], w0[:, :], cond_t[:, :], start=True, stop=True).then_inc(s_pe, 1)
                pe.wait_ge(s_act, 2)
                pe.matmul(p_mlp[:, 384:384 + NB], w1[:, :], h1[:, :], start=True, stop=True).then_inc(s_pe, 1)
                pe.wait_ge(s_act, 3)
                pe.matmul(p_mlp[:, 192:192 + NEXP], h2[:, :], w2[:, :], start=True, stop=True).then_inc(s_pe, 1)
                pe.wait_ge(s_dve, 7)
                pe.transpose(p_agg[0][0:NEXP, 0:NB], att[:, :], sh.ident[:, :]).then_inc(s_pe, 1)
                pe.wait_ge(s_dve, 8)
                for u in range(2):
                    pe.matmul(p_agg[u][:, :], att_t[:, :], experts[:, u * 512:(u + 1) * 512], start=True, stop=True)
                pe.matmul(p_mlp[:, 208:208 + L], att_t[:, :], bias_k[:, :], start=True, stop=True).then_inc(s_pe, 1)
                pe.wait_ge(s_mix, 16 * (BT + 1))
                with pe.Fori(0, NBLK // 2) as jj:
                    def mix_chunk(u, k):
                        j = 2 * jj + u
                        pe.wait_ge(s_lo, KC * j + k + 1)
                        for t in range(TT):
                            pe.matmul(p_h[k][:, t * P:(t + 1) * P], xb[u][:, t, k * P:(k + 1) * P],
                                      mix[:, ds(TT * j + t, 1), :].rearrange("p o n -> p (o n)"),
                                      start=(t == 0), stop=False, skip_group_check=True)
                        pe.matmul(p_h[k][:, :], ones_row[:, :], aggb_row[:, ds(BLK * j, BLK)],
                                  start=False, stop=True, skip_group_check=True).then_inc(s_hp, 1)

                    def dt_block(u):
                        j = 2 * jj + u
                        pe.wait_ge(s_lo, KC * (j + 1) + KC)
                        pe.wait_ge(s_dtpos, j + 1)
                        for n, (l, r) in enumerate(PASSES):
                            for k in range(KC):
                                ins = pe.matmul(p_dt[u][0:H, :], wdt_t[:, l, k, :], ht[u][:, r, k, :],
                                                start=(n == 0 and k == 0), stop=(n == 2 and k == KC - 1))
                        ins.then_inc(s_dtp, 1)

                    pe.wait_ge(s_x[0], 16 * jj + 16)
                    for k in range(KC):
                        mix_chunk(0, k)
                    pe.wait_ge(s_x[1], 16 * jj + 16)
                    mix_chunk(1, 0)
                    mix_chunk(1, 1)
                    dt_block(0)
                    mix_chunk(1, 2)
                    mix_chunk(1, 3)
                    dt_block(1)
                pe.wait_ge(s_dtpos, NBLK + 2)
                for j in range(NBLK):
                    pe.wait_ge(s_dtsp, j + 2)
                    pe.wait_ge(s_dt, j + 1)
                    for t in range(TT):
                        ins = pe.transpose(p_dt[j % 2][:, t * H:(t + 1) * H], dt_t[:, j * BLK + t * P:j * BLK + (t + 1) * P], sh.ident[0:H, 0:H])
                    ins.then_inc(s_dtT, 1)

            @block.scalar
            def _(act):
                act.wait_ge(s_pe, 2)
                act.activation(wdt_t[:, 0, :, :].rearrange("p k h -> p (k h)"), p_wdt[:, 0:KC * H], ACT.Copy).then_inc(s_act, 1)
                act.wait_ge(s_pe, 4)
                act.activation(h1[:, :], p_mlp[:, 256:256 + NB], ACT.Gelu, bias=b0[:, :]).then_inc(s_act, 1)
                act.wait_ge(s_pe, 5)
                act.activation(h2[:, :], p_mlp[:, 384:384 + NB], ACT.Gelu, bias=b1[:, :]).then_inc(s_act, 1)
                act.wait_ge(s_dve, 5)
                act.activation(att[:, :], logit[:, :], ACT.Exp, bias=nmax[:, :], accum_out=esum[:, :]).then_inc(s_act, 1)
                act.wait_ge(s_const, 15)
                act.activation(sh.mask_gtr[:, :], sh.mask_gt[:, :], ACT.Copy).then_inc(s_neg, 1)
                act.wait_ge(s_neg, 2)
                act.activation(sh.neg_a[:, :], alog[:, :], ACT.Exp).then_inc(s_neg, 1)

                def softplus_log(j, u):
                    act.wait_ge(s_dtp, j + 1)
                    act.wait_ge(s_dtsp, j + 1)
                    act.activation(sp_e[:, :], p_dt[u][0:H, :], ACT.Abs, bias=dtb[:, :]).then_inc(s_dtabs, 1)
                    act.wait_ge(s_dtabs, j + 1)
                    act.activation(sp_e[:, :], sp_e[:, :], ACT.Exp, scale=-1.0).then_inc(s_dtexp, 1)
                    act.wait_ge(s_dtexp, 2 * j + 1)
                    act.activation(sp_e[:, :], sp_e[:, :], ACT.Ln, bias=1.0).then_inc(s_dtexp, 1)

                def high_pair(jj, first):
                    for u in range(2):
                        act.wait_ge(s_hst[u], 16 * jj + 16)
                        act.wait_ge(s_dtpos, 2 * jj + u + 1)
                        for k in range(KC):
                            act.wait_ge(s_hp, KC * (2 * jj + u) + k + 1)
                            act.activation(ht[u][:, 0, k, :], p_h[k][:, :], ACT.Copy).then_inc(s_hi, 1)
                        if not (first and u == 0):
                            softplus_log(2 * jj + u - 1, 1 - u)

                high_pair(0, True)
                with act.Fori(1, NBLK // 2) as jj:
                    high_pair(jj, False)
                softplus_log(NBLK - 1, 1)

            @block.vector
            def _(dve):
                plane = bits[:, :, :].rearrange("p (t n w) s -> p t n (w s)", t=OT, n=4)

                def take_bits(half, first, last):
                    for s in range(first, last):
                        ins = dve.tensor_scalar(bits[:, :, s].rearrange("p (t n) -> p t n", t=OT),
                                                qw[:, :, 4 * half:4 * half + 4, :].rearrange("p t n w -> p t (n w)"), s, 1,
                                                ALU.logical_shift_right, ALU.bitwise_and)
                    ins.then_inc(s_bits, 1)

                dve.sem_inc(s_lo, KC)
                dve.sem_inc(s_dtpos, 2)
                dve.sem_inc(s_dtsp, 1)
                dve.sem_inc(s_dt, 2)
                dve.wait_ge(s_pe, 1)
                dve.tensor_copy(cond_t[:, :], p_mlp[:, 0:NB]).then_inc(s_dve, 1)
                dve.tensor_copy(cw_t[:, :], p_mlp[:, NB:NB + L]).then_inc(s_dve, 1)
                dve.wait_ge(s_act, 1)
                dve.tensor_tensor(wdt_t[:, 1, :, :].rearrange("p k h -> p (k h)"), p_wdt[:, 0:KC * H],
                                  wdt_t[:, 0, :, :].rearrange("p k h -> p (k h)").bitcast(F32), ALU.subtract).then_inc(s_dve, 1)
                dve.wait_ge(s_q, 16 * (OT + 2))
                take_bits(0, 0, 14)
                dve.wait_ge(s_pe, 6)
                dve.tensor_tensor(logit[:, :], p_mlp[:, 192:192 + NEXP], b2[:, :], ALU.add).then_inc(s_dve, 1)
                dve.wait_ge(s_dve, 4)
                dve.tensor_reduce(nmax[:, :], logit[:, :], axis=AX.X, op=ALU.max, negate=True).then_inc(s_dve, 1)
                dve.wait_ge(s_act, 4)
                dve.reciprocal(erec[:, :], esum[:, :]).then_inc(s_dve, 1)
                dve.wait_ge(s_dve, 6)
                dve.tensor_scalar(att[:, :], att[:, :], erec[:, :], None, ALU.mult).then_inc(s_dve, 1)
                dve.wait_ge(s_pe, 7)
                dve.tensor_copy(att_t[:, :], p_agg[0][0:NEXP, 0:NB]).then_inc(s_dve, 1)
                take_bits(0, 14, 32)
                dve.wait_ge(s_pe, 8)
                for u in range(2):
                    half = L // 2
                    dve.tensor_copy(agg[:, :, u * half:(u + 1) * half].rearrange("b i o -> b o i"),
                                    p_agg[u][:, :].rearrange("b (o i) -> b o i", i=L))
                dve.tensor_copy(aggb[:, 0, :], p_mlp[:, 208:208 + L]).then_inc(s_dve, 1)
                dve.tensor_tensor(ctxb[:, :], p_mlp[:, 160:160 + L], side[:, :], ALU.add).then_inc(s_dve, 1)
                dve.wait_ge(s_dve, 9)
                dve.tensor_tensor(aggb[:, 1, :], p_mlp[:, 208:208 + L], aggb[:, 0, :].bitcast(F32), ALU.subtract).then_inc(s_dve, 1)
                dve.wait_ge(s_ld, sh.n_small)
                dve.wait_ge(s_neg, 1)
                dve.tensor_scalar(alog[:, :], alog[:, :], LOGA_CAP, None, ALU.min).then_inc(s_neg, 1)
                n = 2
                for half in range(2):
                    if half:
                        dve.wait_ge(s_bits, n)
                        take_bits(1, 0, 32)
                        n += 1
                    for b in range(4):
                        dve.wait_ge(s_bits, n)
                        if half == 0 and b == 0:
                            ins = dve.tensor_copy(code4[:, :, :], plane[:, :, 0, :])
                        else:
                            ins = dve.scalar_tensor_tensor((sh.code8 if half and b == 3 else code4 if half == 0 else code)[:, :, :],
                                                           plane[:, :, b, :], float(1 << (4 * half + b)),
                                                           (code4 if half == 0 or b == 0 else code)[:, :, :], ALU.mult, ALU.add)
                        ins.then_inc(s_bits, 1)
                        n += 1
                dve.wait_ge(s_const, 16)
                dve.tensor_reduce(sh.mask_le[:, :], sh.mask_cb[:, :].rearrange("p (c l) -> p l c", l=L), axis=AX.X,
                                  op=ALU.add).then_inc(s_bits, 1)
                dve.wait_ge(s_neg, 3)
                dve.tensor_scalar(sh.neg_a[:, :], sh.neg_a[:, :], -1.0, None, ALU.mult).then_inc(s_neg, 1)
                dve.wait_ge(s_bits, n + 1)

                def softplus(j, u):
                    blk = dt_t[:, ds(BLK * j, BLK)]
                    dve.wait_ge(s_dtabs, j + 1)
                    dve.tensor_scalar(blk, p_dt[u][0:H, :], dtb[:, :], 0.0, ALU.add, ALU.max).then_inc(s_dtpos, 1)
                    dve.wait_ge(s_dtexp, 2 * j + 2)
                    dve.wait_ge(s_dtpos, j + 3)
                    dve.tensor_tensor(blk, blk, sp_e[:, :], ALU.add).then_inc(s_dtsp, 1)

                def low_pair(jj, first):
                    picked = [0]

                    def pick4(count):
                        for _ in range(count):
                            n = picked[0]
                            picked[0] += 1
                            dve.wait_ge(s_w4, 2 * C4 * OT * jj + n + 1)
                            dve.tensor_scalar(pick[:, n % NPK4, :], code4[:, n % OT, :], sh.code_no[:, ds(2 * C4 * jj + n // OT, 1)],
                                              lut4[:, n % OT, ds(2 * C4 * jj + n // OT, 1)], ALU.is_equal, ALU.mult).then_inc(s_pick, 1)

                    for u in range(2):
                        for k in range(KC):
                            dve.wait_ge(s_hi, KC * (2 * jj + u) + k + 1)
                            dve.tensor_tensor(ht[u][:, 1, k, :], p_h[k][:, :], ht[u][:, 0, k, :].bitcast(F32), ALU.subtract).then_inc(s_lo, 1)
                            pick4(1)
                        if not (first and u == 0):
                            softplus(2 * jj + u - 1, 1 - u)
                        pick4(C4 * OT - KC)

                low_pair(0, True)
                with dve.Fori(1, NBLK // 2) as jj:
                    low_pair(jj, False)
                softplus(NBLK - 1, 1)
                for j in range(NBLK):
                    dve.wait_ge(s_dtT, j + 1)
                    dve.tensor_copy(sh.dt[:, TT * j:TT * (j + 1), :].rearrange("p t h -> p (t h)"), p_dt[j % 2][:, 0:TT * H]).then_inc(s_dt, 1)
                dve.wait_ge(s_neg, 4)
                dve.wait_ge(s_dt, NBLK + 2)


def stage2(nc, a, sh):
    with ExitStack() as ctx:
        def sb(name, shape, dt=F32):
            return ctx.enter_context(nc.sbuf_tensor(name, shape, dt))

        def sem(name):
            return ctx.enter_context(nc.semaphore(name))

        stage = [sb(f"stage{n}", [P, DM]) for n in range(NSTAGE)]
        wt = sb("wt", [P, NCV + CT, 2, KC, P], F32R)
        wot = sb("wot", [P, 2, CT, DM], F32R)
        wnext = sb("wnext", [P, 2, 2, DM], F32R)
        cvw = sb("cvw", [P, NCV, TAPS])
        cvb = sb("cvb", [P, NCV])
        dsk = sb("dsk", [P, CT])
        nw = sb("nw", [P, CT])
        ht = sb("ht", [P, 2, KC, BLK], F32R)
        acc = sb("acc", [P, TT, DM])
        xc = sb("xc", [P, NCV, BLK])
        z = sb("z", [P, CT, BLK])
        y = sb("y", [P, CT, BLK])
        gy = sb("gy", [P, 2, CT, BLK], F32R)
        adt = sb("adt", [P, TT, HG])
        adts = sb("adts", [P, 2, TT * HG], F32R)
        segr = sb("segr", [P, 2, TT * HG, L], F32R)
        decay = y[:, CT // 2:, :].rearrange("p c n -> p (c n)").rearrange("p (t h l) -> p t h l", t=TT, h=HG)
        cbm = sb("cbm", [P, TT, P])
        dtx = sb("dtx", [P, TT, GI])
        m = sb("m", [P, TT, HG, P])
        rv = sb("rv", [P, TT])
        r = sb("r", [P, TT])
        pick = [sb(f"pick8_{n}", [P, DM]) for n in range(2)] + stage[2:]
        warm = sb("warm", [P, 1])

        bank = [ctx.enter_context(nc.psum_tensor(f"bank{n}", [P, 512], F32)) for n in range(8)]
        XT, SEG, CB, YB, OUT, SSQ, NEXT = (3, 4), (5, 7), 6, (6, 7), (2, 3, 4, 5), 6, (5, 1)

        s_stage = [sem(f"s2_stage{n}") for n in range(NSTAGE)]
        s_wps = sem("s2_wps")
        s_whi = sem("s2_whi")
        s_wlo = sem("s2_wlo")
        s_raw = [sem(f"s2_raw{u}") for u in range(2)]
        s_nps = sem("s2_nps")
        s_nhi = sem("s2_nhi")
        s_nlo = sem("s2_nlo")
        s_nst = sem("s2_nst")
        s_wt = [sem(f"s2_wt{n}") for n in range(NCV + CT)]
        s_wot = sem("s2_wot")
        s_cvp = sem("s2_conv_params")
        s_dnp = sem("s2_d_norm_params")
        s_ht = sem("s2_ht")
        s_accin = sem("s2_accin")
        s_accst = sem("s2_accst")
        s_proj = sem("s2_proj")
        s_tap = sem("s2_tap")
        s_cvstep = sem("s2_cvstep")
        s_conv = sem("s2_conv")
        s_silu = sem("s2_silu")
        s_z = sem("s2_z")
        s_adt = sem("s2_adt")
        s_segr = sem("s2_segr")
        s_seg = sem("s2_seg")
        s_exp = sem("s2_exp")
        s_xt = sem("s2_xt")
        s_dtx = sem("s2_dtx")
        s_cb = sem("s2_cb")
        s_cbm = sem("s2_cbm")
        s_yp = sem("s2_yp")
        s_y = sem("s2_y")
        s_u = sem("s2_u")
        s_uhi = sem("s2_uhi")
        s_ulo = sem("s2_ulo")
        s_sq = sem("s2_sq")
        s_sqsum = sem("s2_sqsum")
        s_ssq = sem("s2_ssq")
        s_rv = sem("s2_rv")
        s_r = sem("s2_r")
        s_out = sem("s2_out")
        s_acc = sem("s2_acc")
        s_pick = sem("s2_pick")
        s_w8 = sem("s2_w8")

        NPICK = len(pick)
        NCP, NDP = 6, 3
        NPJ = NCV + CT

        with nc.Block() as block:

            cw = a["L0_attn_conv_weight"]
            cb = a["L0_attn_conv_bias"].rearrange("(c o) -> c o", o=1)
            d_v = a["L0_attn_D"].rearrange("(g c u) -> u g c", g=G, u=2)
            nw_v = a["L0_attn_norm_weight"].rearrange("(g c p) -> g p c", g=G, p=P)

            def load_conv_params(g, queue):
                for lo, n, c0 in ((0, 1, INNER + g * NS), (1, 1, INNER + GN + g * NS), (2, CT, g * GI)):
                    queue.dma_start(cvw[:, lo:lo + n, :], cw[ds(c0, n * P), :].rearrange("(c p) k -> p c k", p=P)).then_inc(s_cvp, 16)
                    queue.dma_start(cvb[:, lo:lo + n], cb[ds(c0, n * P), :].rearrange("(c p) o -> p (c o)", p=P)).then_inc(s_cvp, 16)

            def load_d_norm(g, queue):
                for u in range(2):
                    queue.dma_start(dsk[u * HP:(u + 1) * HP, :], d_v[u, ds(g, 1), :].to_broadcast([HP, CT])).then_inc(s_dnp, 16)
                queue.dma_start(nw[:, :], nw_v[ds(g, 1)].rearrange("o p c -> p (o c)")).then_inc(s_dnp, 16)

            @block.sync
            def _(sp):
                w_in = a["L0_attn_in_proj_w"]
                w_out = a["L0_attn_out_proj_w"]
                acc_v = sh.acc_d.rearrange("(j t p) d -> j p t d", t=TT, p=P)
                x_v = a["x"].rearrange("b i d -> (b i) d").rearrange("(j t p) d -> j p t d", t=TT, p=P)

                def load_h(j):
                    sp.dma_start(ht[:, :, :, :].rearrange("p a k n -> p (a k n)").bitcast(F32), sh.h_d[j]).then_inc(s_ht, 16)

                def rows_of(n, g):
                    if n >= NPJ:
                        return w_out[(n - NPJ) * P:(n - NPJ + 1) * P, ds(g * GI, GI)]
                    first = ([2 * INNER + g * NS, 2 * INNER + GN + g * NS] + [INNER + g * GI + c * P for c in range(CT)]
                             + [g * GI + c * P for c in range(CT)])
                    return w_in[ds(first[n], P), :]

                def next_chunks(j):
                    return 2 + j, (j % 2 if j < NBLK - KC else NPJ + j - (NBLK - KC))

                def load_raw(g, j):
                    for u, n in enumerate(next_chunks(j)):
                        sp.dma_start(stage[u][:, :], rows_of(n, g)).then_inc(s_raw[u], 16)

                def step(g, j, resid, last):
                    it = NBLK * g + j
                    over = last and j == NBLK - 1
                    nxt = g if last else g + 1
                    turn = j == NBLK - 1 and not last
                    sp.wait_ge(s_accst, 16 * it + 16)
                    load_raw(nxt, j)
                    if turn:
                        sp.wait_ge(s_nst, 32 * it + 32)
                    sp.dma_start(acc[:, :, :], resid[j]).then_inc(s_accin, 16)
                    if turn:
                        for n in range(NPJ - 1):
                            sp.wait_ge(s_proj, NPJ * it + n + 1)
                            sp.dma_start(wt[:, n, :, :, :].rearrange("p a k n -> p (a k n)").bitcast(F32),
                                         sh.wt_d[ds(g, 1), n].rearrange("o p n -> p (o n)")).then_inc(s_wt[n], 16)
                            if n == NCV:
                                sp.wait_ge(s_conv, NCV * (it + 1))
                                load_conv_params(nxt, sp)
                    sp.wait_ge(s_nlo, 2 * it + 2)
                    for u, n in enumerate(next_chunks(j)):
                        sp.dma_start(sh.wt_d[ds(g, 1), n].rearrange("o p n -> p (o n)"),
                                     wnext[:, u, :, :].rearrange("p a n -> p (a n)").bitcast(F32)).then_inc(s_nst, 16)
                    sp.wait_ge(s_proj, NPJ * (it + 1))
                    if not over:
                        load_h((j + 1) % NBLK)
                    if turn:
                        n = NPJ - 1
                        sp.wait_ge(s_nst, 32 * it + 64)
                        sp.dma_start(wt[:, n, :, :, :].rearrange("p a k n -> p (a k n)").bitcast(F32),
                                     sh.wt_d[ds(g, 1), n].rearrange("o p n -> p (o n)")).then_inc(s_wt[n], 16)
                        sp.wait_ge(s_u, CT * (it + 1))
                        load_d_norm(nxt, sp)
                        sp.wait_ge(s_out, TT * (it + 1))
                        for k in range(KC):
                            sp.dma_start(wot[:, :, :, k * P:(k + 1) * P].rearrange("p a c n -> p (a c) n").bitcast(F32),
                                         sh.wt_d[ds(g, 1), NPJ + k].rearrange("o p (a n) -> p (o a) n", n=P)).then_inc(s_wot, 16)
                    sp.wait_ge(s_acc, TT * it + 2 * TT)
                    sp.dma_start(acc_v[j], acc[:, :, :]).then_inc(s_accst, 16)

                sp.sem_inc(s_accst, 16)
                sp.sem_inc(s_nst, 32)
                for n in range(NPJ):
                    sp.sem_inc(s_wt[n], 16)
                sp.sem_inc(s_wot, 16 * KC)
                for n in range(NWC):
                    if n >= NSTAGE:
                        sp.wait_ge(s_wps, n - NSTAGE + 1)
                    sp.dma_start(stage[n % NSTAGE][:, :], rows_of(n, 0)).then_inc(s_stage[n % NSTAGE], 16)
                load_h(0)
                sp.wait_ge(s_wps, NWC)
                for j in range(NBLK):
                    step(0, j, x_v, False)
                with sp.Fori(1, G - 1) as g:
                    for j in range(NBLK):
                        step(g, j, acc_v, False)
                for j in range(NBLK):
                    step(G - 1, j, acc_v, True)
                sp.wait_ge(s_accst, 16 * NIT + 16)
                sp.wait_ge(s_nst, 32 * NIT + 32)

            @block.gpsimd
            def _(pool):
                pool.sem_inc(s_segr, 2)
                pool.sem_inc(s_w8, NPICK)
                with pool.Fori(0, NIT) as it:
                    added = [0]

                    def add8(count=1):
                        for _ in range(count):
                            n = added[0]
                            added[0] += 1
                            pool.wait_ge(s_pick, CPI * OT * it + n + 1)
                            pool.wait_ge(s_w8, CPI * OT * it + n + NPICK)
                            pool.tensor_tensor(sh.w8[:, n % OT, :], sh.w8[:, n % OT, :], pick[n % NPICK][:, :], ALU.add).then_inc(s_w8, 1)

                    def low(c):
                        pool.wait_ge(s_uhi, CT * it + c + 1)
                        pool.tensor_tensor(gy[:, 1, c, :], z[:, c, :], gy[:, 0, c, :].bitcast(F32), ALU.subtract).then_inc(s_ulo, 1)

                    for half in range(2):
                        pool.wait_ge(s_adt, 4 * it + 3 + half)
                        pool.wait_ge(s_seg, SEGB * it + SEGB)
                        pool.tensor_tensor(segr[:, half, :, :], adts[:, half, :].bitcast(F32).unsqueeze(2).to_broadcast([P, TT * HG, L]),
                                           sh.mask_le[:, :].unsqueeze(1).to_broadcast([P, TT * HG, L]), ALU.mult).then_inc(s_segr, 1)
                    add8(6)
                    low(0)
                    low(1)
                    add8(2)
                    low(2)
                    low(3)
                    add8(2)
                    pool.wait_ge(s_rv, it + 2)
                    pool.tensor_tensor(r[:, :], rv[:, :], sh.neg_half[:, 0:TT], ALU.pow).then_inc(s_r, 1)
                    add8(CPI * OT - added[0])

            @block.tensor
            def _(pe):
                pe.sem_inc(s_seg, SEGB)
                for n in range(NWC):
                    slot = n % NSTAGE
                    pe.wait_ge(s_stage[slot], 16 * (n // NSTAGE + 1))
                    if n >= PREP:
                        pe.wait_ge(s_wlo, n - PREP + 1)
                    for k in range(KC):
                        ins = pe.transpose(bank[n % PREP][:, k * P:(k + 1) * P], stage[slot][:, k * P:(k + 1) * P], sh.ident[:, :])
                    ins.then_inc(s_wps, 1)
                pe.wait_ge(s_wlo, NWC)
                with pe.Fori(0, G) as g:
                    with pe.Fori(0, NBLK) as j:
                        it = NBLK * g + j

                        def project(n):
                            pe.wait_ge(s_wt[n], 16 * g + 16)
                            pb = bank[PROJ_BANK[n]]
                            for q, (l, rr) in enumerate(PASSES):
                                for k in range(KC):
                                    ins = pe.matmul(pb[:, :], wt[:, n, l, k, :], ht[:, rr, k, :],
                                                    start=(q == 0 and k == 0), stop=(q == 2 and k == KC - 1))
                            ins.then_inc(s_proj, 1)

                        def turn_x(t):
                            for c in range(CT):
                                ins = pe.transpose(bank[XT[t % 2]][:, c * P:(c + 1) * P], xc[:, 2 + c, t * P:(t + 1) * P], sh.ident[:, :])
                            ins.then_inc(s_xt, 1)

                        def scan(c):
                            for u in range(2):
                                for t in range(TT):
                                    if c == 0 and u == 0:
                                        pe.wait_ge(s_dtx, TT * it + t + 1)
                                    h = 2 * c + u
                                    ins = pe.matmul(bank[YB[c % 2]][u * HP:(u + 1) * HP, t * P:(t + 1) * P], dtx[:, t, h * HP:(h + 1) * HP],
                                                    m[:, t, h, :], start=True, stop=True)
                            ins.then_inc(s_yp, 1)

                        pe.wait_ge(s_ht, 16 * it + 16)
                        for n in range(NCV):
                            if n == 0:
                                pe.wait_ge(s_z, CT * it + CT)
                            elif n == 2:
                                pe.wait_ge(s_acc, TT * it + 1)
                            elif n >= 3:
                                pe.wait_ge(s_conv, NCV * it + n - 2)
                            project(n)
                        pe.wait_ge(s_segr, 2 * it + 4)
                        pe.wait_ge(s_acc, TT * it + TT)
                        pe.wait_ge(s_y, CT * it + CT)
                        for q in range(SEGB):
                            for half in range(2):
                                ins = pe.matmul(bank[SEG[q]][:, :], sh.mask_gtr[:, :],
                                                segr[:, half, q * 2 * HG:(q + 1) * 2 * HG, :].rearrange("p h l -> p (h l)"),
                                                start=(half == 0), stop=(half == 1))
                            ins.then_inc(s_seg, 1)
                        pe.wait_ge(s_conv, NCV * it + 4)
                        project(NCV)
                        pe.wait_ge(s_silu, NCV * it + 2)
                        pe.wait_ge(s_rv, it + 1)
                        for t in range(TT):
                            ins = pe.matmul(bank[CB][:, t * P:(t + 1) * P], xc[:, 0, t * P:(t + 1) * P], xc[:, 1, t * P:(t + 1) * P],
                                            start=True, stop=True)
                        ins.then_inc(s_cb, 1)
                        for c in (1, 2):
                            pe.wait_ge(s_conv, NCV * it + 4 + c)
                            project(NCV + c)
                            for t in (2 * c - 2, 2 * c - 1):
                                if c == 1:
                                    pe.wait_ge(s_silu, NCV * it + NCV)
                                else:
                                    pe.wait_ge(s_dtx, TT * it + t - 1)
                                turn_x(t)
                        for u in range(2):
                            pe.wait_ge(s_raw[u], 16 * it + 16)
                            if u == 0:
                                pe.wait_ge(s_exp, SEGB * it + 1)
                            else:
                                pe.wait_ge(s_z, CT * it + CT + 2)
                            for k in range(KC):
                                ins = pe.transpose(bank[NEXT[u]][:, k * P:(k + 1) * P], stage[u][:, k * P:(k + 1) * P], sh.ident[:, :])
                            ins.then_inc(s_nps, 1)
                        pe.wait_ge(s_cbm, it + 1)
                        scan(0)
                        pe.wait_ge(s_exp, SEGB * it + SEGB)
                        scan(1)
                        pe.wait_ge(s_z, CT * it + CT + 1)
                        project(NCV + 3)
                        for c in (2, 3):
                            pe.wait_ge(s_y, CT * it + CT + c - 1)
                            scan(c)
                        pe.wait_ge(s_z, CT * it + CT + 3)
                        pe.wait_ge(s_nlo, 2 * it + 2)
                        pe.wait_ge(s_dtx, TT * it + TT)
                        pe.wait_ge(s_wot, 16 * KC * g + 16 * KC)
                        for c in range(CT):
                            if c == CT - 2:
                                pe.wait_ge(s_y, CT * it + CT + 3)
                                pe.wait_ge(s_sqsum, (CT - 1) * (it + 1))
                                for t in range(TT):
                                    ins = pe.matmul(bank[SSQ][:, t * NSQ:(t + 1) * NSQ], y[:, 0, t * P:(t + 1) * P], sh.ones[:, 0:NSQ],
                                                    start=True, stop=True)
                                ins.then_inc(s_ssq, 1)
                            pe.wait_ge(s_ulo, CT * it + c + 1)
                            for t in range(TT):
                                for q, (l, rr) in enumerate(PASSES):
                                    ins = pe.matmul(bank[OUT[t]][:, :], gy[:, l, c, t * P:(t + 1) * P], wot[:, rr, c, :],
                                                    start=(c == 0 and q == 0), stop=(c == CT - 1 and q == 2))
                                if c == CT - 1:
                                    ins.then_inc(s_out, 1)

            @block.scalar
            def _(act):
                act.sem_inc(s_z, CT)
                load_conv_params(0, act)
                load_d_norm(0, act)
                for n in range(NWC):
                    act.wait_ge(s_wps, n + 1)
                    if n < NPJ:
                        act.activation(wt[:, n, 0, :, :].rearrange("p k c -> p (k c)"), bank[n % PREP][:, :], ACT.Copy).then_inc(s_whi, 1)
                    else:
                        k = n - NPJ
                        act.activation(wot[:, 0, :, k * P:(k + 1) * P], bank[n % PREP][:, :].rearrange("p (c d) -> p c d", c=CT),
                                       ACT.Copy).then_inc(s_whi, 1)
                with act.Fori(0, G) as g:
                    with act.Fori(0, NBLK) as j:
                        it = NBLK * g + j

                        def silu(n):
                            act.wait_ge(s_conv, NCV * it + n + 1)
                            act.activation(xc[:, n, :], xc[:, n, :], ACT.Silu).then_inc(s_silu, 1)

                        def gate(c):
                            act.wait_ge(s_proj, NPJ * it + NCV + c + 1)
                            act.activation(z[:, c, :], bank[PROJ_BANK[NCV + c]][:, :], ACT.Silu).then_inc(s_z, 1)

                        def high(c):
                            act.wait_ge(s_u, CT * it + c + 1)
                            act.activation(gy[:, 0, c, :], z[:, c, :], ACT.Copy).then_inc(s_uhi, 1)
                            act.activation(y[:, c, :], y[:, c, :], ACT.Square).then_inc(s_sq, 1)

                        act.activation(warm[:, :], sh.ones[:, 0:1], ACT.Silu)
                        for n in range(NCV):
                            act.wait_ge(s_proj, NPJ * it + n + 1)
                            if n == 0:
                                act.wait_ge(s_cvp, 16 * NCP * g + 16 * NCP)
                            act.activation(xc[:, n, :], bank[PROJ_BANK[n]][:, :], ACT.Identity, bias=cvb[:, n:n + 1],
                                           scale=cvw[:, n, TAPS - 1:TAPS]).then_inc(s_tap, 1)
                            if 0 < n < NCV - 1:
                                silu(n - 1)
                        for q in range(SEGB):
                            act.wait_ge(s_seg, SEGB * it + SEGB + q + 1)
                            act.activation(decay[:, 2 * q:2 * q + 2, :, :].rearrange("p t h l -> p (t h l)"),
                                           bank[SEG[q]][:, :], ACT.Exp).then_inc(s_exp, 1)
                        silu(NCV - 2)
                        silu(NCV - 1)
                        gate(0)
                        gate(1)
                        gate(2)
                        for u in range(2):
                            act.wait_ge(s_nps, 2 * it + u + 1)
                            act.wait_ge(s_nst, 32 * it + 32)
                            act.activation(wnext[:, u, 0, :], bank[NEXT[u]][:, :], ACT.Copy).then_inc(s_nhi, 1)
                        high(0)
                        high(1)
                        gate(3)
                        high(2)
                        high(3)

            @block.vector
            def _(dve):
                dve.sem_inc(s_y, CT)
                dve.sem_inc(s_acc, TT)
                dve.sem_inc(s_rv, 1)
                for n in range(NWC):
                    dve.wait_ge(s_whi, n + 1)
                    if n < NPJ:
                        dve.tensor_tensor(wt[:, n, 1, :, :].rearrange("p k c -> p (k c)"), bank[n % PREP][:, :],
                                          wt[:, n, 0, :, :].rearrange("p k c -> p (k c)").bitcast(F32), ALU.subtract).then_inc(s_wlo, 1)
                    else:
                        k = n - NPJ
                        dve.tensor_tensor(wot[:, 1, :, k * P:(k + 1) * P], bank[n % PREP][:, :].rearrange("p (c d) -> p c d", c=CT),
                                          wot[:, 0, :, k * P:(k + 1) * P].bitcast(F32), ALU.subtract).then_inc(s_wlo, 1)
                with dve.Fori(0, G) as g:
                    with dve.Fori(0, NBLK) as j:
                        it = NBLK * g + j
                        picked = [0]

                        def pick8(count=1):
                            for _ in range(count):
                                n = picked[0]
                                picked[0] += 1
                                dve.wait_ge(s_w8, CPI * OT * it + n + 1)
                                dve.tensor_scalar(pick[n % NPICK][:, :], sh.code8[:, n % OT, :], sh.code_no[:, ds(CPI * it + n // OT, 1)],
                                                  sh.lut8[:, n % OT, ds(CPI * it + n // OT, 1)], ALU.is_equal, ALU.mult).then_inc(s_pick, 1)

                        dve.wait_ge(s_segr, 2 * it + 2)
                        dve.tensor_tensor(adt[:, :, :], sh.dt[:, ds(TT * j, TT), ds(HG * g, HG)],
                                          sh.neg_a[:, ds(HG * g, HG)].unsqueeze(1).to_broadcast([P, TT, HG]), ALU.mult).then_inc(s_adt, 1)
                        dve.wait_ge(s_adt, 4 * it + 1)
                        dve.tensor_scalar(adt[:, :, :], adt[:, :, :], DECAY_FLOOR, None, ALU.max).then_inc(s_adt, 1)
                        dve.wait_ge(s_adt, 4 * it + 2)
                        adt_v = adt[:, :, :].rearrange("p t h -> p (t h)")
                        dve.tensor_copy(adts[:, 0, :], adt_v).then_inc(s_adt, 1)
                        dve.wait_ge(s_adt, 4 * it + 3)
                        dve.tensor_tensor(adts[:, 1, :], adt_v, adts[:, 0, :].bitcast(F32), ALU.subtract).then_inc(s_adt, 1)
                        for n in range(NCV):
                            dve.wait_ge(s_tap, NCV * it + n + 1)
                            for k in range(1, TAPS):
                                src = bank[PROJ_BANK[n]][:, :].rearrange("p (b l) -> p b l", l=L)[:, :, 0:L - k]
                                dst = xc[:, n, :].rearrange("p (b l) -> p b l", l=L)[:, :, k:L]
                                ins = dve.scalar_tensor_tensor(dst, src, cvw[:, n, TAPS - 1 - k:TAPS - k], dst, ALU.mult, ALU.add)
                                if k < TAPS - 1:
                                    ins.then_inc(s_cvstep, 1)
                                    dve.wait_ge(s_cvstep, (TAPS - 2) * (NCV * it + n) + k)
                            ins.then_inc(s_conv, 1)
                            if n < 4:
                                pick8()
                        dve.wait_ge(s_cb, it + 1)
                        dve.tensor_tensor(cbm[:, :, :], bank[CB][:, :].rearrange("p (t n) -> p t n", t=TT),
                                          sh.mask_cb[:, :].unsqueeze(1).to_broadcast([P, TT, P]), ALU.mult).then_inc(s_cbm, 1)

                        def scan_matrix(t):
                            dve.wait_ge(s_exp, SEGB * it + t // 2 + 1)
                            dve.tensor_tensor(m[:, t, :, :].rearrange("p h (c l) -> p h c l", l=L),
                                              cbm[:, t, :].rearrange("p (c l) -> p c l", l=L).unsqueeze(1).to_broadcast([P, HG, BT, L]),
                                              decay[:, t, :, :].unsqueeze(2).to_broadcast([P, HG, BT, L]), ALU.mult)

                        def times_dt(t):
                            dve.wait_ge(s_xt, TT * it + t + 1)
                            dve.tensor_tensor(dtx[:, t, :].rearrange("p (h c) -> p h c", h=HG),
                                              bank[XT[t % 2]][:, :].rearrange("p (h c) -> p h c", h=HG),
                                              sh.dt[:, ds(TT * j + t, 1), ds(HG * g, HG)].rearrange("p o h -> p (o h)").unsqueeze(2).to_broadcast([P, HG, HP]),
                                              ALU.mult).then_inc(s_dtx, 1)

                        dve.wait_ge(s_cbm, it + 1)
                        scan_matrix(0)
                        scan_matrix(1)
                        times_dt(0)
                        times_dt(1)
                        scan_matrix(2)
                        scan_matrix(3)
                        times_dt(2)
                        times_dt(3)
                        for u in range(2):
                            dve.wait_ge(s_nhi, 2 * it + u + 1)
                            dve.tensor_tensor(wnext[:, u, 1, :], bank[NEXT[u]][:, :], wnext[:, u, 0, :].bitcast(F32),
                                              ALU.subtract).then_inc(s_nlo, 1)
                        pick8(2)
                        for c in range(CT):
                            dve.wait_ge(s_yp, CT * it + c + 1)
                            if c == 0:
                                dve.wait_ge(s_dnp, 16 * NDP * g + 16 * NDP)
                            dve.scalar_tensor_tensor(y[:, c, :], xc[:, 2 + c, :], dsk[:, c:c + 1], bank[YB[c % 2]][:, :],
                                                     ALU.mult, ALU.add).then_inc(s_y, 1)
                            dve.wait_ge(s_z, CT * it + CT + c + 1)
                            dve.wait_ge(s_y, CT * it + CT + c + 1)
                            dve.scalar_tensor_tensor(z[:, c, :], z[:, c, :], nw[:, c:c + 1], y[:, c, :], ALU.mult, ALU.mult).then_inc(s_u, 1)
                            if c == 1:
                                pick8(2)
                        for c in range(1, CT):
                            dve.wait_ge(s_sq, CT * it + c + 1)
                            if c > 1:
                                dve.wait_ge(s_sqsum, (CT - 1) * it + c - 1)
                            dve.tensor_tensor(y[:, 0, :], y[:, 0, :], y[:, c, :], ALU.add).then_inc(s_sqsum, 1)
                        pick8(4)
                        dve.wait_ge(s_ssq, it + 1)
                        dve.tensor_scalar(rv[:, :], bank[SSQ][:, 0:TT * NSQ].rearrange("p (t n) -> p t n", t=TT)[:, :, 0], 1.0 / GI, EPS,
                                          ALU.mult, ALU.add).then_inc(s_rv, 1)
                        dve.wait_ge(s_r, it + 1)
                        dve.wait_ge(s_accin, 16 * it + 16)
                        for t in range(TT):
                            dve.wait_ge(s_out, TT * it + t + 1)
                            dve.scalar_tensor_tensor(acc[:, t, :], bank[OUT[t]][:, :], r[:, t:t + 1], acc[:, t, :],
                                                     ALU.mult, ALU.add).then_inc(s_acc, 1)
                        pick8(CPI * OT - picked[0])


def stage3(nc, a, sh, out):
    with ExitStack() as ctx:
        def sb(name, shape, dt=F32):
            return ctx.enter_context(nc.sbuf_tensor(name, shape, dt))

        def sem(name):
            return ctx.enter_context(nc.semaphore(name))

        w4 = sb("w4_nat", [P, OT, DM])
        wq = sb("wq", [P, 2, 2, R, DM], F32R)
        cbn = sb("cbn", [P, CG, KW])
        cbq = sb("cbq", [P, NQ, R, L])
        gmask = sb("gmask", [P, P])
        ctxb = sb("ctx_all", [P, TOK])
        bias = sb("bias", [P, DM])
        x2 = sb("x2", [P, TT, DM])
        x2s = [sb(f"x2s{u}", [P, BLK // L, XW]) for u in range(2)]
        xb = sb("x2b", [P, TT, DM])
        x3 = [sb(f"x3_{u}", [P, R, P]) for u in range(2)]
        sq = [sb(f"sq{u}", [P, R, P]) for u in range(2)]
        sqs = [sb(f"sqs{u}", [P, P]) for u in range(2)]
        hot = sb("hot", [P, TT])
        cold = sb("cold", [P, TT])
        x3t = sb("x3t", [P, 2, TT, R, P], F32R)
        res = sb("res", [P, TT, DM])

        p_cv = [ctx.enter_context(nc.psum_tensor(f"p_cv{u}", [P, 512], F32)) for u in range(2)]
        p_ss = [ctx.enter_context(nc.psum_tensor(f"p_ss{u}", [P, 512], F32)) for u in range(2)]
        p_y = [[ctx.enter_context(nc.psum_tensor(f"p_y{u}{q}", [P, 512], F32)) for q in range(2)] for u in range(2)]
        p_tr = p_y[0] + p_y[1]

        s_w = sem("s3_w")
        s_par = sem("s3_params")
        s_mask = sem("s3_mask")
        s_halo = sem("s3_halo")
        s_cbn = sem("s3_cbn")
        s_cbq = sem("s3_cbq")
        s_wps = sem("s3_wps")
        s_whi = sem("s3_whi")
        s_wlo = sem("s3_wlo")
        s_x2 = sem("s3_x2")
        s_x2s = [[sem(f"s3_x2s{u}{h}") for h in range(2)] for u in range(2)]
        s_xb = sem("s3_xb")
        s_cv = sem("s3_cv")
        s_x3 = sem("s3_x3")
        s_sq = sem("s3_sq")
        s_sqs = sem("s3_sqs")
        s_ss = sem("s3_ss")
        s_hot = sem("s3_hot")
        s_x3hi = sem("s3_x3hi")
        s_x3lo = sem("s3_x3lo")
        s_y = sem("s3_y")
        s_half = sem("s3_half")
        s_fin = sem("s3_fin")
        s_out = sem("s3_out")

        with nc.Block() as block:
            x2_v = sh.acc_d.rearrange("(j t p) d -> j p t d", t=TT, p=P)
            x2s_v = sh.acc_d.rearrange("(j b i) d -> j i b d", b=BLK // L, i=L)
            out_v = out.rearrange("b i d -> (b i) d").rearrange("(j t p) d -> j p t d", t=TT, p=P)

            @block.sync
            def _(sp):
                def load_rows(j):
                    sp.dma_start(x2[:, :, :], x2_v[ds(j, 1)].rearrange("o p t d -> p (o t) d")).then_inc(s_x2, 16)

                def load_shifted(j, u, halves=(0, 1)):
                    for h in halves:
                        bs = slice(h * BLK // L // 2, (h + 1) * BLK // L // 2)
                        for s in range(R):
                            sp.dma_start(x2s[u][s * L:(s + 1) * L, bs, R - s:R - s + DM],
                                         x2s_v[ds(j, 1), :, bs, :].rearrange("o i b d -> i (o b) d")).then_inc(s_x2s[u][h], 16)

                def store(j):
                    sp.wait_ge(s_fin, TT * (j + 1) + 2)
                    sp.dma_start(out_v[ds(j, 1)].rearrange("o p t d -> p (o t) d"), res[:, :, :]).then_inc(s_out, 16)

                sp.sem_inc(s_out, 16)
                sp.dma_start(w4[:, :, :].rearrange("p t i -> p (t i)"), sh.w4_d).then_inc(s_w, 16)
                w_v = a["L0_cond2_weight"].rearrange("(q o) i k -> q i o k", o=CG)
                for s in range(R // 2):
                    for q in range(L // CG):
                        lo = s * L + q * CG
                        sp.dma_start(cbn[lo:lo + CG, :, :], w_v[q]).then_inc(s_cbn, 16)
                sp.wait_ge(s_cbn, 16 * R * (L // CG))
                sp.wait_ge(s_halo, 4)
                load_shifted(0, 0, (0,))
                sp.dma_start(ctxb[:, :], sh.ctxb_d.rearrange("b o -> (b o)").partition_broadcast(P)).then_inc(s_par, 16)
                sp.dma_start(bias[:, :], a["L0_ffn_bias"].partition_broadcast(P)).then_inc(s_par, 16)
                load_shifted(0, 0, (1,))
                load_rows(0)
                load_shifted(1, 1)
                with sp.Fori(0, NBLK // 2 - 1) as jj:
                    for u in range(2):
                        j = 2 * jj + u
                        sp.wait_ge(s_xb, TT * (j + 1))
                        load_rows(j + 1)
                        sp.wait_ge(s_cv, TT * (j + 1))
                        load_shifted(j + 2, u)
                        store(j)
                sp.wait_ge(s_xb, TT * (NBLK - 1))
                load_rows(NBLK - 1)
                store(NBLK - 2)
                store(NBLK - 1)
                sp.wait_ge(s_out, 16 * NBLK + 16)

            @block.gpsimd
            def _(pool):
                for u in range(2):
                    pool.memset(x2s[u][:, :, 0:R], 0.0).then_inc(s_halo, 1)
                    pool.memset(x2s[u][:, :, DM:], 0.0).then_inc(s_halo, 1)
                pool.memset(cbq[:, :, :, :], 0.0).then_inc(s_mask, 1)
                pool.memset(gmask[:, :], 1.0).then_inc(s_mask, 1)
                v = gmask[:, :].rearrange("p (q o) -> p q o", o=CG)
                for n, (base, step, cm) in enumerate(((0, -CG, 1), (CG - 1, CG, -1))):
                    pool.wait_ge(s_mask, n + 2)
                    pool.affine_select(out=v, in_=v, compare_op=ALU.is_ge, fill=0.0, base=base,
                                       pattern=[[step, P // CG], [0, CG]], channel_multiplier=cm).then_inc(s_mask, 1)
                pool.wait_ge(s_par, 32)
                with pool.Fori(0, NBLK) as j:
                    def low(t):
                        pool.wait_ge(s_x3hi, TT * j + t + 1)
                        pool.tensor_tensor(x3t[:, 1, t, :, :].rearrange("p r n -> p (r n)"), x3[t % 2][:, :, :].rearrange("p r n -> p (r n)"),
                                           x3t[:, 0, t, :, :].rearrange("p r n -> p (r n)").bitcast(F32), ALU.subtract).then_inc(s_x3lo, 1)

                    def with_bias(t):
                        pool.wait_ge(s_fin, TT * j + 2)
                        pool.tensor_tensor(xb[:, t, :], x2[:, t, :], bias[:, :], ALU.add).then_inc(s_xb, 1)

                    low(0)
                    low(1)
                    pool.wait_ge(s_x2, 16 * j + 16)
                    for t in range(TT):
                        with_bias(t)
                        if t in (1, 3):
                            low(2 + t // 2)

            @block.tensor
            def _(pe):
                pe.sem_inc(s_y, TT)
                n = 0
                for q, w in ((1, sh.w8), (0, w4)):
                    if q == 0:
                        pe.wait_ge(s_w, 16)
                    for r in range(R):
                        if n >= 4:
                            pe.wait_ge(s_wlo, n - 3)
                        for t in range(OT):
                            ins = pe.transpose(p_tr[n % 4][:, t * P:(t + 1) * P], w[:, t, :].rearrange("p (m r) -> p r m", r=R)[:, r, :],
                                               sh.ident[:, :])
                        ins.then_inc(s_wps, 1)
                        n += 1
                pe.wait_ge(s_wlo, n)
                pe.wait_ge(s_cbq, NCBQ)
                with pe.Fori(0, NBLK // 2) as jj:
                    for u in range(2):
                        j = 2 * jj + u

                        def conv(t):
                            pe.wait_ge(s_x3, TT * j + t + 1)
                            for b in range(BT):
                                for q in range(NQ):
                                    ins = pe.matmul(p_cv[t % 2][:, b * P:(b + 1) * P],
                                                    x2s[u][:, BT * t + b, R * q:R * q + DM].rearrange("p (m r) -> p r m", r=R)[:, 0, :],
                                                    cbq[:, q, :, :].rearrange("p r o -> p (r o)"),
                                                    start=(q == 0), stop=(q == NQ - 1))
                            ins.then_inc(s_cv, 1)

                        def squares(t):
                            pe.wait_ge(s_sqs, TT * j + t + 3)
                            pe.wait_ge(s_hot, 2 * (TT * j + t) + 2)
                            pe.matmul(p_ss[t % 2][:, 0:NSQ], sqs[t % 2][:, :], sh.ones[:, 0:NSQ], start=True, stop=True).then_inc(s_ss, 1)

                        def ffn(t):
                            pe.wait_ge(s_x3lo, TT * j + t + 3)
                            pe.wait_ge(s_fin, TT * j + t + 1)
                            for q in range(2):
                                for n, (l, rr) in enumerate(PASSES):
                                    for r in range(R):
                                        ins = pe.matmul(p_y[t % 2][q][:, :], x3t[:, l, t, r, :], wq[:, q, rr, r, :],
                                                        start=(n == 0 and r == 0), stop=(n == 2 and r == R - 1))
                            ins.then_inc(s_y, 1)

                        pe.wait_ge(s_x2s[u][0], 16 * R * jj + 16 * R)
                        conv(0)
                        conv(1)
                        squares(0)
                        ffn(0)
                        pe.wait_ge(s_x2s[u][1], 16 * R * jj + 16 * R)
                        conv(2)
                        squares(1)
                        ffn(1)
                        conv(3)
                        squares(2)
                        ffn(2)
                        squares(3)
                        ffn(3)

            @block.scalar
            def _(act):
                w_v = a["L0_cond2_weight"].rearrange("(q o) i k -> q i o k", o=CG)
                for s in range(R // 2, R):
                    for q in range(L // CG):
                        lo = s * L + q * CG
                        act.dma_start(cbn[lo:lo + CG, :, :], w_v[q]).then_inc(s_cbn, 16)
                n = 0
                for q in (1, 0):
                    for r in range(R):
                        act.wait_ge(s_wps, n + 1)
                        act.activation(wq[:, q, 0, r, :], p_tr[n % 4][:, :], ACT.Copy).then_inc(s_whi, 1)
                        n += 1
                with act.Fori(0, NBLK) as j:
                    for t in range(TT):
                        act.wait_ge(s_x3, TT * j + t + 3)
                        act.wait_ge(s_y, TT * j + t + 1)
                        act.activation(x3t[:, 0, t, :, :], x3[t % 2][:, :, :], ACT.Copy).then_inc(s_x3hi, 1)
                        act.wait_ge(s_sqs, TT * j + t + 1)
                        act.activation(sq[t % 2][:, :, :], x3[t % 2][:, :, :], ACT.Square).then_inc(s_sq, 1)

            @block.vector
            def _(dve):
                dve.sem_inc(s_x3, 2)
                dve.sem_inc(s_x3lo, 2)
                dve.sem_inc(s_sqs, 2)
                dve.sem_inc(s_hot, 4)
                dve.sem_inc(s_fin, 2)
                def make_conv_weights():
                    dve.wait_ge(s_cbn, 16 * R * (L // CG))
                    dve.wait_ge(s_mask, 4)
                    for s in range(R):
                        rows = slice(s * L, (s + 1) * L)
                        same = gmask[rows, rows].rearrange("p (g o) -> p g o", o=CG)
                        for q in range(NQ):
                            for r in range(R):
                                k = R * q + s - r
                                if 0 <= k < KW:
                                    dve.tensor_tensor(cbq[rows, q, r, :].rearrange("p (g o) -> p g o", o=CG),
                                                      cbn[rows, :, k].unsqueeze(1).to_broadcast([L, L // CG, CG]), same,
                                                      ALU.mult).then_inc(s_cbq, 1)

                n = 0
                for q in (1, 0):
                    if q == 0:
                        make_conv_weights()
                    for r in range(R):
                        dve.wait_ge(s_whi, n + 1)
                        dve.tensor_tensor(wq[:, q, 1, r, :], p_tr[n % 4][:, :], wq[:, q, 0, r, :].bitcast(F32), ALU.subtract).then_inc(s_wlo, 1)
                        n += 1
                dve.wait_ge(s_par, 32)
                with dve.Fori(0, NBLK) as j:
                    def context(t):
                        dve.wait_ge(s_cv, TT * j + t + 1)
                        dve.wait_ge(s_x3lo, TT * j + t + 1)
                        dve.tensor_tensor(x3[t % 2][:, :, :].rearrange("p r (b o) -> p r b o", o=L),
                                          p_cv[t % 2][:, :].rearrange("p (b r o) -> p r b o", r=R, o=L),
                                          ctxb[:, ds((TT * j + t) * P, P)].rearrange("p (b o) -> p b o", o=L).unsqueeze(1).to_broadcast([P, R, BT, L]),
                                          ALU.add).then_inc(s_x3, 1)

                    def norm(t):
                        dve.wait_ge(s_sq, TT * j + t + 1)
                        dve.wait_ge(s_hot, 2 * (TT * j + t) + 2)
                        dve.tensor_reduce(sqs[t % 2][:, :], sq[t % 2][:, :, :].rearrange("p r n -> p n r"), axis=AX.X, op=ALU.add).then_inc(s_sqs, 1)

                    def choose(t):
                        dve.wait_ge(s_ss, TT * j + t + 1)
                        dve.tensor_scalar(hot[:, t:t + 1], p_ss[t % 2][:, 0:1], MASK_T2, None, ALU.is_gt).then_inc(s_hot, 1)
                        dve.tensor_scalar(cold[:, t:t + 1], p_ss[t % 2][:, 0:1], MASK_T2, None, ALU.is_le).then_inc(s_hot, 1)

                    def finish(t):
                        dve.wait_ge(s_y, TT * j + t + 1 + TT)
                        dve.wait_ge(s_xb, TT * j + t + 1)
                        dve.wait_ge(s_hot, 2 * (TT * j + t + 1) + 4)
                        if t == 0:
                            dve.wait_ge(s_out, 16 * j + 16)
                        dve.scalar_tensor_tensor(res[:, t, :], p_y[t % 2][1][:, :], hot[:, t:t + 1], xb[:, t, :],
                                                 ALU.mult, ALU.add).then_inc(s_half, 1)
                        dve.wait_ge(s_half, TT * j + t + 1)
                        dve.scalar_tensor_tensor(res[:, t, :], p_y[t % 2][0][:, :], cold[:, t:t + 1], res[:, t, :],
                                                 ALU.mult, ALU.add).then_inc(s_fin, 1)

                    context(0)
                    norm(0)
                    context(1)
                    norm(1)
                    choose(0)
                    context(2)
                    norm(2)
                    choose(1)
                    finish(0)
                    context(3)
                    norm(3)
                    choose(2)
                    finish(1)
                    choose(3)
                    finish(2)
                    finish(3)


def build(nc, a, out):
    sh = Shared()
    with ExitStack() as ctx:
        def sb(name, shape, dt=F32):
            return ctx.enter_context(nc.sbuf_tensor(name, shape, dt))

        ctx.enter_context(nc.allow_non_contiguous_dma(reason="parameters laid out by channel, a few KB"))
        sh.ident = sb("ident", [P, P])
        sh.mask_cb = sb("mask_cb", [P, P])
        sh.mask_gt = sb("mask_gt", [P, P])
        sh.mask_gtr = sb("mask_gtr", [P, P], F32R)
        sh.mask_le = sb("mask_le", [P, L])
        sh.neg_half = sb("neg_half", [P, TT])
        sh.ones = sb("ones", [P, P])
        sh.code_no = sb("code_no", [P, NCODE])
        sh.dt = sb("dt_all", [P, TOK // P, H])
        sh.neg_a = sb("neg_a", [P, H])
        sh.code8 = sb("code8", [P, OT, DM], BF16)
        sh.lut8 = sb("lut8", [P, OT, NCODE])
        sh.w8 = sb("w8", [P, OT, DM])
        sh.h_d = nc.dram_tensor("h_d", (NBLK, P, 2 * KC * BLK), F32).ap()
        sh.acc_d = nc.dram_tensor("acc_d", (TOK, DM), F32).ap()
        sh.agg_d = nc.dram_tensor("agg_d", (NB, L, L), F32).ap()
        sh.aggb_d = nc.dram_tensor("aggb_d", (2, NB, L), F32).ap()
        sh.ctxb_d = nc.dram_tensor("ctxb_d", (NB, L), F32).ap()
        sh.wt_d = nc.dram_tensor("wt_d", (G, NWC, P, 2 * KC * P), F32).ap()
        sh.w4_d = nc.dram_tensor("w4_d", (P, OT * DM), F32).ap()
        stage1(nc, a, sh)
        stage2(nc, a, sh)
        stage3(nc, a, sh, out)


_INS = ["x", "cond_128", "fside_S_0", "L0_cond_W0", "L0_cond_b0", "L0_cond_W1", "L0_cond_b1", "L0_cond_W2", "L0_cond_b2",
        "L0_cond_weight", "L0_cond_bias_k", "L0_attn_in_proj_w", "L0_attn_conv_weight", "L0_attn_conv_bias",
        "L0_attn_dt_bias", "L0_attn_A_log", "L0_attn_D", "L0_attn_norm_weight", "L0_attn_out_proj_w",
        "L0_cond2_weight", "L0_cond2_c_weight", "L0_ffn_qweight", "L0_ffn_lut4", "L0_ffn_lut8", "L0_ffn_bias"]


def kernel(**inputs):
    import numpy as np
    import concourse.bacc as bacc
    from concourse.bass_utils import run_bass_kernel_spmd

    nc = bacc.Bacc("TRN2", target_bir_lowering=False, num_devices=1)
    arrays, aps = {}, {}
    for name in _INS:
        v = np.ascontiguousarray(inputs[name])
        arrays[f"in_{name}"] = v
        aps[name] = nc.dram_tensor(f"in_{name}", v.shape, mybir.dt.from_np(v.dtype), kind="ExternalInput").ap()
    out = nc.dram_tensor("out_0", (NB, L, DM), F32, kind="ExternalOutput").ap()
    build(nc, aps, out)
    got = run_bass_kernel_spmd(nc, [arrays], core_ids=[0])
    return got.results[0]["out_0"]
```
